# Optimizing a Trainium2 kernel written in Bass

```python
import numpy as np
import jax
import jax.numpy as jnp

def _softmax(x, axis=-1):
    return jax.nn.softmax(x, axis=axis)

def _gelu(x):
    return jax.nn.gelu(x, approximate=True)

def _silu(x):
    return jax.nn.silu(x)

def _sigmoid(x):
    return jax.nn.sigmoid(x)

def _layernorm(x, axis=-1, eps=1e-05):
    m = jnp.mean(x, axis=axis, keepdims=True)
    v = jnp.var(x, axis=axis, keepdims=True)
    return (x - m) / jnp.sqrt(v + eps)

def _scatter_add(tgt, idx, src, axis=0):
    return tgt.at[idx].add(src)

def _segment_sum(src, seg, n):
    return jax.ops.segment_sum(src, seg, n)
kernel_name = 'mk_flamingo_gated_d2_seqx_r4_29240d'

def setup_inputs(seed: int=0):
    np.random.seed(seed)
    _w = jnp.asarray

    def _rec_inputs():
        import jax
        import jax.numpy as jnp
        _rk = jax.random.key(seed)
        x = -0.0005207 + 1.001 * jax.random.normal(jax.random.fold_in(_rk, 1), (8, 100, 256), jnp.float32)
        _lenS = 100 - jax.random.randint(jax.random.fold_in(_rk, 7), (8,), 0, max(1, 100 // 4) + 1, jnp.int32)
        _lenS2 = 361 - jax.random.randint(jax.random.fold_in(_rk, 8), (8,), 0, max(1, 361 // 4) + 1, jnp.int32)
        _ctx_1024P = jax.random.normal(jax.random.fold_in(_rk, 11), (8, 16, 256), jnp.float32)
        _ctx_1024c = jax.random.dirichlet(jax.random.fold_in(_rk, 511), 0.3 * jnp.ones((16,), jnp.float32), (8, 361))
        _ctx_1024t = jnp.einsum('bsk,bkd->bsd', _ctx_1024c, _ctx_1024P)
        _ctx_1024t = _ctx_1024t * jax.lax.rsqrt(jnp.mean(jnp.square(_ctx_1024t)) + 1e-12) * 0.953939
        ctx_1024 = -5.72187e-05 + 0.999849 * (_ctx_1024t + 0.3 * jax.random.normal(jax.random.fold_in(_rk, 611), (8, 361, 256), jnp.float32))
        _validS = jnp.arange(100)[None, :] < _lenS[:, None]
        _validS2 = jnp.arange(361)[None, :] < _lenS2[:, None]
        _causal = jnp.tril(jnp.ones((100, 100), dtype=bool))
        mask_Bx1x1xS2_bf1 = jnp.ones((8, 1, 1, 361), dtype=bool)
        _g = jax.random.normal(jax.random.fold_in(_rk, 9001), (2, 2), jnp.float32)
        _g = jnp.sign(_g) * jnp.maximum(jnp.abs(_g), 1.0) + (_g == 0) * 1.0
        g_xattn = _g[0]
        g_ffn = _g[1]
        return (x, ctx_1024, mask_Bx1x1xS2_bf1, g_xattn, g_ffn)
    x, ctx_1024, mask_Bx1x1xS2_bf1, g_xattn, g_ffn = _rec_inputs()

    def _L0_xattn_setup():
        import jax, jax.numpy as jnp
        import numpy as np
        key = jax.random.key(seed)
        ks = jax.random.split(key, 5)
        b, n_q, n_kv = (16, 128, 1024)
        query_dim, context_dim, heads, dim_head = (256, 256, 16, 64)
        inner = heads * dim_head
        x = jax.random.normal(ks[0], (b, n_q, query_dim), dtype=jnp.float32)
        context = jax.random.normal(ks[1], (b, n_kv, context_dim), dtype=jnp.float32)
        Wq = jax.random.normal(ks[2], (query_dim, inner), dtype=jnp.float32) * query_dim ** (-0.5)
        Wkv = jax.random.normal(ks[3], (context_dim, 2 * inner), dtype=jnp.float32) * context_dim ** (-0.5)
        Wout = jax.random.normal(ks[4], (inner, query_dim), dtype=jnp.float32) * inner ** (-0.5)
        bout = jnp.zeros((query_dim,), dtype=jnp.float32)
        return {'x': x, 'context': context, 'Wq': Wq, 'Wkv': Wkv, 'Wout': Wout, 'bout': bout}
    _L0_xattn_all = _L0_xattn_setup()
    _L0_xattn_in = {k: v for k, v in _L0_xattn_all.items() if k in ('Wq', 'Wkv', 'Wout', 'bout')}
    del _L0_xattn_all

    def _L0_ffn_setup():
        import jax, jax.numpy as jnp
        import numpy as np
        B, T, C = (2, 512, 256)
        H, D = (16, 64)
        CR = 8
        R = C // CR
        ROPE = D // 2
        NOPE = D - ROPE
        E, K, I, S = (8, 2, 128, 1)
        THETA = 100000.0
        EPS = 1e-05

        def _rmsnorm(x, w):
            rms = jnp.sqrt(jnp.mean(x * x, axis=-1, keepdims=True) + EPS)
            return w * (x / rms)

        def _rope(xh):
            d = xh.shape[-1]
            t = jnp.arange(xh.shape[2], dtype=jnp.float32)
            freqs = 1.0 / THETA ** (jnp.arange(0, d, 2, dtype=jnp.float32) / d)
            ang = jnp.outer(t, freqs)
            cos, sin = (jnp.cos(ang), jnp.sin(ang))
            xr = xh.reshape(xh.shape[:-1] + (d // 2, 2))
            x0, x1 = (xr[..., 0], xr[..., 1])
            rot = jnp.stack([x0 * cos - x1 * sin, x0 * sin + x1 * cos], axis=-1)
            return rot.reshape(xh.shape)

        def _attention(x, Wq, Wkva, Wkvb, Wo):
            b, t, _ = x.shape
            q = (x @ Wq).reshape(b, t, H, D).transpose(0, 2, 1, 3)
            ckv = x @ Wkva
            kv_latent, k_rope = (ckv[:, :, :R], ckv[:, :, R:])
            kv = (kv_latent @ Wkvb).reshape(b, t, H, NOPE).transpose(0, 2, 1, 3)
            k_rope = jnp.broadcast_to(k_rope[:, None, :, :], (b, H, t, ROPE))
            q_nope, q_rope = (q[..., :NOPE], q[..., NOPE:])
            q = jnp.concatenate([q_nope, _rope(q_rope)], axis=-1)
            k = jnp.concatenate([kv, _rope(k_rope)], axis=-1)
            v = jnp.concatenate([kv, jnp.zeros_like(k_rope)], axis=-1)
            att = jnp.einsum('bhqd,bhkd->bhqk', q, k) / jnp.sqrt(jnp.float32(D))
            mask = jnp.tril(jnp.ones((t, t), dtype=bool))
            att = jnp.where(mask, att, jnp.float32(-jnp.inf))
            att = jax.nn.softmax(att, axis=-1)
            y = jnp.einsum('bhqk,bhkd->bhqd', att, v)
            y = y.transpose(0, 2, 1, 3).reshape(b, t, H * D)
            return y @ Wo

        def _experts(x_flat, Wg, Wu, Wd):
            g = jax.nn.silu(jnp.einsum('nc,eci->nei', x_flat, Wg))
            u = jnp.einsum('nc,eci->nei', x_flat, Wu)
            return jnp.einsum('nei,eic->nec', g * u, Wd)

        def _moe(x, Wgate, expert_bias, Wg, Wu, Wd, sWg, sWu, sWd):
            b, t, c = x.shape
            xf = x.reshape(-1, c)
            shared = jnp.mean(_experts(xf, sWg, sWu, sWd), axis=1)
            logits = xf @ Wgate + expert_bias
            probs = jax.nn.softmax(logits, axis=-1)
            topk_p, topk_i = jax.lax.top_k(probs, K)
            topk_p = topk_p / jnp.sum(topk_p, axis=-1, keepdims=True)
            comb = jnp.sum(jax.nn.one_hot(topk_i, E, dtype=xf.dtype) * topk_p[..., None], axis=1)
            routed = jnp.einsum('ne,nec->nc', comb, _experts(xf, Wg, Wu, Wd))
            return (shared + routed).reshape(b, t, c)
        key = jax.random.key(seed)
        ks = jax.random.split(key, 16)
        w = lambda k, shp: jax.random.normal(k, shp, dtype=jnp.float32) * 0.02
        return {'x': jax.random.normal(ks[0], (B, T, C), dtype=jnp.float32), 'w_ln1': jnp.ones((C,), jnp.float32), 'Wq': w(ks[1], (C, H * D)), 'Wkva': w(ks[2], (C, R + ROPE)), 'Wkvb': w(ks[3], (R, H * NOPE)), 'Wo': w(ks[4], (H * D, C)), 'w_ln2': jnp.ones((C,), jnp.float32), 'Wgate': w(ks[5], (C, E)), 'expert_bias': jnp.zeros((E,), jnp.float32), 'Wg': w(ks[6], (E, C, I)), 'Wu': w(ks[7], (E, C, I)), 'Wd': w(ks[8], (E, I, C)), 'sWg': w(ks[9], (S, C, I)), 'sWu': w(ks[10], (S, C, I)), 'sWd': w(ks[11], (S, I, C))}
    _L0_ffn_all = _L0_ffn_setup()
    _L0_ffn_in = {k: v for k, v in _L0_ffn_all.items() if k in ('w_ln1', 'Wq', 'Wkva', 'Wkvb', 'Wo', 'w_ln2', 'Wgate', 'expert_bias', 'Wg', 'Wu', 'Wd', 'sWg', 'sWu', 'sWd')}
    del _L0_ffn_all

    def _L1_xattn_setup():
        import jax, jax.numpy as jnp
        import numpy as np
        D_MODEL = 256
        NUM_HEADS = 16
        D_K = D_MODEL // NUM_HEADS
        key = jax.random.key(seed)
        ks = jax.random.split(key, 12)
        b, t1, t2 = (4, 512, 512)
        s = 1.0 / np.sqrt(D_MODEL)
        inp = {'q': jax.random.normal(ks[0], (b, t1, D_MODEL), jnp.float32), 'k': jax.random.normal(ks[1], (b, t2, D_MODEL), jnp.float32), 'v': jax.random.normal(ks[2], (b, t2, D_MODEL), jnp.float32), 'mask': jnp.ones((b, 1, 1, t2), dtype=bool), 'w_q': jax.random.normal(ks[3], (D_MODEL, D_MODEL), jnp.float32) * s, 'b_q': jax.random.normal(ks[4], (D_MODEL,), jnp.float32) * s, 'w_k': jax.random.normal(ks[5], (D_MODEL, D_MODEL), jnp.float32) * s, 'b_k': jax.random.normal(ks[6], (D_MODEL,), jnp.float32) * s, 'w_v': jax.random.normal(ks[7], (D_MODEL, D_MODEL), jnp.float32) * s, 'b_v': jax.random.normal(ks[8], (D_MODEL,), jnp.float32) * s, 'w_o': jax.random.normal(ks[9], (D_MODEL, D_MODEL), jnp.float32) * s, 'b_o': jax.random.normal(ks[10], (D_MODEL,), jnp.float32) * s}
        return inp
    _L1_xattn_all = _L1_xattn_setup()
    _L1_xattn_in = {k: v for k, v in _L1_xattn_all.items() if k in ('w_q', 'b_q', 'w_k', 'b_k', 'w_v', 'b_v', 'w_o', 'b_o')}
    del _L1_xattn_all

    def _L1_ffn_setup():
        import jax, jax.numpy as jnp
        import numpy as np
        E = 8
        K = 2
        D = 256
        H = 684
        B, S = (2, 512)

        def _moe_forward(x, centroid, Wg, bg, W1, b1, W2, b2):
            T = x.shape[0] * x.shape[1]
            xs = x.reshape(T, D)
            d2 = jnp.sum(xs * xs, axis=-1, keepdims=True) + jnp.sum(centroid * centroid, axis=-1)[None, :] - 2.0 * (xs @ centroid.T)
            dist = jnp.sqrt(jnp.maximum(d2, 1e-12))
            w, sel = jax.lax.top_k(dist, K)
            w = jax.nn.softmax(w.astype(jnp.float32), axis=1).astype(x.dtype)
            we = jnp.zeros((T, E), dtype=x.dtype).at[jnp.arange(T)[:, None], sel].add(w)
            out = jnp.zeros_like(xs)
            for e in range(E):
                h = jax.nn.silu(xs @ Wg[e] + bg[e]) * (xs @ W1[e] + b1[e])
                out = out + we[:, e:e + 1] * (h @ W2[e] + b2[e])
            return out.reshape(x.shape)
        key = jax.random.key(seed)
        ks = jax.random.split(key, 9)
        scale = 0.02
        return {'x': jax.random.normal(ks[0], (B, S, D), dtype=jnp.float32), 'centroid': jax.random.normal(ks[1], (E, D), dtype=jnp.float32), 'Wg': jax.random.normal(ks[2], (E, D, H), dtype=jnp.float32) * scale, 'bg': jnp.zeros((E, H), dtype=jnp.float32), 'W1': jax.random.normal(ks[3], (E, D, H), dtype=jnp.float32) * scale, 'b1': jnp.zeros((E, H), dtype=jnp.float32), 'W2': jax.random.normal(ks[4], (E, H, D), dtype=jnp.float32) * scale, 'b2': jnp.zeros((E, D), dtype=jnp.float32)}
    _L1_ffn_all = _L1_ffn_setup()
    _L1_ffn_in = {k: v for k, v in _L1_ffn_all.items() if k in ('centroid', 'Wg', 'bg', 'W1', 'b1', 'W2', 'b2')}
    del _L1_ffn_all
    return {'x': x, 'ctx_1024': ctx_1024, 'mask_Bx1x1xS2_bf1': mask_Bx1x1xS2_bf1, 'g_xattn': g_xattn, 'g_ffn': g_ffn, 'L0_xattn_Wq': _L0_xattn_in['Wq'], 'L0_xattn_Wkv': _L0_xattn_in['Wkv'], 'L0_xattn_Wout': _L0_xattn_in['Wout'], 'L0_xattn_bout': _L0_xattn_in['bout'], 'L0_ffn_w_ln1': _L0_ffn_in['w_ln1'], 'L0_ffn_Wq': _L0_ffn_in['Wq'], 'L0_ffn_Wkva': _L0_ffn_in['Wkva'], 'L0_ffn_Wkvb': _L0_ffn_in['Wkvb'], 'L0_ffn_Wo': _L0_ffn_in['Wo'], 'L0_ffn_w_ln2': _L0_ffn_in['w_ln2'], 'L0_ffn_Wgate': _L0_ffn_in['Wgate'], 'L0_ffn_expert_bias': _L0_ffn_in['expert_bias'], 'L0_ffn_Wg': _L0_ffn_in['Wg'], 'L0_ffn_Wu': _L0_ffn_in['Wu'], 'L0_ffn_Wd': _L0_ffn_in['Wd'], 'L0_ffn_sWg': _L0_ffn_in['sWg'], 'L0_ffn_sWu': _L0_ffn_in['sWu'], 'L0_ffn_sWd': _L0_ffn_in['sWd'], 'L1_xattn_w_q': _L1_xattn_in['w_q'], 'L1_xattn_b_q': _L1_xattn_in['b_q'], 'L1_xattn_w_k': _L1_xattn_in['w_k'], 'L1_xattn_b_k': _L1_xattn_in['b_k'], 'L1_xattn_w_v': _L1_xattn_in['w_v'], 'L1_xattn_b_v': _L1_xattn_in['b_v'], 'L1_xattn_w_o': _L1_xattn_in['w_o'], 'L1_xattn_b_o': _L1_xattn_in['b_o'], 'L1_ffn_centroid': _L1_ffn_in['centroid'], 'L1_ffn_Wg': _L1_ffn_in['Wg'], 'L1_ffn_bg': _L1_ffn_in['bg'], 'L1_ffn_W1': _L1_ffn_in['W1'], 'L1_ffn_b1': _L1_ffn_in['b1'], 'L1_ffn_W2': _L1_ffn_in['W2'], 'L1_ffn_b2': _L1_ffn_in['b2']}

def reference(x, ctx_1024, mask_Bx1x1xS2_bf1, g_xattn, g_ffn, L0_xattn_Wq, L0_xattn_Wkv, L0_xattn_Wout, L0_xattn_bout, L0_ffn_w_ln1, L0_ffn_Wq, L0_ffn_Wkva, L0_ffn_Wkvb, L0_ffn_Wo, L0_ffn_w_ln2, L0_ffn_Wgate, L0_ffn_expert_bias, L0_ffn_Wg, L0_ffn_Wu, L0_ffn_Wd, L0_ffn_sWg, L0_ffn_sWu, L0_ffn_sWd, L1_xattn_w_q, L1_xattn_b_q, L1_xattn_w_k, L1_xattn_b_k, L1_xattn_w_v, L1_xattn_b_v, L1_xattn_w_o, L1_xattn_b_o, L1_ffn_centroid, L1_ffn_Wg, L1_ffn_bg, L1_ffn_W1, L1_ffn_b1, L1_ffn_W2, L1_ffn_b2):
    import jax
    import jax.numpy as jnp

    def _L0_xattn_ref(x, context, Wq, Wkv, Wout, bout):
        import jax, jax.numpy as jnp
        import numpy as np
        heads, dim_head = (16, 64)
        b, n_q, _ = x.shape
        n_kv = context.shape[1]
        scale = dim_head ** (-0.5)
        q = x @ Wq
        kv = context @ Wkv
        k, v = jnp.split(kv, 2, axis=-1)

        def split_heads(t):
            bb, n, _ = t.shape
            return t.reshape(bb, n, heads, dim_head).transpose(0, 2, 1, 3)
        q, k, v = map(split_heads, (q, k, v))
        i_idx = jnp.arange(n_q)[:, None]
        j_idx = jnp.arange(n_kv)[None, :]
        mask = j_idx % n_q == i_idx
        sim = jnp.einsum('bhid,bhjd->bhij', q, k) * scale
        max_neg = -jnp.finfo(sim.dtype).max
        sim = jnp.where(mask[None, None, :, :], sim, max_neg)
        attn = jax.nn.softmax(sim, axis=-1)
        out = jnp.einsum('bhij,bhjd->bhid', attn, v)
        out = out.transpose(0, 2, 1, 3).reshape(b, n_q, heads * dim_head)
        return out @ Wout + bout

    def _L0_ffn_ref(x, w_ln1, Wq, Wkva, Wkvb, Wo, w_ln2, Wgate, expert_bias, Wg, Wu, Wd, sWg, sWu, sWd):
        import jax, jax.numpy as jnp
        import numpy as np
        B, T, C = (2, 512, 256)
        H, D = (16, 64)
        CR = 8
        R = C // CR
        ROPE = D // 2
        NOPE = D - ROPE
        E, K, I, S = (8, 2, 128, 1)
        THETA = 100000.0
        EPS = 1e-05

        def _rmsnorm(x, w):
            rms = jnp.sqrt(jnp.mean(x * x, axis=-1, keepdims=True) + EPS)
            return w * (x / rms)

        def _rope(xh):
            d = xh.shape[-1]
            t = jnp.arange(xh.shape[2], dtype=jnp.float32)
            freqs = 1.0 / THETA ** (jnp.arange(0, d, 2, dtype=jnp.float32) / d)
            ang = jnp.outer(t, freqs)
            cos, sin = (jnp.cos(ang), jnp.sin(ang))
            xr = xh.reshape(xh.shape[:-1] + (d // 2, 2))
            x0, x1 = (xr[..., 0], xr[..., 1])
            rot = jnp.stack([x0 * cos - x1 * sin, x0 * sin + x1 * cos], axis=-1)
            return rot.reshape(xh.shape)

        def _attention(x, Wq, Wkva, Wkvb, Wo):
            b, t, _ = x.shape
            q = (x @ Wq).reshape(b, t, H, D).transpose(0, 2, 1, 3)
            ckv = x @ Wkva
            kv_latent, k_rope = (ckv[:, :, :R], ckv[:, :, R:])
            kv = (kv_latent @ Wkvb).reshape(b, t, H, NOPE).transpose(0, 2, 1, 3)
            k_rope = jnp.broadcast_to(k_rope[:, None, :, :], (b, H, t, ROPE))
            q_nope, q_rope = (q[..., :NOPE], q[..., NOPE:])
            q = jnp.concatenate([q_nope, _rope(q_rope)], axis=-1)
            k = jnp.concatenate([kv, _rope(k_rope)], axis=-1)
            v = jnp.concatenate([kv, jnp.zeros_like(k_rope)], axis=-1)
            att = jnp.einsum('bhqd,bhkd->bhqk', q, k) / jnp.sqrt(jnp.float32(D))
            mask = jnp.tril(jnp.ones((t, t), dtype=bool))
            att = jnp.where(mask, att, jnp.float32(-jnp.inf))
            att = jax.nn.softmax(att, axis=-1)
            y = jnp.einsum('bhqk,bhkd->bhqd', att, v)
            y = y.transpose(0, 2, 1, 3).reshape(b, t, H * D)
            return y @ Wo

        def _experts(x_flat, Wg, Wu, Wd):
            g = jax.nn.silu(jnp.einsum('nc,eci->nei', x_flat, Wg))
            u = jnp.einsum('nc,eci->nei', x_flat, Wu)
            return jnp.einsum('nei,eic->nec', g * u, Wd)

        def _moe(x, Wgate, expert_bias, Wg, Wu, Wd, sWg, sWu, sWd):
            b, t, c = x.shape
            xf = x.reshape(-1, c)
            shared = jnp.mean(_experts(xf, sWg, sWu, sWd), axis=1)
            logits = xf @ Wgate + expert_bias
            probs = jax.nn.softmax(logits, axis=-1)
            topk_p, topk_i = jax.lax.top_k(probs, K)
            topk_p = topk_p / jnp.sum(topk_p, axis=-1, keepdims=True)
            comb = jnp.sum(jax.nn.one_hot(topk_i, E, dtype=xf.dtype) * topk_p[..., None], axis=1)
            routed = jnp.einsum('ne,nec->nc', comb, _experts(xf, Wg, Wu, Wd))
            return (shared + routed).reshape(b, t, c)
        x = x + _attention(_rmsnorm(x, w_ln1), Wq, Wkva, Wkvb, Wo)
        residual = x
        xn = _rmsnorm(x, w_ln2)
        x_out = _moe(xn, Wgate, expert_bias, Wg, Wu, Wd, sWg, sWu, sWd)
        return residual + x_out

    def _L1_xattn_ref(q, k, v, mask, w_q, b_q, w_k, b_k, w_v, b_v, w_o, b_o):
        import jax, jax.numpy as jnp
        import numpy as np
        D_MODEL = 256
        NUM_HEADS = 16
        D_K = D_MODEL // NUM_HEADS
        b, t1, _ = q.shape
        t2 = k.shape[1]
        qh = (q @ w_q.T + b_q).reshape(b, t1, NUM_HEADS, D_K).transpose(0, 2, 1, 3)
        kh = (k @ w_k.T + b_k).reshape(b, t2, NUM_HEADS, D_K).transpose(0, 2, 1, 3)
        vh = (v @ w_v.T + b_v).reshape(b, t2, NUM_HEADS, D_K).transpose(0, 2, 1, 3)
        scores = jnp.einsum('bhqd,bhkd->bhqk', qh, kh) / jnp.sqrt(jnp.asarray(D_K, qh.dtype))
        scores = jnp.where(mask, scores, jnp.asarray(-jnp.inf, scores.dtype))
        attn = jax.nn.softmax(scores, axis=-1)
        out = jnp.einsum('bhqk,bhkd->bhqd', attn, vh)
        out = out.transpose(0, 2, 1, 3).reshape(b, t1, D_MODEL)
        return out @ w_o.T + b_o

    def _L1_ffn_ref(x, centroid, Wg, bg, W1, b1, W2, b2):
        import jax, jax.numpy as jnp
        import numpy as np
        E = 8
        K = 2
        D = 256
        H = 684
        B, S = (2, 512)

        def _moe_forward(x, centroid, Wg, bg, W1, b1, W2, b2):
            T = x.shape[0] * x.shape[1]
            xs = x.reshape(T, D)
            d2 = jnp.sum(xs * xs, axis=-1, keepdims=True) + jnp.sum(centroid * centroid, axis=-1)[None, :] - 2.0 * (xs @ centroid.T)
            dist = jnp.sqrt(jnp.maximum(d2, 1e-12))
            w, sel = jax.lax.top_k(dist, K)
            w = jax.nn.softmax(w.astype(jnp.float32), axis=1).astype(x.dtype)
            we = jnp.zeros((T, E), dtype=x.dtype).at[jnp.arange(T)[:, None], sel].add(w)
            out = jnp.zeros_like(xs)
            for e in range(E):
                h = jax.nn.silu(xs @ Wg[e] + bg[e]) * (xs @ W1[e] + b1[e])
                out = out + we[:, e:e + 1] * (h @ W2[e] + b2[e])
            return out.reshape(x.shape)
        return _moe_forward(x, centroid, Wg, bg, W1, b1, W2, b2)
    x = x + jnp.tanh(g_xattn[0]) * _L0_xattn_ref(_layernorm(x, axis=-1), ctx_1024, L0_xattn_Wq, L0_xattn_Wkv, L0_xattn_Wout, L0_xattn_bout)
    x = x + jnp.tanh(g_ffn[0]) * _L0_ffn_ref(_layernorm(x, axis=-1), L0_ffn_w_ln1, L0_ffn_Wq, L0_ffn_Wkva, L0_ffn_Wkvb, L0_ffn_Wo, L0_ffn_w_ln2, L0_ffn_Wgate, L0_ffn_expert_bias, L0_ffn_Wg, L0_ffn_Wu, L0_ffn_Wd, L0_ffn_sWg, L0_ffn_sWu, L0_ffn_sWd)
    x = x + jnp.tanh(g_xattn[1]) * _L1_xattn_ref(_layernorm(x, axis=-1), ctx_1024, ctx_1024, mask_Bx1x1xS2_bf1, L1_xattn_w_q, L1_xattn_b_q, L1_xattn_w_k, L1_xattn_b_k, L1_xattn_w_v, L1_xattn_b_v, L1_xattn_w_o, L1_xattn_b_o)
    x = x + jnp.tanh(g_ffn[1]) * _L1_ffn_ref(_layernorm(x, axis=-1), L1_ffn_centroid, L1_ffn_Wg, L1_ffn_bg, L1_ffn_W1, L1_ffn_b1, L1_ffn_W2, L1_ffn_b2)
    return x

_drawn_inputs = setup_inputs


def setup_inputs(seed=0):
    import zlib

    import numpy as np

    out = dict(_drawn_inputs(seed))
    spreads = {'g_ffn': (-1.0, 0.6),
     'L0_xattn_bout': (0.0, 0.1),
     'L0_ffn_w_ln1': (1.0, 0.6),
     'L0_ffn_w_ln2': (1.0, 0.6),
     'L0_ffn_expert_bias': (0.0, 0.8),
     'L1_ffn_bg': (0.0, 0.8),
     'L1_ffn_b1': (0.0, 0.8),
     'L1_ffn_b2': (0.0, 0.435)}
    factors = {'L0_ffn_Wq': 8.0,
     'L0_ffn_Wkva': 5.714,
     'L0_ffn_Wkvb': 5.628,
     'L0_ffn_Wo': 5.453,
     'L0_ffn_Wgate': 4.472,
     'L0_ffn_Wg': 4.143,
     'L0_ffn_Wu': 4.112,
     'L0_ffn_Wd': 3.995,
     'L0_ffn_sWg': 3.104,
     'L0_ffn_sWu': 3.079,
     'L0_ffn_sWd': 2.953,
     'L1_xattn_b_k': 64.0,
     'L1_xattn_b_q': 8.0,
     'L1_xattn_b_v': 3.485,
     'L1_xattn_b_o': 3.296,
     'L1_ffn_Wg': 3.451,
     'L1_ffn_W1': 3.625}
    for name, (base, spread) in spreads.items():
        noise = np.random.default_rng([zlib.crc32(name.encode()), seed]).standard_normal(out[name].shape)
        drawn = base * np.exp(spread * noise) if base else spread * noise
        out[name] = jnp.asarray(drawn.astype(out[name].dtype))
    for name, factor in factors.items():
        out[name] = (out[name] * factor).astype(out[name].dtype)
    return out
```

```python
from contextlib import ExitStack

import numpy as np

import concourse.bass as bass
from concourse import mybir

F32 = mybir.dt.float32
F32R = mybir.dt.float32r
U8 = mybir.dt.uint8
ALU = mybir.AluOpType
ACT = mybir.ActivationFunctionType
AX_X = mybir.AxisListType.X

B, S, D = 8, 100, 256
KV = 361
T = B * S
P = 128
KD = D // P
HALF = T // 2
HB = HALF // S
H0, DH0 = 16, 64
TI0 = H0 * DH0 // P
NC = -(-KV // S)
NOPE = ROPE = LAT = 32
H1, DH1 = 16, 16
E0, I0 = 8, 128
E1, HID1 = 8, 684
HT1 = 6
HW1 = HID1 // HT1
CH = 121
CHS = [CH, CH, KV - 2 * CH]
NEG = -1.0e30
EPS = 1e-5
THETA = 100000.0


def program(nc, t):
    with ExitStack() as ctx:
        base = {}

        def sb(name, shape, dt=F32):
            base[name] = nc.sbuf_base
            return ctx.enter_context(nc.sbuf_tensor(name, shape, dt))

        def part(name, shape, region, at):
            return nc.alloc_sbuf_tensor_at(name, shape, F32R, offset=base[region] + 4 * at)

        X = sb("X", [P, KD, T])
        Y = sb("Y", [P, KD, T])
        XC = sb("XC", [P, KD, T])
        SQ = sb("SQ", [P, KD, T])
        STD = sb("STD", [P, 2, HALF])
        CTX = sb("CTX", [P, 3, KD, KV])
        RQ = sb("RQ", [P, 6400])
        RO = sb("RO", [P, 6400])
        RW = sb("RW", [P, 12640])
        RB = sb("RB", [P, 11400])
        WK = sb("WK", [P, 6, 400])
        IDN = sb("IDN", [P, P])
        AVG = sb("AVG", [P, P])
        HS = sb("HS", [P, TI0 * H0])
        CS = sb("CS", [P, 2, S])
        CM = sb("CM", [S, S])
        PAR = sb("PAR", [P, 8])
        RANK = sb("RANK", [S, 8])
        ONES = sb("ONES", [P, S])
        COLS = sb("COLS", [P, 16])
        G4 = sb("G4", [P, 4])
        TG = sb("TG", [P, 4])
        GB = sb("GB", [P, 4])
        SM0 = sb("SM0", [H0, 6, S])
        RT = sb("RT", [S, 14, B * 8])
        RTC = sb("RTC", [S, 8, B])
        WT8 = sb("WT8", [8, T])
        EB = sb("EB", [S, 8])
        B2E = sb("B2E", [E1, D])
        SM1 = sb("SM1", [S, 3, 6])
        PS = ctx.enter_context(nc.psum_tensor("PS", [P, 8, 512], F32))

        def cut(region, at, n, parts=P):
            return region[0:parts, at:at + n]

        WQ0 = cut(RW, 0, 2048).rearrange("p (k c) -> p k c", k=KD)
        WKV0 = cut(RW, 2048, 4096).rearrange("p (k c) -> p k c", k=KD)
        WOUT0 = cut(RW, 6144, 2048).rearrange("p (t c) -> p t c", t=TI0)
        PROD = cut(RW, 8192, 1200).rearrange("p (s c) -> p s c", s=3)
        VSB = cut(RW, 9392, 1200).rearrange("p (s c) -> p s c", s=3)
        PV = cut(RW, 10592, 800).rearrange("p (s c) -> p s c", s=2)
        SE = cut(RW, 11392, 1200, H0).rearrange("p (s c) -> p s c", s=3)
        SPREAD = SQ[:, :, :].rearrange("p k c -> p (k c)")[0:H0, 0:TI0 * P].rearrange("p (t c) -> p t c", t=TI0)
        QT0 = cut(RQ, 0, TI0 * T).rearrange("p (t c) -> p t c", t=TI0)
        OT0 = cut(RO, 0, TI0 * T).rearrange("p (t c) -> p t c", t=TI0)
        WQT = cut(RB, 0, 2048).rearrange("p (t c) -> p t c", t=8)
        GKV = cut(RB, 2048, 1024).rearrange("p (t c) -> p t c", t=8)
        WKVA = cut(RB, 3072, 256).rearrange("p (k c) -> p k c", k=KD)
        WQA = cut(RB, 3328, 2048).rearrange("p (k c) -> p k c", k=KD)
        BDV = cut(RB, 5376, 512).rearrange("p (t c) -> p t c", t=4)
        WO0 = cut(RB, 5888, 1024).rearrange("p (t c) -> p t c", t=4)
        WOA = cut(RB, 6912, 1024).rearrange("p (t c) -> p t c", t=4)
        CK = cut(RB, 7936, 800)
        CK2 = cut(RB, 8736, 800)
        PT0 = cut(RB, 9536, 1600, S).rearrange("p (s c) -> p s c", s=2)
        LT = cut(RB, 11136, 256, S).rearrange("p (b c) -> p b c", b=B)
        QP = QT0
        UT = cut(RO, 0, 3200).rearrange("p (t c) -> p t c", t=4)
        SMB = cut(RO, 3200, 1600, S).rearrange("p (s c) -> p s c", s=2)
        PB = cut(RO, 4800, 1600, S).rearrange("p (s c) -> p s c", s=2)
        WG0 = cut(RW, 0, 2304).rearrange("p (k c) -> p k c", k=KD)
        WU0 = cut(RW, 2304, 2304).rearrange("p (k c) -> p k c", k=KD)
        WD0 = cut(RW, 4608, 2304).rearrange("p (t c) -> p t c", t=E0 + 1)
        WGT0 = cut(RW, 6912, 16).rearrange("p (k c) -> p k c", k=KD)
        W1A = cut(RW, 6928, 2048).rearrange("p (w k c) -> p w k c", w=4, k=KD)
        MK8 = cut(RW, 8976, 722, S)
        MKB = cut(RW, 9698, 2888, S).rearrange("p (b c) -> p b c", b=B)
        QC = cut(RQ, 0, 1600).rearrange("p (m c) -> p m c", m=KD)
        VP = cut(RQ, 1600, 3072, CH).rearrange("p (s a c d) -> p s a c d", s=2, a=2, c=3)
        KT = cut(RQ, 4672, 1444).rearrange("p (s m c) -> p s m c", s=2, m=KD)
        QX = cut(RO, 0, 3200).rearrange("p (s m a c) -> p s m a c", s=2, m=KD, a=8)
        SMK = cut(RO, 3200, 4 * KV, S).rearrange("p (s c) -> p s c", s=4)
        OT1 = cut(RO, 4672, 1600).rearrange("p (t c) -> p t c", t=KD)
        PC = cut(RB, 8544, 5 * 3 * CH, S).rearrange("p (s c) -> p s c", s=5)
        PTC = cut(RB, 8544 + 5 * 3 * CH, 900, CH).rearrange("p (s c) -> p s c", s=3)
        WEB = cut(RQ, 0, E1 * T).rearrange("p (e c) -> p e c", e=E1)
        RING = RB[:, 0:2 * (4 * HID1 + HT1 * D)].rearrange("p (s c) -> p s c", s=2)
        BIAS1 = cut(RW, 0, 2 * E1 * HT1, HW1)
        CENT = cut(RW, 96, 16).rearrange("p (k c) -> p k c", k=KD)
        CENT2 = cut(RW, 112, 16).rearrange("p (k c) -> p k c", k=KD)
        CENTSQ = cut(RW, 128, 16).rearrange("p (k c) -> p k c", k=KD)
        EXPERT = 4 * HID1 + HT1 * D
        RINGH = part("RINGH", [P, 2, EXPERT], "RW", 192)
        RINGL = part("RINGL", [P, 2, EXPERT], "RB", 0)
        XH = part("XH", [P, KD, T], "RO", 0)
        XL = part("XL", [P, KD, T], "RO", KD * T)
        HTH = part("HTH", [P, 3, HALF], "RO", 2 * KD * T)
        HTL = part("HTL", [P, 3, HALF], "RO", 2 * KD * T + 3 * HALF)
        SIL = WK[:, 0:3, :]
        HT = WK[:, 3:6, :]
        QS = WK[:, 0:3, :]
        SH = WK[:, 3:6, :]

        names = """x_loaded constants_loaded vectors_loaded a_wq_loaded a_wkv_loaded a_wout_loaded context_loaded0
            context_loaded1 context_loaded2 b_weights_loaded moe0_weights_loaded c_weights_loaded
            mask_loaded moe1_small_loaded expert_loaded0 expert_loaded1 out_stored zeros_set
            psum_tails_set a_spread_rows_built dve_step_done gates_ready gated_biases_ready
            norm_mean_summed norm_centred norm_squared norm_variance_summed norm_log_taken
            norm_rstd_ready norm_done a_query_summed a_query_copied a_keys_summed a_products_ready
            a_similarity_summed a_shifted a_exp_taken a_weights_ready a_weights_spread
            a_values_summed a_values_copied a_weighted a_heads_mixed a_output_summed a_output_gated
            a_added_to_x b_weights_folded b_folded_copied b_latent_summed b_latent_rotated
            b_latent_copied b_latent_rows_summed b_latent_rows_copied b_query_summed b_query_copied
            b_query_read b_query_rotated b_scores_summed b_scores_shifted b_exp_taken b_probs_ready
            b_probs_turned b_turned_copied b_heads_mixed b_mixed_copied b_output_summed b_added_to_y
            router_scores_summed router_scores_shifted router_function_taken router_weights_ready
            router_weights_turned router_turned_copied router_weights_spread router_spread_copied
            router_squares_ready gate_summed up_summed gate_activated hidden_ready hidden_weighed
            hidden_high_ready hidden_low_ready down_summed moe_added_to_x x_high_ready x_low_ready
            expert_high_ready expert_low_ready c_query_summed c_query_copied c_query_split
            c_keys_summed c_keys_copied c_values_summed c_values_copied c_scores_summed
            c_maximum_found c_exp_taken c_sum_inverted c_probs_ready c_probs_turned c_turned_copied
            c_heads_mixed c_mixed_copied c_output_summed c_output_gated c_added_to_x mask_ready""".split()
        sem = {n: ctx.enter_context(nc.semaphore(n)) for n in names}

        def half(n):
            return slice(n * HALF, (n + 1) * HALF)

        def tok(b):
            return slice(b * S, (b + 1) * S)

        NORM = [(X, XC, "layer"), (X, Y, "layer"), (Y, XC, 0), (Y, XC, 2), (X, XC, "layer"), (X, XC, "layer")]
        LAYER = {0: 0, 1: 1, 4: 2, 5: 3}
        SOURCE = [("x_loaded", lambda n: 16), ("a_added_to_x", lambda n: 2 * n + 2), ("norm_done", lambda n: 2 + n + 1),
                  ("b_added_to_y", lambda n: 2 * n + 2), ("moe_added_to_x", lambda n: 2 * n + 2), ("c_added_to_x", lambda n: 2 * n + 2)]

        TILES0 = [(e, 0) for e in range(E0 + 1)]
        TILES1 = [(e, m) for e in range(E1) for m in range(HT1)]
        N0, N1 = 2 * len(TILES0), 2 * len(TILES1)
        ROUTED0, ROUTED1 = 2 * E0, N1

        def ring(e):
            return expert(RING[:, e % 2, :])

        def expert(r):
            return (r[:, 0:2 * HID1].rearrange("p (k c) -> p k c", k=KD),
                    r[:, 2 * HID1:4 * HID1].rearrange("p (k c) -> p k c", k=KD),
                    r[0:HW1, 4 * HID1:4 * HID1 + HT1 * D].rearrange("p (m c) -> p m c", m=HT1))

        def tile_of(r, m, down):
            if down:
                return expert(r)[2][:, m, :]
            return r[:, 0:4 * HID1].rearrange("p (w c) -> p w c", w=4)[:, :, m * HW1:(m + 1) * HW1]

        SPLIT = HT1

        HEADS1 = [(ti, par, j) for ti in range(KD) for par in range(2) for j in range(4)]

        PIECES = [3, 5, 7, 9]
        TURN, MIX = 3, 5

        block = ctx.enter_context(nc.Block())

        @block.sync
        def _(sp):
            def load(dst, src, name):
                sp.dma_start(dst, src).then_inc(sem[name], 16)

            load(X[:, :, :], t["xT"], "x_loaded")
            for dst, name in ((IDN, "ident"), (AVG, "avg"), (HS, "headsum"), (CS, "rope"), (CM, "causal"),
                              (PAR, "parity"), (RANK, "rank"), (ONES, "ones")):
                load(dst[:, :] if len(dst.shape) == 2 else dst[:, :, :], t[name], "constants_loaded")
            load(WQ0, t["WQ0"], "a_wq_loaded")

            def load_ctx(i):
                b = i % B
                if i >= 3:
                    j = i - 3
                    if j < B:
                        sp.wait_ge(sem["a_values_summed"], TI0 * (j + 1))
                    else:
                        sp.wait_ge(sem["c_values_summed"], 2 * (j - B + 1))
                load(CTX[:, i % 3, :, :], t["ctxT"][:, b, :, :], f"context_loaded{i % 3}")

            load(COLS[:, :], t["cols"], "vectors_loaded")
            load(G4[:, :], t["gates"].partition_broadcast(P), "vectors_loaded")
            load(EB[:, :], t["ebias"].partition_broadcast(S), "vectors_loaded")
            load(B2E[:, :], t["b2"], "vectors_loaded")
            load_ctx(0)
            load(WKV0, t["WKV0"], "a_wkv_loaded")
            load_ctx(1)
            load_ctx(2)
            load(WOUT0, t["WOUT0"], "a_wout_loaded")
            for dst, name in ((WQT, "WQT"), (GKV, "GKV"), (WKVA, "WKVA"), (BDV, "BDV"), (WO0, "WO0")):
                load(dst, t[name], "b_weights_loaded")
            for b in range(3, B):
                load_ctx(b)
            sp.wait_ge(sem["a_output_summed"], 4)
            sp.wait_ge(sem["a_heads_mixed"], TI0 * B)
            for dst, name in ((WG0, "WG0"), (WU0, "WU0"), (WD0, "WD0"), (WGT0, "WGT0")):
                load(dst, t[name], "moe0_weights_loaded")
            load(W1A, t["W1A"], "c_weights_loaded")
            load(MK8.bitcast(U8), t["mask"].partition_broadcast(S), "mask_loaded")
            for i in range(B, B + 3):
                load_ctx(i)

            def load_expert(e):
                g, u, d = ring(e)
                if e >= 2:
                    sp.wait_ge(sem["down_summed"], N0 + 2 * HT1 * (e - 1))
                load(g, t["WG1"][e], f"expert_loaded{e % 2}")
                load(u, t["WU1"][e], f"expert_loaded{e % 2}")
                load(d, t["WD1"][e], f"expert_loaded{e % 2}")

            sp.wait_ge(sem["b_output_summed"], 4)
            sp.wait_ge(sem["b_mixed_copied"], 2 * B)
            load_expert(0)
            load_expert(1)
            for i in range(B + 3, 2 * B):
                load_ctx(i)
            sp.wait_ge(sem["down_summed"], N0)
            load(BIAS1, t["bias1"], "moe1_small_loaded")
            load(CENT, t["centT"], "moe1_small_loaded")
            for e in range(2, E1):
                load_expert(e)
            sp.wait_ge(sem["moe_added_to_x"], 8)
            load_out = sp.dma_start(t["outT"], X[:, :, :])
            load_out.then_inc(sem["out_stored"], 16)
            sp.wait_ge(sem["out_stored"], 16)

        @block.tensor
        def _(pe):
            def mm(out, lhsT, rhs, start, stop):
                return pe.matmul(out, lhsT, rhs, start=start, stop=stop)

            def norm(i):
                src, _, kind = NORM[i]
                for n in range(2):
                    if kind == "layer":
                        pe.wait_ge(sem[SOURCE[i][0]], SOURCE[i][1](n))
                        for k in range(KD):
                            m = mm(PS[:, 4 + n, 0:HALF], AVG[:, :], src[:, k, half(n)], k == 0, k == KD - 1)
                        m.then_inc(sem["norm_mean_summed"], 1)
                for n in range(2):
                    pe.wait_ge(sem["norm_squared"], 2 * i + n + 1)
                    for k in range(KD):
                        m = mm(PS[:, 4 + n, 0:HALF], AVG[:, :], SQ[:, k, half(n)], k == 0, k == KD - 1)
                    m.then_inc(sem["norm_variance_summed"], 1)

            pe.wait_ge(sem["constants_loaded"], 16 * 8)
            norm(0)
            pe.wait_ge(sem["a_wq_loaded"], 16)
            for i in range(2 * TI0):
                ti, n = divmod(i, 2)
                pe.wait_ge(sem["norm_done"], n + 1)
                if i > 1:
                    pe.wait_ge(sem["a_query_copied"], i - 1)
                for k in range(KD):
                    m = mm(PS[:, 4 + i % 2, 0:HALF], WQ0[:, k, ti * P:(ti + 1) * P], XC[:, k, half(n)], k == 0, k == 1)
                m.then_inc(sem["a_query_summed"], 1)
            pe.wait_ge(sem["a_wkv_loaded"], 16)
            pe.wait_ge(sem["a_query_copied"], 2 * TI0)
            pe.wait_ge(sem["psum_tails_set"], 1)

            def sim(b, ti):
                i = TI0 * b + ti
                pe.wait_ge(sem["a_products_ready"], i + 1)
                if b > 1:
                    pe.wait_ge(sem["a_shifted"], b - 1)
                mm(PS[0:H0, 2 + b % 2, 0:KV], HS[:, ti * H0:(ti + 1) * H0], PROD[:, i % 3, 0:KV],
                       ti == 0, ti == TI0 - 1).then_inc(sem["a_similarity_summed"], 1)

            def keys(b):
                pe.wait_ge(sem[f"context_loaded{b % 3}"], 16 * (b // 3 + 1))
                for ti in range(TI0):
                    i = TI0 * b + ti
                    if i > 1:
                        pe.wait_ge(sem["a_products_ready"], i - 1)
                    for k in range(KD):
                        m = mm(PS[:, i % 2, 0:KV], WKV0[:, k, ti * P:(ti + 1) * P], CTX[:, b % 3, k, :], k == 0, k == 1)
                    m.then_inc(sem["a_keys_summed"], 1)
                    if i:
                        sim((i - 1) // TI0, (i - 1) % TI0)

            def values(b):
                pe.wait_ge(sem["a_weights_ready"], b + 1)
                pe.wait_ge(sem["a_spread_rows_built"], 1)
                for ti in range(TI0):
                    i = TI0 * b + ti
                    if i > 1:
                        pe.wait_ge(sem["a_weighted"], i - 1)
                    mm(PS[:, 6 + i % 2, 0:KV], SPREAD[:, ti, :], SE[:, 1 + b % 2, 0:KV], True, True).then_inc(sem["a_weights_spread"], 1)
                    if i > 1:
                        pe.wait_ge(sem["a_values_copied"], i - 1)
                    for k in range(KD):
                        m = mm(PS[:, 4 + i % 2, 0:KV], WKV0[:, k, (TI0 + ti) * P:(TI0 + ti + 1) * P],
                               CTX[:, b % 3, k, :], k == 0, k == 1)
                    m.then_inc(sem["a_values_summed"], 1)

            for b in range(B):
                keys(b)
                if b:
                    values(b - 1)
            sim(B - 1, TI0 - 1)
            values(B - 1)
            pe.wait_ge(sem["a_wout_loaded"], 16)
            pe.wait_ge(sem["a_heads_mixed"], TI0 * B)
            for n in range(2):
                for mo in range(KD):
                    for ti in range(TI0):
                        m = mm(PS[:, 2 * n + mo, 0:HALF], WOUT0[:, ti, mo * P:(mo + 1) * P], OT0[:, ti, half(n)],
                               ti == 0, ti == TI0 - 1)
                    m.then_inc(sem["a_output_summed"], 1)

            pe.wait_ge(sem["b_weights_loaded"], 16 * 5)
            for i in range(4):
                if i > 1:
                    pe.wait_ge(sem["b_folded_copied"], i - 1)
                for ti in range(4):
                    c = i // 2
                    tq = 4 * (i % 2) + ti
                    m = mm(PS[:, 6 + i % 2, ti * P:(ti + 1) * P], WQT[:, tq, c * P:(c + 1) * P], GKV[:, tq, :], True, True)
                m.then_inc(sem["b_weights_folded"], 1)
            for i in range(2):
                pe.wait_ge(sem["b_folded_copied"], i + 3)
                for j in range(2):
                    m = mm(PS[:, 6 + i, j * D:(j + 1) * D], BDV[:, 2 * i + j, :], WO0[:, 2 * i + j, :], True, True)
                m.then_inc(sem["b_weights_folded"], 1)
            norm(1)
            norm(2)
            for n in range(2):
                pe.wait_ge(sem["norm_done"], 4 + n + 1)
                pe.wait_ge(sem["a_output_gated"], 4)
                for k in range(KD):
                    m = mm(PS[:, n, 0:HALF], WKVA[:, k, :], XC[:, k, half(n)], k == 0, k == 1)
                m.then_inc(sem["b_latent_summed"], 1)
            for b in range(B):
                for k in range(KD):
                    m = mm(PS[0:S, 2, b * LAT:(b + 1) * LAT], XC[:, k, tok(b)], WKVA[:, k, 0:LAT], k == 0, k == 1)
            m.then_inc(sem["b_latent_rows_summed"], 1)
            pe.wait_ge(sem["b_folded_copied"], 6)
            for i in range(16):
                tq, n = divmod(i, 2)
                if i > 3:
                    pe.wait_ge(sem["b_query_copied"], i - 3)
                for k in range(KD):
                    m = mm(PS[:, 4 + i % 4, 0:HALF], WQA[:, k, tq * P:(tq + 1) * P], XC[:, k, half(n)], k == 0, k == 1)
                m.then_inc(sem["b_query_summed"], 1)

            def qk(i):
                b, g = divmod(i, 2)
                if i == 0:
                    pe.wait_ge(sem["b_latent_rows_copied"], 1)
                    pe.wait_ge(sem["b_latent_rotated"], 2)
                    pe.wait_ge(sem["b_query_rotated"], 16)
                if i > 1:
                    pe.wait_ge(sem["b_scores_shifted"], i - 1)
                for x in range(4):
                    for par in range(2):
                        lo = slice(64 * par, 64 * par + 64)
                        m = mm(PS[0:S, 2 * (i % 2) + par, x * S:(x + 1) * S], QP[lo, 4 * g + x, tok(b)],
                               CK[lo, tok(b)], True, True)
                m.then_inc(sem["b_scores_summed"], 1)

            def turn(i):
                pe.wait_ge(sem["b_probs_ready"], i + 1)
                for q in range(2):
                    if 2 * i + q > 1:
                        pe.wait_ge(sem["b_turned_copied"], 2 * i + q - 1)
                    for x in range(4):
                        m = pe.transpose(PS[0:S, 4 + q, x * S:(x + 1) * S], PB[:, i % 2, (4 * q + x) * S:(4 * q + x + 1) * S],
                                         IDN[0:S, 0:S])
                    m.then_inc(sem["b_probs_turned"], 1)

            def mix(i):
                b, g = divmod(i, 2)
                pe.wait_ge(sem["b_turned_copied"], 2 * i + 2)
                if i > 1:
                    pe.wait_ge(sem["b_mixed_copied"], i - 1)
                for j in range(4):
                    at = (4 * (j % 2) + j // 2) * S
                    rhs = PT0[:, i % 2, at:at + 3 * S].rearrange("p (x c) -> p x c", c=S)[:, 0:3:2, :]
                    m = mm(PS[32 * j:32 * j + 32, 6 + i % 2, 0:2 * S], LT[:, b, :], rhs, True, True)
                m.then_inc(sem["b_heads_mixed"], 1)

            for i in range(2 * B + 2):
                if i < 2 * B:
                    qk(i)
                if 1 <= i <= 2 * B:
                    turn(i - 1)
                if i >= 2:
                    mix(i - 2)
            pe.wait_ge(sem["b_mixed_copied"], 2 * B)
            for n in range(2):
                for mo in range(KD):
                    for ti in range(4):
                        m = mm(PS[:, 2 * n + mo, 0:HALF], WOA[:, ti, mo * P:(mo + 1) * P], UT[:, ti, half(n)],
                               ti == 0, ti == 3)
                    m.then_inc(sem["b_output_summed"], 1)
            norm(3)

            def mixture(which, tiles):
                first = 0 if which == 0 else N0
                pe.wait_ge(sem["norm_done"], (8, 12)[which])
                if which:
                    pe.wait_ge(sem["router_squares_ready"], 3)
                    pe.wait_ge(sem["vectors_loaded"], 64)
                for b in range(B):
                    out = PS[0:S, 6, b * 8:(b + 1) * 8]
                    if which == 0:
                        pe.wait_ge(sem["moe0_weights_loaded"], 64)
                        pairs = [(XC[:, k, tok(b)], WGT0[:, k, :]) for k in range(KD)]
                    else:
                        pairs = [(XC[:, k, tok(b)], CENT2[:, k, :]) for k in range(KD)]
                        pairs += [(SQ[:, k, tok(b)], ONES[:, 0:8]) for k in range(KD)]
                        pairs += [(ONES[:, 0:S], CENTSQ[:, k, :]) for k in range(KD)]
                    for c, (lhsT, rhs) in enumerate(pairs):
                        m = mm(out, lhsT, rhs, c == 0, c == len(pairs) - 1)
                m.then_inc(sem["router_scores_summed"], 1)
                pe.wait_ge(sem["router_weights_ready"], which + 1)
                for q in range(2):
                    for b in range(4):
                        bb = 4 * q + b
                        m = pe.transpose(PS[0:8, 4 + q, b * S:(b + 1) * S], RT[:, 13, bb * 8:(bb + 1) * 8], IDN[0:S, 0:S])
                    m.then_inc(sem["router_weights_turned"], 1)
                pe.wait_ge(sem["router_turned_copied"], 2 * which + 2)
                for i in range(16):
                    e, n = divmod(i, 2)
                    if 16 * which + i > 3:
                        pe.wait_ge(sem["router_spread_copied"], 16 * which + i - 3)
                    lhsT = IDN[0:8, e:e + 1].to_broadcast([8, P])
                    mm(PS[:, 4 + i % 4, 0:HALF], lhsT, WT8[:, half(n)], True, True).then_inc(sem["router_weights_spread"], 1)
                pe.wait_ge(sem["router_spread_copied"], 16 * which + 16)

                if which:
                    for n in range(2):
                        for mo in range(KD):
                            mm(PS[:, 2 * n + mo, 0:HALF], B2E[:, mo * P:(mo + 1) * P], WT8[:, half(n)], True, False)

                def up(i):
                    (e, m_), n = tiles[i // 2], i % 2
                    if which == 0:
                        g, u, w = WG0[:, :, e * I0:(e + 1) * I0], WU0[:, :, e * I0:(e + 1) * I0], I0
                    else:
                        hi, lo = expert(RINGH[:, e % 2, :]), expert(RINGL[:, e % 2, :])
                        pe.wait_ge(sem["expert_low_ready"], 2 * (i // 2) + 1)
                        pe.wait_ge(sem["x_low_ready"], n + 1)
                        if first + i > 1:
                            pe.wait_ge(sem["hidden_ready"], first + i - 1)
                        for c, name in enumerate(("gate_summed", "up_summed")):
                            out = PS[0:HW1, 4 + c + 2 * (i % 2), 0:HALF]
                            cols = slice(m_ * HW1, (m_ + 1) * HW1)
                            for k in range(KD):
                                mm(out, hi[c][:, k, cols], XH[:, k, half(n)], k == 0, False)
                                mm(out, hi[c][:, k, cols], XL[:, k, half(n)], False, False)
                                m = mm(out, lo[c][:, k, cols], XH[:, k, half(n)], False, k == 1)
                            m.then_inc(sem[name], 1)
                        return
                    if first + i > 1:
                        pe.wait_ge(sem["hidden_ready"], first + i - 1)
                    for bank, wt, name in ((4, g, "gate_summed"), (5, u, "up_summed")):
                        for k in range(KD):
                            m = mm(PS[0:w, bank + 2 * (i % 2), 0:HALF], wt[:, k, :], XC[:, k, half(n)], k == 0, k == 1)
                        m.then_inc(sem[name], 1)

                def down(i):
                    (e, m_), n = tiles[i // 2], i % 2
                    if which == 0:
                        wd, w = WD0[:, e, :], I0
                    else:
                        pe.wait_ge(sem["expert_low_ready"], 2 * (i // 2) + 2)
                        pe.wait_ge(sem["hidden_low_ready"], i + 1)
                        hi, lo = expert(RINGH[:, e % 2, :])[2][:, m_, :], expert(RINGL[:, e % 2, :])[2][:, m_, :]
                        for mo in range(KD):
                            out, cols = PS[:, 2 * n + mo, 0:HALF], slice(mo * P, (mo + 1) * P)
                            mm(out, hi[:, cols], HTH[0:HW1, i % 3, :], False, False)
                            mm(out, hi[:, cols], HTL[0:HW1, i % 3, :], False, False)
                            m = mm(out, lo[:, cols], HTH[0:HW1, i % 3, :], False, i >= 2 * len(tiles) - 2)
                        m.then_inc(sem["down_summed"], 1)
                        return
                    if which == 0 and i >= ROUTED0:
                        pe.wait_ge(sem["hidden_ready"], first + i + 1)
                    else:
                        pe.wait_ge(sem["hidden_weighed"], i + 1)
                    for mo in range(KD):
                        m = mm(PS[:, 2 * n + mo, 0:HALF], wd[:, mo * P:(mo + 1) * P], HT[0:w, i % 3, :],
                               which == 0 and i < 2, i >= 2 * len(tiles) - 2)
                    m.then_inc(sem["down_summed"], 1)

                count = 2 * len(tiles)
                for i in range(count + 2):
                    if i < count:
                        up(i)
                    if i >= 2:
                        down(i - 2)

            pe.wait_ge(sem["b_added_to_y"], 4)
            mixture(0, TILES0)
            norm(4)

            pe.wait_ge(sem["c_weights_loaded"], 16)
            for i in range(4):
                n, mo = divmod(i, 2)
                pe.wait_ge(sem["norm_done"], 8 + n + 1)
                pe.wait_ge(sem["moe_added_to_x"], 4)
                for k in range(KD):
                    m = mm(PS[:, i, 0:HALF], W1A[:, 0, k, mo * P:(mo + 1) * P], XC[:, k, half(n)], k == 0, k == 1)
                m.then_inc(sem["c_query_summed"], 1)

            def project(b, piece):
                ci = B + b
                if piece == 0:
                    pe.wait_ge(sem[f"context_loaded{ci % 3}"], 16 * (ci // 3 + 1))
                    if 4 * b > 0:
                        pe.wait_ge(sem["c_values_copied"], 4 * b)
                if piece < 2:
                    if 2 * b + piece > 0:
                        pe.wait_ge(sem["c_keys_copied"], 2 * b + piece)
                    for k in range(KD):
                        m = mm(PS[:, 7, 0:KV], W1A[:, 1, k, piece * P:(piece + 1) * P], CTX[:, ci % 3, k, :], k == 0, k == 1)
                    m.then_inc(sem["c_keys_summed"], 1)
                elif piece == 2:
                    pe.wait_ge(sem["c_keys_copied"], 2 * b + 2)
                    for c in range(2):
                        for k in range(KD):
                            m = mm(PS[0:CH, 7, c * D:(c + 1) * D], CTX[:, ci % 3, k, c * CH:(c + 1) * CH],
                                   W1A[:, 2, k, :], k == 0, k == 1)
                    m.then_inc(sem["c_values_summed"], 1)
                else:
                    pe.wait_ge(sem["c_values_copied"], 4 * b + 2)
                    for k in range(KD):
                        m = mm(PS[0:CHS[2], 7, 0:D], CTX[:, ci % 3, k, 2 * CH:KV], W1A[:, 2, k, :], k == 0, k == 1)
                    m.then_inc(sem["c_values_summed"], 1)

            def scores(i):
                b, h = i // 16, i % 16
                if h == 0:
                    pe.wait_ge(sem["c_keys_copied"], 2 * b + 2)
                    pe.wait_ge(sem["c_query_split"], KD * (b + 1))
                if i > 3:
                    pe.wait_ge(sem["c_maximum_found"], i - 3)
                mm(PS[0:S, i % 4, 0:KV], QX[:, b % 2, h // 8, h % 8, :], KT[:, b % 2, h // 8, :], True, True).then_inc(sem["c_scores_summed"], 1)

            def turn_p(i):
                pe.wait_ge(sem["c_probs_ready"], i + 1)
                if i > 1:
                    pe.wait_ge(sem["c_turned_copied"], i - 1)
                for c in range(3):
                    m = pe.transpose(PS[0:CH, 4 + i % 2, c * S:(c + 1) * S], PC[:, i % 5, c * CH:(c + 1) * CH], IDN[0:S, 0:S])
                m.then_inc(sem["c_probs_turned"], 1)

            def mix_v(i):
                b, (ti, par, j) = i // 16, HEADS1[i % 16]
                pe.wait_ge(sem["c_turned_copied"], i + 1)
                if i % 16 == 0:
                    pe.wait_ge(sem["c_values_copied"], 4 * b + 4)
                    if b > 0:
                        pe.wait_ge(sem["c_mixed_copied"], b)
                for c in range(3):
                    at = ti * P + 32 * j
                    m = mm(PS[32 * j:32 * j + 32, 6, ti * S:(ti + 1) * S], VP[0:CHS[c], b % 2, par, c, at:at + 32],
                           PTC[0:CHS[c], i % 3, c * S:(c + 1) * S], par == 0 and c == 0, par == 1 and c == 2)
                m.then_inc(sem["c_heads_mixed"], 1)

            for piece in range(4):
                project(0, piece)
            for i in range(16 * B + MIX):
                if i < 16 * B:
                    if i % 16 in PIECES and i // 16 + 1 < B:
                        project(i // 16 + 1, PIECES.index(i % 16))
                    scores(i)
                if 0 <= i - TURN < 16 * B:
                    turn_p(i - TURN)
                if i >= MIX:
                    mix_v(i - MIX)
            pe.wait_ge(sem["c_mixed_copied"], B)
            for n in range(2):
                for mo in range(KD):
                    for ti in range(KD):
                        m = mm(PS[:, 2 * n + mo, 0:HALF], W1A[:, 3, ti, mo * P:(mo + 1) * P], OT1[:, ti, half(n)],
                               ti == 0, ti == KD - 1)
                    m.then_inc(sem["c_output_summed"], 1)
            norm(5)
            mixture(1, TILES1)

        @block.scalar
        def _(act):
            def norm(i):
                src, _, kind = NORM[i]
                for n in range(2):
                    if kind == "layer":
                        act.wait_ge(sem["norm_centred"], 2 * LAYER[i] + n + 1)
                        src_ = XC
                    else:
                        act.wait_ge(sem[SOURCE[i][0]], SOURCE[i][1](n))
                        src_ = src
                    if 2 * i > 0:
                        act.wait_ge(sem["norm_variance_summed"], 2 * i)
                    act.activation(SQ[:, :, half(n)], src_[:, :, half(n)], ACT.Square).then_inc(sem["norm_squared"], 1)
                for n in range(2):
                    act.wait_ge(sem["norm_variance_summed"], 2 * i + n + 1)
                    if 2 * i - 1 + n > 0:
                        act.wait_ge(sem["norm_done"], 2 * i - 1 + n)
                    act.activation(STD[:, n, :], PS[:, 4 + n, 0:HALF], ACT.Ln, bias=COLS[:, 15:16]).then_inc(sem["norm_log_taken"], 1)
                    act.wait_ge(sem["norm_log_taken"], 2 * i + n + 1)
                    act.activation(STD[:, n, :], STD[:, n, :], ACT.Exp, scale=-0.5).then_inc(sem["norm_rstd_ready"], 1)

            def add_bias(name, first, col, gate, done, slots):
                for i in range(4):
                    n, mo = divmod(i, 2)
                    act.wait_ge(sem[name], i + 1)
                    if i == 0:
                        act.wait_ge(sem["gated_biases_ready"], 4)
                    act.activation(slots[i], PS[:, i, 0:HALF], ACT.Identity, bias=GB[:, col + mo:col + mo + 1],
                                       scale=TG[:, gate:gate + 1]).then_inc(sem[done], 1)

            act.wait_ge(sem["vectors_loaded"], 64)
            act.activation(TG[:, :], G4[:, :], ACT.Tanh).then_inc(sem["gates_ready"], 1)
            act.preload_act_table_set("natural_log_exp_and_others")
            norm(0)
            for i in range(2 * TI0):
                ti, n = divmod(i, 2)
                act.wait_ge(sem["a_query_summed"], i + 1)
                act.activation(QT0[:, ti, half(n)], PS[:, 4 + i % 2, 0:HALF], ACT.Copy, scale=DH0 ** -0.5).then_inc(sem["a_query_copied"], 1)

            def exps(b):
                act.wait_ge(sem["a_shifted"], b + 1)
                if b > 0:
                    act.wait_ge(sem["a_weights_ready"], b)
                act.activation(SE[:, 0, :], SE[:, 0, :], ACT.Exp).then_inc(sem["a_exp_taken"], 1)

            def vcopy(b):
                act.wait_ge(sem["zeros_set"], 1)
                for ti in range(TI0):
                    i = TI0 * b + ti
                    act.wait_ge(sem["a_values_summed"], i + 1)
                    if i > 2:
                        act.wait_ge(sem["a_weighted"], i - 2)
                    act.copy(VSB[:, i % 3, 0:KV], PS[:, 4 + i % 2, 0:KV]).then_inc(sem["a_values_copied"], 1)

            exps(0)
            for b in range(B - 1):
                vcopy(b)
                exps(b + 1)
            vcopy(B - 1)
            add_bias("a_output_summed", 0, 0, 0, "a_output_gated", [WK[:, i, :] for i in range(4)])

            for i in range(6):
                act.wait_ge(sem["b_weights_folded"], i + 1)
                if i < 4:
                    dst = WQA[:, i // 2, 512 * (i % 2):512 * (i % 2) + 512]
                    src = PS[:, 6 + i % 2, :]
                else:
                    dst = WOA[:, 2 * (i - 4):2 * (i - 4) + 2, :]
                    src = PS[:, 6 + i % 2, :].rearrange("p (t c) -> p t c", t=2)
                act.copy(dst, src).then_inc(sem["b_folded_copied"], 1)
            norm(1)
            norm(2)
            for n in range(2):
                act.wait_ge(sem["b_latent_summed"], n + 1)
                act.copy(CK[:, half(n)], PS[:, n, 0:HALF]).then_inc(sem["b_latent_copied"], 1)
            act.wait_ge(sem["b_latent_rows_summed"], 1)
            act.copy(LT, PS[0:S, 2, 0:B * LAT].rearrange("p (b c) -> p b c", b=B)).then_inc(sem["b_latent_rows_copied"], 1)
            act.wait_ge(sem["a_added_to_x"], 4)
            for i in range(16):
                act.wait_ge(sem["b_query_summed"], i + 1)
                if 2 * (i - 2) > 0:
                    act.wait_ge(sem["b_query_read"], 2 * (i - 2))
                act.copy(QS[:, i % 3, :], PS[:, 4 + i % 4, 0:HALF]).then_inc(sem["b_query_copied"], 1)

            def exp_b(i):
                act.wait_ge(sem["b_scores_shifted"], i + 1)
                if 2 * (i - 1) > 0:
                    act.wait_ge(sem["b_probs_turned"], 2 * (i - 1))
                act.activation(PB[:, i % 2, :], SMB[:, i % 2, :], ACT.Exp, scale=0.125).then_inc(sem["b_exp_taken"], 1)

            def turn_b(i):
                for q in range(2):
                    act.wait_ge(sem["b_probs_turned"], 2 * i + q + 1)
                    if i > 1:
                        act.wait_ge(sem["b_heads_mixed"], i - 1)
                    act.copy(PT0[:, i % 2, 4 * q * S:4 * (q + 1) * S], PS[0:S, 4 + q, 0:4 * S]).then_inc(sem["b_turned_copied"], 1)

            def mix_b(i):
                b, g = divmod(i, 2)
                act.wait_ge(sem["b_heads_mixed"], i + 1)
                act.copy(UT[:, 2 * g:2 * g + 2, tok(b)],
                             PS[:, 6 + i % 2, 0:2 * S].rearrange("p (t c) -> p t c", t=2)).then_inc(sem["b_mixed_copied"], 1)

            for i in range(2 * B + 2):
                if i < 2 * B:
                    exp_b(i)
                if 1 <= i <= 2 * B:
                    turn_b(i - 1)
                if i >= 2:
                    mix_b(i - 2)
            norm(3)

            def split_hi(e, m):
                act.wait_ge(sem[f"expert_loaded{e % 2}"], 48 * (e // 2 + 1))
                if N0 + 2 * HT1 * (e - 1) if e > 1 else N0 > 0:
                    act.wait_ge(sem["down_summed"], N0 + 2 * HT1 * (e - 1) if e > 1 else N0)
                if e:
                    act.wait_ge(sem["c_output_summed"], 4)
                for down in range(2):
                    rows = HW1 if down else P
                    act.copy(tile_of(RINGH[0:rows, e % 2, :], m, down), tile_of(RING[0:rows, e % 2, :], m, down)).then_inc(sem["expert_high_ready"], 1)

            def mixture(which, tiles):
                first = (0, N0)[which]
                if which == 1:
                    for n in range(2):
                        act.wait_ge(sem["norm_done"], 10 + n + 1)
                        act.wait_ge(sem["c_output_summed"], 4)
                        act.copy(XH[:, :, half(n)], XC[:, :, half(n)]).then_inc(sem["x_high_ready"], 1)
                    act.wait_ge(sem["norm_done"], 12)
                    act.activation(SQ[:, :, :], XC[:, :, :], ACT.Square).then_inc(sem["router_squares_ready"], 1)
                    act.wait_ge(sem["moe1_small_loaded"], 32)
                    act.activation(CENTSQ, CENT, ACT.Square).then_inc(sem["router_squares_ready"], 1)
                    act.activation(CENT2, CENT, ACT.Copy, scale=-2.0).then_inc(sem["router_squares_ready"], 1)
                    act.wait_ge(sem["router_scores_shifted"], 2)
                    act.activation(RT[:, 0, :], RT[:, 0, :], ACT.Sqrt).then_inc(sem["router_function_taken"], 1)
                act.wait_ge(sem["router_scores_shifted"], (1, 3)[which])
                dst = RT[:, 0, :] if which == 0 else RTC[:, 2, :]
                act.activation(dst, dst, ACT.Exp).then_inc(sem["router_function_taken"], 1)
                for q in range(2):
                    act.wait_ge(sem["router_weights_turned"], 2 * which + q + 1)
                    act.copy(WT8[:, half(q)], PS[0:8, 4 + q, 0:HALF]).then_inc(sem["router_turned_copied"], 1)
                for i in range(16):
                    e, n = divmod(i, 2)
                    act.wait_ge(sem["router_weights_spread"], 16 * which + i + 1)
                    act.copy(WEB[:, e, half(n)], PS[:, 4 + i % 4, 0:HALF]).then_inc(sem["router_spread_copied"], 1)
                for i in range(2 * len(tiles)):
                    e, m_ = tiles[i // 2]
                    w = (I0, HW1)[which]
                    act.wait_ge(sem["gate_summed"], first + i + 1)
                    if first + i > 2:
                        act.wait_ge(sem["hidden_ready"], first + i - 2)
                    col = e * HT1 + m_
                    bias = 0.0 if which == 0 else BIAS1[:, col:col + 1]
                    act.activation(SIL[0:w, i % 3, :], PS[0:w, 4 + 2 * (i % 2), 0:HALF], ACT.Silu, bias=bias).then_inc(sem["gate_activated"], 1)
                    if which == 1:
                        act.wait_ge(sem["hidden_weighed"], ROUTED0 + i + 1)
                        act.copy(HTH[0:w, i % 3, :], HT[0:w, i % 3, :]).then_inc(sem["hidden_high_ready"], 1)
                        if i % 12 >= SPLIT and e + 1 < E1:
                            split_hi(e + 1, i % 12 - SPLIT)

            mixture(0, TILES0)
            act.preload_act_table_set("natural_log_exp_and_others")
            norm(4)

            def copies(b, piece):
                if piece < 2:
                    act.wait_ge(sem["c_keys_summed"], 2 * b + piece + 1)
                    if b >= 2:
                        act.wait_ge(sem["c_scores_summed"], 16 * (b - 1))
                    act.activation(KT[:, b % 2, piece, :], PS[:, 7, 0:KV], ACT.Identity,
                                       bias=COLS[:, 8 + piece:9 + piece]).then_inc(sem["c_keys_copied"], 1)
                    return
                if b >= 2:
                    act.wait_ge(sem["c_heads_mixed"], 16 * (b - 1))
                act.wait_ge(sem["zeros_set"], 3)
                if 2 * b + piece > 1:
                    act.wait_ge(sem["c_values_summed"], 2 * b + piece - 1)
                for par in range(2):
                    if piece == 2:
                        src = PS[0:CH, 7, :].rearrange("p (c h d) -> p c h d", c=2, d=32)
                        dst = VP[:, b % 2, par, 0:2, :].rearrange("p c (h d) -> p c h d", d=32)
                        src, dst = (a[:, :, :, 16 * par:16 * par + 16] for a in (src, dst))
                    else:
                        src = PS[0:CHS[2], 7, 0:D].rearrange("p (h d) -> p h d", d=32)
                        dst = VP[0:CHS[2], b % 2, par, 2, :].rearrange("p (h d) -> p h d", d=32)
                        src, dst = (a[:, :, 16 * par:16 * par + 16] for a in (src, dst))
                    act.copy(dst, src).then_inc(sem["c_values_copied"], 1)

            def exp_c(i):
                act.wait_ge(sem["c_maximum_found"], i + 1)
                if i > 4:
                    act.wait_ge(sem["c_probs_turned"], i - 4)
                if i > 5:
                    act.wait_ge(sem["c_sum_inverted"], i - 5)
                act.activation(PC[:, i % 5, 0:KV], SMK[:, i % 4, :], ACT.Exp, bias=SM1[:, 0, i % 6:i % 6 + 1],
                                   scale=-1.0, accum_out=SM1[:, 1, i % 6:i % 6 + 1]).then_inc(sem["c_exp_taken"], 1)

            def turn_c(i):
                act.wait_ge(sem["c_probs_turned"], i + 1)
                if i > 2:
                    act.wait_ge(sem["c_heads_mixed"], i - 2)
                act.copy(PTC[:, i % 3, :], PS[0:CH, 4 + i % 2, 0:3 * S]).then_inc(sem["c_turned_copied"], 1)

            for piece in range(4):
                copies(0, piece)
            for i in range(16 * B + TURN + 1):
                if i < 16 * B:
                    exp_c(i)
                if i % 16 == 12 and i // 16 < HT1:
                    split_hi(0, i // 16)
                if i % 16 in PIECES and i // 16 + 1 < B:
                    copies(i // 16 + 1, PIECES.index(i % 16))
                if i > TURN:
                    turn_c(i - TURN - 1)
            add_bias("c_output_summed", 0, 2, 1, "c_output_gated", [WK[:, i, :] for i in range(4)])
            norm(5)
            mixture(1, TILES1)

        @block.gpsimd
        def _(pool):
            pool.memset(VSB, 0.0).then_inc(sem["zeros_set"], 1)
            pool.wait_ge(sem["moe_added_to_x"], 4)
            pool.memset(PC[:, :, KV:3 * CH], 0.0).then_inc(sem["zeros_set"], 1)
            pool.memset(VP, 0.0).then_inc(sem["zeros_set"], 1)
            pool.wait_ge(sem["c_query_copied"], 4)
            for b in range(B):
                for mo in range(KD):
                    if b >= 2:
                        pool.wait_ge(sem["c_scores_summed"], 16 * (b - 1))
                    q = QC[:, mo, tok(b)].unsqueeze(1).to_broadcast([P, 8, S])
                    one = PAR[:, :].unsqueeze(2).to_broadcast([P, 8, S])
                    pool.tensor_tensor(QX[:, b % 2, mo, :, :], q, one, ALU.mult).then_inc(sem["c_query_split"], 1)

        @block.vector
        def _(dve):
            chain = [0]

            def link(ins):
                chain[0] += 1
                ins.then_inc(sem["dve_step_done"], 1)
                dve.wait_ge(sem["dve_step_done"], chain[0])

            def norm(i):
                src, dst, kind = NORM[i]
                for n in range(2):
                    if kind == "layer":
                        li = LAYER[i]
                        dve.wait_ge(sem["norm_mean_summed"], 2 * li + n + 1)
                        mean = PS[:, 4 + n, 0:HALF].unsqueeze(1).to_broadcast([P, KD, HALF])
                        dve.tensor_tensor(XC[:, :, half(n)], src[:, :, half(n)], mean, ALU.subtract).then_inc(sem["norm_centred"], 1)
                for n in range(2):
                    dve.wait_ge(sem["norm_rstd_ready"], 2 * i + n + 1)
                    if kind == "layer":
                        dve.wait_ge(sem["norm_centred"], 2 * LAYER[i] + n + 1)
                        rstd = STD[:, n, :].unsqueeze(1).to_broadcast([P, KD, HALF])
                        dve.tensor_tensor(dst[:, :, half(n)], XC[:, :, half(n)], rstd, ALU.mult).then_inc(sem["norm_done"], 1)
                    else:
                        for k in range(KD):
                            ins = dve.scalar_tensor_tensor(XC[:, k, half(n)], src[:, k, half(n)],
                                                           COLS[:, kind + k:kind + k + 1], STD[:, n, :],
                                                           ALU.mult, ALU.mult)
                        ins.then_inc(sem["norm_done"], 1)

            dve.memset(PS[:, 0:2, KV:HALF], 0.0)
            dve.memset(PS[:, 6:8, KV:HALF], 0.0)
            dve.memset(PS[0:H0, 2:4, KV:HALF], NEG).then_inc(sem["psum_tails_set"], 1)
            dve.wait_ge(sem["gates_ready"], 1)
            dve.wait_ge(sem["vectors_loaded"], 64)
            for i in range(4):
                gate, col = i // 2, (4, 12)[i // 2] + i % 2
                dve.tensor_tensor(GB[:, i:i + 1], COLS[:, col:col + 1], TG[:, gate:gate + 1], ALU.mult).then_inc(sem["gated_biases_ready"], 1)
            dve.wait_ge(sem["constants_loaded"], 16 * 8)
            dve.wait_ge(sem["x_loaded"], 16)
            norm(0)

            dve.wait_ge(sem["norm_variance_summed"], 2)
            dve.tensor_copy(SPREAD.rearrange("p t (a d) -> p (t a) d", d=DH0),
                                IDN[0:H0, 0:H0].unsqueeze(2).to_broadcast([H0, H0, DH0])).then_inc(sem["a_spread_rows_built"], 1)
            dve.wait_ge(sem["a_query_copied"], 2 * TI0)

            def products(b, tis):
                for ti in tis:
                    i = TI0 * b + ti
                    dve.wait_ge(sem["a_keys_summed"], i + 1)
                    if i > 2:
                        dve.wait_ge(sem["a_similarity_summed"], i - 2)
                    q = QT0[:, ti, tok(b)].unsqueeze(1).to_broadcast([P, NC, S])
                    k = PS[:, i % 2, 0:HALF].rearrange("p (c i) -> p c i", c=NC)
                    out = PROD[:, i % 3, :].rearrange("p (c i) -> p c i", c=NC)
                    dve.tensor_tensor(out, k, q, ALU.mult).then_inc(sem["a_products_ready"], 1)

            def softmax_a(b):
                dve.wait_ge(sem["a_similarity_summed"], TI0 * (b + 1))
                s = PS[0:H0, 2 + b % 2, 0:HALF]
                link(dve.tensor_reduce(SM0[:, 0, :], s.rearrange("p (c i) -> p i c", c=NC), AX_X, ALU.max))
                top = SM0[:, 0, :].unsqueeze(1).to_broadcast([H0, NC, S])
                e = SE[:, 0, :].rearrange("p (c i) -> p c i", c=NC)
                if b > 0:
                    dve.wait_ge(sem["a_weights_ready"], b)
                dve.tensor_tensor(e, s.rearrange("p (c i) -> p c i", c=NC), top, ALU.subtract).then_inc(sem["a_shifted"], 1)
                dve.wait_ge(sem["a_exp_taken"], b + 1)
                link(dve.tensor_reduce(SM0[:, 1, :], SE[:, 0, :].rearrange("p (c i) -> p i c", c=NC), AX_X, ALU.add))
                link(dve.reciprocal(SM0[:, 2, :], SM0[:, 1, :]))
                if TI0 * (b - 1) > 0:
                    dve.wait_ge(sem["a_weights_spread"], TI0 * (b - 1))
                inv = SM0[:, 2, :].unsqueeze(1).to_broadcast([H0, NC, S])
                dve.tensor_tensor(SE[:, 1 + b % 2, :].rearrange("p (c i) -> p c i", c=NC), e, inv, ALU.mult).then_inc(sem["a_weights_ready"], 1)

            def weigh(b):
                for ti in range(TI0):
                    i = TI0 * b + ti
                    dve.wait_ge(sem["a_weights_spread"], i + 1)
                    dve.wait_ge(sem["a_values_copied"], i + 1)
                    if i > 1:
                        dve.wait_ge(sem["a_heads_mixed"], i - 1)
                    if i == 0:
                        dve.wait_ge(sem["zeros_set"], 1)
                    dve.tensor_tensor(PV[:, i % 2, :], PS[:, 6 + i % 2, 0:HALF], VSB[:, i % 3, :], ALU.mult).then_inc(sem["a_weighted"], 1)
                    dve.wait_ge(sem["a_weighted"], i + 1)
                    dve.tensor_reduce(OT0[:, ti, tok(b)], PV[:, i % 2, :].rearrange("p (c i) -> p i c", c=NC),
                                          AX_X, ALU.add).then_inc(sem["a_heads_mixed"], 1)

            for b in range(B):
                products(b, range(0, 2))
                if b:
                    softmax_a(b - 1)
                products(b, range(2, TI0))
                if b:
                    weigh(b - 1)
            softmax_a(B - 1)
            weigh(B - 1)

            def add_to_x(name, done):
                for i in range(4):
                    n, mo = divmod(i, 2)
                    dve.wait_ge(sem[name], i + 1)
                    dve.tensor_tensor(X[:, mo, half(n)], X[:, mo, half(n)], WK[:, i, :], ALU.add).then_inc(sem[done], 1)

            add_to_x("a_output_gated", "a_added_to_x")

            norm(1)
            dve.wait_ge(sem["norm_done"], 4)
            norm(2)

            for n in range(2):
                dve.wait_ge(sem["b_latent_copied"], n + 1)
                co = CS[:, 0, :].unsqueeze(1).to_broadcast([P, HB, S])
                si = CS[:, 1, :].unsqueeze(1).to_broadcast([P, HB, S])
                v = lambda a: a.rearrange("p (b i) -> p b i", b=HB)
                link(dve.stream_shuffle(CK2[:, half(n)], CK[:, half(n)], [q ^ 1 for q in range(32)]))
                link(dve.tensor_tensor(v(CK2[:, half(n)]), v(CK2[:, half(n)]), si, ALU.mult))
                link(dve.tensor_tensor(v(CK[:, half(n)]), v(CK[:, half(n)]), co, ALU.mult))
                dve.tensor_tensor(CK[:, half(n)], CK[:, half(n)], CK2[:, half(n)], ALU.add).then_inc(sem["b_latent_rotated"], 1)
            for i in range(16):
                tq, n = divmod(i, 2)
                dve.wait_ge(sem["b_query_copied"], i + 1)
                v = lambda a: a.rearrange("p (b i) -> p b i", b=HB)
                dst = QP[:, tq, half(n)]
                if i > 2:
                    dve.wait_ge(sem["b_query_rotated"], i - 2)
                dve.stream_shuffle(SH[:, i % 3, :], QS[:, i % 3, :], [q ^ 1 for q in range(32)]).then_inc(sem["b_query_read"], 1)
                dve.tensor_tensor(v(dst), v(QS[:, i % 3, :]), co, ALU.mult).then_inc(sem["b_query_read"], 1)
                dve.wait_ge(sem["b_query_read"], 2 * i + 1)
                link(dve.tensor_tensor(v(SH[:, i % 3, :]), v(SH[:, i % 3, :]), si, ALU.mult))
                dve.tensor_tensor(dst, dst, SH[:, i % 3, :], ALU.add).then_inc(sem["b_query_rotated"], 1)

            for i in range(2 * B):
                dve.wait_ge(sem["b_scores_summed"], i + 1)
                if i > 1:
                    dve.wait_ge(sem["b_exp_taken"], i - 1)
                s = PS[0:S, 2 * (i % 2):2 * (i % 2) + 2, 0:4 * S].rearrange("p a (x c) -> p a x c", x=4)
                o = SMB[:, i % 2, :]
                o4 = o.rearrange("p (a x c) -> p a x c", a=2, x=4)
                o3 = o.rearrange("p (h c) -> p h c", h=8)
                mask = CM[:, :].unsqueeze(1).unsqueeze(1).to_broadcast([S, 2, 4, S])
                link(dve.tensor_tensor(o4, s, mask, ALU.add))
                link(dve.tensor_reduce(RTC[:, 0, :], o3, AX_X, ALU.max))
                dve.tensor_tensor(o3, o3, RTC[:, 0, :].unsqueeze(2).to_broadcast([S, 8, S]), ALU.subtract).then_inc(sem["b_scores_shifted"], 1)
                dve.wait_ge(sem["b_exp_taken"], i + 1)
                p3 = PB[:, i % 2, :].rearrange("p (h c) -> p h c", h=8)
                link(dve.tensor_reduce(RTC[:, 1, :], p3, AX_X, ALU.add))
                link(dve.reciprocal(RTC[:, 2, :], RTC[:, 1, :]))
                dve.tensor_tensor(p3, p3, RTC[:, 2, :].unsqueeze(2).to_broadcast([S, 8, S]), ALU.mult).then_inc(sem["b_probs_ready"], 1)
            for i in range(4):
                n, mo = divmod(i, 2)
                dve.wait_ge(sem["b_output_summed"], i + 1)
                dve.tensor_tensor(Y[:, mo, half(n)], PS[:, i, 0:HALF], Y[:, mo, half(n)], ALU.add).then_inc(sem["b_added_to_y"], 1)
            norm(3)

            def router(which):
                def v(i):
                    return RT[:, i, :].rearrange("p (b e) -> p b e", b=B)

                def wide(a):
                    return a.unsqueeze(2).to_broadcast([S, B, 8])

                dve.wait_ge(sem["router_scores_summed"], which + 1)
                ps = PS[0:S, 6, 0:B * 8].rearrange("p (b e) -> p b e", b=B)
                if which == 0:
                    link(dve.tensor_tensor(v(0), ps, EB[:, :].unsqueeze(1).to_broadcast([S, B, 8]), ALU.add))
                    link(dve.tensor_reduce(RTC[:, 0, :], v(0), AX_X, ALU.max))
                    dve.tensor_tensor(v(0), v(0), wide(RTC[:, 0, :]), ALU.subtract).then_inc(sem["router_scores_shifted"], 1)
                    dve.wait_ge(sem["router_function_taken"], 1)
                else:
                    dve.tensor_scalar(RT[:, 0, :], PS[0:S, 6, 0:B * 8], 1e-12, None, ALU.max).then_inc(sem["router_scores_shifted"], 1)
                    dve.wait_ge(sem["router_function_taken"], 2)
                for c in range(2):
                    src, top, one = (v(0), v(3))[c], RTC[:, 3 + c, :], v(1 + 3 * c)
                    link(dve.tensor_reduce(top, src, AX_X, ALU.max))
                    link(dve.tensor_tensor(v(5), src, wide(top), ALU.is_equal))
                    link(dve.tensor_tensor(v(5), v(5), RANK[:, :].unsqueeze(1).to_broadcast([S, B, 8]), ALU.mult))
                    link(dve.tensor_reduce(RTC[:, 5, :], v(5), AX_X, ALU.max))
                    link(dve.tensor_tensor(one, v(5), wide(RTC[:, 5, :]), ALU.is_equal))
                    if c == 0:
                        link(dve.scalar_tensor_tensor(RT[:, 3, :], RT[:, 1, :], NEG, RT[:, 0, :], ALU.mult, ALU.add))
                if which == 0:
                    link(dve.tensor_tensor(RTC[:, 5, :], RTC[:, 3, :], RTC[:, 4, :], ALU.add))
                    link(dve.reciprocal(RTC[:, 6, :], RTC[:, 5, :]))
                    link(dve.tensor_tensor(v(5), v(1), v(4), ALU.add))
                    link(dve.tensor_tensor(v(5), v(5), v(0), ALU.mult))
                    dve.tensor_tensor(v(13), v(5), wide(RTC[:, 6, :]), ALU.mult).then_inc(sem["router_weights_ready"], 1)
                else:
                    dve.tensor_tensor(RTC[:, 2, :], RTC[:, 4, :], RTC[:, 3, :], ALU.subtract).then_inc(sem["router_scores_shifted"], 1)
                    dve.wait_ge(sem["router_function_taken"], 3)
                    link(dve.tensor_scalar(RTC[:, 5, :], RTC[:, 2, :], 1.0, None, ALU.add))
                    link(dve.reciprocal(RTC[:, 6, :], RTC[:, 5, :]))
                    link(dve.tensor_tensor(RTC[:, 2, :], RTC[:, 2, :], RTC[:, 6, :], ALU.mult))
                    link(dve.tensor_tensor(v(1), v(1), wide(RTC[:, 6, :]), ALU.mult))
                    link(dve.tensor_tensor(v(4), v(4), wide(RTC[:, 2, :]), ALU.mult))
                    dve.tensor_tensor(v(13), v(1), v(4), ALU.add).then_inc(sem["router_weights_ready"], 1)

            def split_lo(e, m):
                for down in range(2):
                    rows = HW1 if down else P
                    dve.wait_ge(sem["expert_high_ready"], 2 * (HT1 * e + m) + down + 1)
                    raw = tile_of(RING[0:rows, e % 2, :], m, down)
                    hi = tile_of(RINGH[0:rows, e % 2, :], m, down)
                    dve.tensor_tensor(tile_of(RINGL[0:rows, e % 2, :], m, down), raw, hi, ALU.subtract).then_inc(sem["expert_low_ready"], 1)

            def hidden_lo(i):
                dve.wait_ge(sem["hidden_high_ready"], i + 1)
                h = [a[0:HW1, i % 3, :] for a in (HTL, HT, HTH)]
                dve.tensor_tensor(h[0], h[1], h[2], ALU.subtract).then_inc(sem["hidden_low_ready"], 1)

            def mixture(which, tiles):
                if which:
                    for n in range(2):
                        dve.wait_ge(sem["x_high_ready"], n + 1)
                        dve.tensor_tensor(XL[:, :, half(n)], XC[:, :, half(n)], XH[:, :, half(n)], ALU.subtract).then_inc(sem["x_low_ready"], 1)
                router(which)
                first, fw = (0, N0)[which], (0, ROUTED0)[which]
                w = (I0, HW1)[which]
                for i in range(2 * len(tiles)):
                    (e, m_), n = tiles[i // 2], i % 2
                    dve.wait_ge(sem["up_summed"], first + i + 1)
                    dve.wait_ge(sem["gate_activated"], first + i + 1)
                    if first + i > 2:
                        dve.wait_ge(sem["down_summed"], first + i - 2)
                    if which:
                        if i > 2:
                            dve.wait_ge(sem["hidden_low_ready"], i - 2)
                    col = E1 * HT1 + e * HT1 + m_
                    b1 = 0.0 if which == 0 else BIAS1[:, col:col + 1]
                    h = HT[0:w, i % 3, :]
                    dve.scalar_tensor_tensor(h, PS[0:w, 5 + 2 * (i % 2), 0:HALF], b1, SIL[0:w, i % 3, :],
                                                 ALU.add, ALU.mult).then_inc(sem["hidden_ready"], 1)
                    if which == 1 or i < ROUTED0:
                        dve.wait_ge(sem["hidden_ready"], first + i + 1)
                        if i < 2:
                            dve.wait_ge(sem["router_spread_copied"], 16 * which + 16)
                        dve.tensor_tensor(h, h, WEB[0:w, e, half(n)], ALU.mult).then_inc(sem["hidden_weighed"], 1)
                    if which and i:
                        hidden_lo(i - 1)
                    if which and i % 12 >= SPLIT and e + 1 < E1:
                        split_lo(e + 1, i % 12 - SPLIT)
                if which:
                    hidden_lo(2 * len(tiles) - 1)
                for i in range(4):
                    n, mo = divmod(i, 2)
                    dve.wait_ge(sem["down_summed"], first + 2 * len(tiles) - 1 + n)
                    ps, x = PS[:, i, 0:HALF], X[:, mo, half(n)]
                    if which == 0:
                        link(dve.tensor_tensor(Y[:, mo, half(n)], ps, Y[:, mo, half(n)], ALU.add))
                        dve.scalar_tensor_tensor(x, Y[:, mo, half(n)], TG[:, 2:3], x, ALU.mult, ALU.add).then_inc(sem["moe_added_to_x"], 1)
                    else:
                        dve.scalar_tensor_tensor(x, ps, TG[:, 3:4], x, ALU.mult, ALU.add).then_inc(sem["moe_added_to_x"], 1)

            mixture(0, TILES0)
            norm(4)

            dve.wait_ge(sem["mask_loaded"], 16)
            link(dve.tensor_copy(MKB.rearrange("p b c -> p (b c)"), MK8.bitcast(U8)))
            dve.tensor_scalar(MKB.rearrange("p b c -> p (b c)"), MKB.rearrange("p b c -> p (b c)"),
                                  -NEG, NEG, ALU.mult, ALU.add).then_inc(sem["mask_ready"], 1)
            for i in range(4):
                n, mo = divmod(i, 2)
                dve.wait_ge(sem["c_query_summed"], i + 1)
                dve.tensor_scalar(QC[:, mo, half(n)], PS[:, i, 0:HALF], COLS[:, 6 + mo:7 + mo], None,
                                      ALU.add).then_inc(sem["c_query_copied"], 1)
            dve.wait_ge(sem["mask_ready"], 1)

            def top(i):
                b = i // 16
                dve.wait_ge(sem["c_scores_summed"], i + 1)
                if i > 3:
                    dve.wait_ge(sem["c_exp_taken"], i - 3)
                dve.tensor_tensor_reduce(SMK[:, i % 4, :], PS[0:S, i % 4, 0:KV], MKB[:, b, :], -0.25, -2.0 * NEG,
                                             ALU.add, ALU.min, SM1[:, 0, i % 6:i % 6 + 1]).then_inc(sem["c_maximum_found"], 1)

            def over(i):
                dve.wait_ge(sem["c_exp_taken"], i + 1)
                dve.reciprocal(SM1[:, 2, i % 6:i % 6 + 1], SM1[:, 1, i % 6:i % 6 + 1]).then_inc(sem["c_sum_inverted"], 1)
                dve.wait_ge(sem["c_sum_inverted"], i + 1)
                if i == 0:
                    dve.wait_ge(sem["zeros_set"], 3)
                dve.tensor_scalar(PC[:, i % 5, 0:KV], PC[:, i % 5, 0:KV], SM1[:, 2, i % 6:i % 6 + 1], None,
                                      ALU.mult).then_inc(sem["c_probs_ready"], 1)

            def outs(b):
                dve.wait_ge(sem["c_heads_mixed"], 16 * (b + 1))
                for ti in range(KD):
                    ins = dve.tensor_scalar(OT1[:, ti, tok(b)], PS[:, 6, ti * S:(ti + 1) * S],
                                            COLS[:, 10 + ti:11 + ti], None, ALU.add)
                ins.then_inc(sem["c_mixed_copied"], 1)

            for i in range(16 * B + MIX + 1):
                if i < 16 * B:
                    top(i)
                if 2 <= i < 16 * B + 2:
                    over(i - 2)
                if i % 16 == 15 and i // 16 < HT1:
                    split_lo(0, i // 16)
                if i >= 16 + MIX and (i - MIX) % 16 == 0:
                    outs((i - MIX) // 16 - 1)
            add_to_x("c_output_gated", "c_added_to_x")
            norm(5)
            mixture(1, TILES1)


def _rope_tables():
    freqs = (np.float32(1.0) / np.float32(THETA) ** (np.arange(0, ROPE, 2, dtype=np.float32) / np.float32(ROPE)))
    ang = np.outer(np.arange(S, dtype=np.float32), freqs.astype(np.float32)).astype(np.float32)
    tables = np.zeros((P, 2, S), np.float32)
    for p in range(P):
        r = p % 64 - NOPE
        if r < 0:
            tables[p, 0] = 1.0
        else:
            tables[p, 0] = np.cos(ang[:, r // 2])
            tables[p, 1] = np.sin(ang[:, r // 2]) * (-1.0 if r % 2 == 0 else 1.0)
    return tables


def kernel(**inputs):
    import concourse.bacc as _bacc
    from concourse.bass_utils import run_bass_kernel_spmd as _run

    a = {k: np.asarray(v) for k, v in inputs.items()}
    f = np.float32

    def rows(w):
        return np.ascontiguousarray(w.reshape(-1, P, w.shape[-1]).transpose(1, 0, 2))

    def col(v):
        return v.reshape(KD, P).T

    arrays = {}
    arrays["xT"] = rows(a["x"].reshape(T, D).T)
    arrays["ctxT"] = np.ascontiguousarray(a["ctx_1024"].transpose(2, 0, 1).reshape(KD, P, B, KV).transpose(1, 2, 0, 3))
    arrays["mask"] = np.ascontiguousarray(a["mask_Bx1x1xS2_bf1"].reshape(B * KV)).view(np.uint8)
    arrays["gates"] = np.ascontiguousarray(np.stack([a["g_xattn"][0], a["g_xattn"][1], a["g_ffn"][0], a["g_ffn"][1]]))
    arrays["ident"] = np.eye(P, dtype=f)
    arrays["avg"] = np.full((P, P), 1.0 / D, f)
    heads = np.zeros((P, TI0, H0), f)
    for ti in range(TI0):
        for p in range(P):
            heads[p, ti, 2 * ti + p // DH0] = 1.0
    arrays["headsum"] = heads.reshape(P, TI0 * H0)
    arrays["rope"] = _rope_tables()
    arrays["causal"] = np.triu(np.full((S, S), NEG, f), 1)
    arrays["parity"] = np.stack([(np.arange(P) // DH1 == 2 * (h % 4) + h // 4).astype(f) for h in range(8)], 1)
    arrays["rank"] = np.tile(np.arange(8, 0, -1, dtype=f), (S, 1))
    arrays["ones"] = np.ones((P, S), f)
    cols = np.zeros((P, 16), f)
    for at, name in ((0, "L0_ffn_w_ln1"), (2, "L0_ffn_w_ln2"), (4, "L0_xattn_bout"), (6, "L1_xattn_b_q"),
                     (8, "L1_xattn_b_k"), (10, "L1_xattn_b_v"), (12, "L1_xattn_b_o")):
        cols[:, at:at + 2] = col(a[name])
    cols[:, 15] = EPS
    arrays["cols"] = cols
    arrays["ebias"] = a["L0_ffn_expert_bias"]
    arrays["b2"] = a["L1_ffn_b2"]
    arrays["WQ0"] = rows(a["L0_xattn_Wq"])
    arrays["WKV0"] = rows(a["L0_xattn_Wkv"])
    arrays["WOUT0"] = rows(a["L0_xattn_Wout"])
    arrays["WQT"] = rows(a["L0_ffn_Wq"].T)
    wkvb = a["L0_ffn_Wkvb"].reshape(LAT, 16, NOPE)
    gkv = np.zeros((P, 8, P), f)
    bdv = np.zeros((P, 4, P), f)
    wo = np.zeros((P, 4, D), f)
    for h in range(16):
        lo = 64 * (h % 2)
        gkv[lo:lo + NOPE, h // 2, lo:lo + LAT] = wkvb[:, h, :].T
        gkv[lo + NOPE:lo + 64, h // 2, lo + LAT:lo + 64] = np.eye(ROPE, dtype=f)
        j = 32 * (h % 4)
        bdv[j:j + NOPE, h // 4, j:j + LAT] = wkvb[:, h, :].T
        wo[j:j + NOPE, h // 4, :] = a["L0_ffn_Wo"][64 * h:64 * h + NOPE]
    arrays["GKV"], arrays["BDV"], arrays["WO0"] = gkv, bdv, wo
    arrays["WKVA"] = rows(np.concatenate([a["L0_ffn_Wkva"]] * 2, 1))

    def experts(name, shared):
        w = np.concatenate([a[name], a[shared]], 0)
        return w

    for dst, name, shared in (("WG0", "L0_ffn_Wg", "L0_ffn_sWg"), ("WU0", "L0_ffn_Wu", "L0_ffn_sWu")):
        w = experts(name, shared)
        arrays[dst] = rows(np.ascontiguousarray(w.transpose(1, 0, 2)).reshape(D, -1))
    arrays["WD0"] = np.ascontiguousarray(experts("L0_ffn_Wd", "L0_ffn_sWd").transpose(1, 0, 2))
    arrays["WGT0"] = rows(a["L0_ffn_Wgate"])
    arrays["W1A"] = np.ascontiguousarray(np.stack([rows(a["L1_xattn_" + n].T) for n in ("w_q", "w_k", "w_v", "w_o")], 1))
    bias1 = np.stack([a["L1_ffn_bg"], a["L1_ffn_b1"]]).reshape(2 * E1 * HT1, HW1)
    arrays["bias1"] = np.ascontiguousarray(bias1.T)
    arrays["centT"] = rows(a["L1_ffn_centroid"].T)
    arrays["WG1"] = np.ascontiguousarray(a["L1_ffn_Wg"].reshape(E1, KD, P, HID1).transpose(0, 2, 1, 3))
    arrays["WU1"] = np.ascontiguousarray(a["L1_ffn_W1"].reshape(E1, KD, P, HID1).transpose(0, 2, 1, 3))
    arrays["WD1"] = np.ascontiguousarray(a["L1_ffn_W2"].reshape(E1, HT1, HW1, D).transpose(0, 2, 1, 3))

    nc = _bacc.Bacc("TRN2", target_bir_lowering=False, num_devices=1)
    t = {}
    for name, v in arrays.items():
        arrays[name] = v = np.ascontiguousarray(v)
        t[name] = nc.dram_tensor(name, v.shape, mybir.dt.from_np(v.dtype), kind="ExternalInput").ap()
    t["outT"] = nc.dram_tensor("outT", (P, KD, T), F32, kind="ExternalOutput").ap()
    program(nc, t)
    r = _run(nc, [arrays], core_ids=[0])
    out = r.results[0]["outT"]
    return np.ascontiguousarray(out.transpose(1, 0, 2).reshape(D, B, S).transpose(1, 2, 0))
```

```python
from contextlib import ExitStack

import numpy as np

import concourse.bass as bass
from concourse import mybir

F32 = mybir.dt.float32
BF16 = mybir.dt.bfloat16
F32R = mybir.dt.float32r
U8 = mybir.dt.uint8
ALU = mybir.AluOpType
ACT = mybir.ActivationFunctionType
AX_X = mybir.AxisListType.X

B, S, D = 8, 100, 256
KV = 361
KVE = KV + KV % 2
T = B * S
P = 128
KD = D // P
HALF = T // 2
HB = HALF // S
H0, DH0 = 16, 64
TI0 = H0 * DH0 // P
NC = -(-KV // S)
NOPE = ROPE = LAT = 32
H1, DH1 = 16, 16
E0, I0 = 8, 128
E1, HID1 = 8, 684
HT1 = 6
HW1 = HID1 // HT1
CH = 121
CHS = [CH, CH, KV - 2 * CH]
NEG = -1.0e30
EPS = 1e-5
THETA = 100000.0


def program(nc, t):
    with ExitStack() as ctx:
        base = {}

        def sb(name, shape, dt=F32):
            base[name] = -(-nc.sbuf_base // 32) * 32
            return ctx.enter_context(nc.sbuf_tensor(name, shape, dt))

        def part(name, shape, region, at):
            return nc.alloc_sbuf_tensor_at(name, shape, F32R, offset=base[region] + 4 * at)

        TURN, MIX = 4, 8
        NPC = TURN + 3
        X = sb("X", [P, KD, T])
        Y = sb("Y", [P, KD, T])
        XC = sb("XC", [P, KD, T])
        SQ = sb("SQ", [P, KD, T])
        STD = sb("STD", [P, 2, HALF])
        CTX = sb("CTX", [P, 3, KD, KVE])
        RQ = sb("RQ", [P, 6400])
        RO = sb("RO", [P, 6400])
        RW = sb("RW", [P, 12640])
        RB = sb("RB", [P, 11400])
        WK = sb("WK", [P, 6, 400])
        IDN = sb("IDN", [P, P])
        AVG = sb("AVG", [P, P])
        HS = sb("HS", [P, TI0 * H0])
        CS = sb("CS", [P, 2, S])
        CM = sb("CM", [S, S])
        PAR = sb("PAR", [P, 8])
        RANK = sb("RANK", [S, 8])
        ONES = sb("ONES", [P, S])
        COLS = sb("COLS", [P, 16])
        G4 = sb("G4", [P, 4])
        TG = sb("TG", [P, 4])
        GB = sb("GB", [P, 4])
        SM0 = sb("SM0", [H0, 6, S])
        RT = sb("RT", [S, 14, B * 8])
        RTC = sb("RTC", [S, 8, B])
        EB = sb("EB", [S, 8])
        UNIT = sb("UNIT", [40, 8], F32R)
        B2E = sb("B2E", [40, D])
        SM1 = sb("SM1", [S, 3, 6])
        PS = ctx.enter_context(nc.psum_tensor("PS", [P, 8, 512], F32))

        def cut(region, at, n, parts=P):
            return region[0:parts, at:at + n]

        WQ0 = cut(RW, 0, 2048).rearrange("p (k c) -> p k c", k=KD)
        WKV0 = cut(RW, 2048, 4096).rearrange("p (k c) -> p k c", k=KD)
        WOUT0 = cut(RW, 6144, 2048).rearrange("p (t c) -> p t c", t=TI0)
        PROD = cut(RW, 8192, 1200).rearrange("p (s c) -> p s c", s=3)
        VSB = cut(RW, 9392, 1200).rearrange("p (s c) -> p s c", s=3)
        PV = cut(RW, 10592, 800).rearrange("p (s c) -> p s c", s=2)
        SE = cut(RW, 11392, 1200, H0).rearrange("p (s c) -> p s c", s=3)
        SPREAD = part("SPREAD", [H0, TI0, P], "SQ", 0)
        WKV0H = part("WKV0H", [P, KD, 2 * TI0 * P], "RB", 6912)
        WKV0L = part("WKV0L", [P, KD, 2 * TI0 * P], "RW", 2048)
        CTXH = part("CTXH", [P, 3, KD, KVE], "WK", 0)
        CTXL = part("CTXL", [P, 3, KD, KVE], "CTX", 0)
        PRODH = part("PRODH", [P, 4, HALF], "XC", 0)
        PRODL = part("PRODL", [P, 4, HALF], "Y", 0)
        HSR = part("HSR", [P, TI0 * H0], "RB", 3328 + 4 * HALF)
        SEH = part("SEH", [H0, 2, HALF], "RB", 3328)
        SEL = part("SEL", [H0, 2, HALF], "RB", 3328 + 2 * HALF)
        QT0 = cut(RQ, 0, TI0 * T).rearrange("p (t c) -> p t c", t=TI0)
        OT0 = cut(RO, 0, TI0 * T).rearrange("p (t c) -> p t c", t=TI0)
        WQT = cut(RB, 0, 2048).rearrange("p (t c) -> p t c", t=8)
        GKV = cut(RB, 2048, 1024).rearrange("p (t c) -> p t c", t=8)
        WKVA = cut(RB, 3072, 256).rearrange("p (k c) -> p k c", k=KD)
        WQA = cut(RB, 3328, 2048).rearrange("p (k c) -> p k c", k=KD)
        BDV = cut(RB, 5376, 512).rearrange("p (t c) -> p t c", t=4)
        WO0 = cut(RB, 5888, 1024).rearrange("p (t c) -> p t c", t=4)
        WOA = cut(RB, 6912, 1024).rearrange("p (t c) -> p t c", t=4)
        CK = cut(RB, 7936, 800)
        CK2 = cut(RB, 8736, 800)
        CKM = cut(RB, 0, 1600).rearrange("p (a c) -> p a c", a=2)
        CMB = cut(RB, 1600, S // 2, S).bitcast(BF16)
        IDNB = cut(RB, 1600 + S // 2, S // 2, S).bitcast(BF16)
        PT0 = cut(RB, 9536, 1600, S).rearrange("p (s c) -> p s c", s=2)
        LT = cut(RB, 11136, 256, S).rearrange("p (b c) -> p b c", b=B)
        QP = QT0
        UT = cut(RO, 0, 3200).rearrange("p (t c) -> p t c", t=4)
        SMB = cut(RO, 3200, 1600, S).rearrange("p (s c) -> p s c", s=2)
        PB = cut(RO, 4800, 1600, S).rearrange("p (s c) -> p s c", s=2)
        WGU0 = cut(RW, 0, 4608).rearrange("p (w c) -> p w c", w=2 * KD)
        WD0 = cut(RW, 4608, 2304).rearrange("p (t c) -> p t c", t=E0 + 1)
        WGU0L = part("WGU0L", [P, 2 * KD, (E0 + 1) * I0], "RW", 0)
        WD0L = part("WD0L", [P, E0 + 1, D], "RW", 4608)
        WGU0H = part("WGU0H", [P, 2 * KD, (E0 + 1) * I0], "RB", 4480)
        WD0H = part("WD0H", [P, E0 + 1, D], "RB", 9088)
        XH = part("XH", [P, KD, T], "RO", 0)
        XL = part("XL", [P, KD, T], "RO", KD * T)
        HTH = part("HTH", [P, 3, HALF], "RO", 2 * KD * T)
        HTL = part("HTL", [P, 3, HALF], "RO", 2 * KD * T + 3 * HALF)
        WTS = part("WTS", [40, T], "SQ", 0)
        WGT0 = cut(RW, 6912, 16).rearrange("p (k c) -> p k c", k=KD)
        W1A = cut(RW, 6928, 2048).rearrange("p (w k c) -> p w k c", w=4, k=KD)
        MK8 = cut(RW, 8976, 722, S)
        MKB = cut(RW, 9698, 2888, S).rearrange("p (b c) -> p b c", b=B)
        QCH = part("QCH", [P, KD, T], "RQ", 0)
        QCL = part("QCL", [P, KD, T], "RQ", KD * T)
        VP = cut(RQ, 3200, 3072, CH).rearrange("p (s a c d) -> p s a c d", s=2, a=2, c=3)
        KTH = [part("KTH0", [P, KD, KVE], "WK", 4 * HALF), part("KTH1", [P, KD, KVE], "XC", 0)]
        KTL = part("KTL", [P, 2, KD, KVE], "RW", 4480)
        QXH = part("QXH", [P, 2, KD, 8, S], "RO", 0)
        QXL = part("QXL", [P, 2, KD, 8, S], "RO", 3200)
        SMK = SQ[:, :, :].rearrange("p k c -> p (k c)")[0:S, 0:4 * KV].rearrange("p (s c) -> p s c", s=4)
        OT1 = Y
        PC = cut(RB, 8544, NPC * 3 * CH, S).rearrange("p (s c) -> p s c", s=NPC)
        PTC = WK[0:CH, 0:4, 0:3 * S]
        WEB = cut(RQ, 0, E1 * T).rearrange("p (e c) -> p e c", e=E1)
        RING = RB[:, 0:2 * (4 * HID1 + HT1 * D)].rearrange("p (s c) -> p s c", s=2)
        BIAS1 = cut(RW, 0, 2 * E1 * HT1, HW1)
        CENT = cut(RW, 96, 16).rearrange("p (k c) -> p k c", k=KD)
        CENT2 = cut(RW, 112, 16).rearrange("p (k c) -> p k c", k=KD)
        CSQ = cut(RW, 144, 8, S)
        CENTSQ = cut(RW, 128, 16).rearrange("p (k c) -> p k c", k=KD)
        EXPERT = 4 * HID1 + HT1 * D
        RINGH = part("RINGH", [P, 2, EXPERT], "RW", 192)
        RINGL = part("RINGL", [P, 2, EXPERT], "RB", 0)
        B2H = part("B2H", [40, D], "RO", 5600)
        B2L = part("B2L", [40, D], "RO", 5600 + D)
        RTH = part("RTH", [S, B * 8], "RT", 11 * B * 8)
        RTX = RT[:, 6:11, :].rearrange("p a c -> p (a c)").rearrange("p (b c) -> p b c", c=40)
        SIL = WK[:, 0:3, :]
        HT = WK[:, 3:6, :]
        QS = WK[:, 0:3, :]
        SH = WK[:, 3:6, :]

        names = """x_loaded constants_loaded vectors_loaded a_wq_loaded a_wkv_loaded a_wout_loaded context_loaded0
            context_loaded1 context_loaded2 b_weights_loaded moe0_weights_loaded c_weights_loaded
            mask_loaded moe1_small_loaded expert_loaded0 expert_loaded1 out_stored zeros_set
            pads_set a_head_rows_rounded psum_tails_set a_spread_rows_built dve_step_done
            gates_ready gated_biases_ready norm_mean_summed norm_centred norm_squared
            norm_variance_summed norm_log_taken norm_rstd_ready norm_done a_query_summed
            a_query_copied a_weights_high_ready a_weights_low_ready a_context_high_ready
            a_context_low_ready a_probs_high_ready a_probs_low_ready a_products_high_ready
            a_products_low_ready a_keys_summed a_products_ready a_similarity_summed a_shifted
            a_exp_taken a_weights_ready a_weights_spread a_values_summed a_values_copied a_weighted
            a_heads_mixed a_output_summed a_output_gated a_added_to_x b_weights_folded
            b_folded_copied b_latent_summed b_latent_rotated b_latent_copied b_latent_rows_summed
            b_latent_rows_copied b_zero_keys_set b_mask_rounded b_query_summed b_query_copied
            b_query_read b_query_cosines b_query_rotated b_scores_summed b_maxima_found
            b_scores_shifted b_exp_taken b_probs_ready b_probs_turned b_turned_copied b_heads_mixed
            b_mixed_copied b_output_summed b_added_to_y router_scores_summed router_scores_shifted
            router_function_taken router_weights_ready router_weights_turned router_turned_copied
            router_high_ready router_weights_spread router_spread_copied router_spread_copied_odd
            router_squares_ready centroid_lengths_summed centroid_lengths_copied unit_rows_ready
            output_bias_high_ready output_bias_low_ready gate_summed up_summed gate_activated
            hidden_ready hidden_weighed hidden_high_ready hidden_low_ready down_summed
            moe_added_to_x x_high_ready x_low_ready expert_high_ready expert_low_ready
            c_query_summed c_query_copied c_query_split c_pads_set c_keys_summed c_keys_copied
            c_keys_low_ready c_query_low_ready c_values_summed c_values_copied c_scores_summed
            c_maximum_found c_exp_taken c_sum_inverted c_probs_ready c_probs_turned c_turned_copied
            c_heads_mixed c_mixed_copied c_output_summed c_output_gated c_added_to_x mask_ready""".split()
        sem = {n: ctx.enter_context(nc.semaphore(n)) for n in names}

        def half(n):
            return slice(n * HALF, (n + 1) * HALF)

        def tok(b):
            return slice(b * S, (b + 1) * S)

        NORM = [(X, XC, "layer"), (X, Y, "layer"), (Y, XC, 0), (Y, XC, 2), (X, XC, "layer"), (X, XC, "layer")]
        LAYER = {0: 0, 1: 1, 4: 2, 5: 3}
        SOURCE = [("x_loaded", lambda n: 16), ("a_added_to_x", lambda n: 2 * n + 2), ("norm_done", lambda n: 2 + n + 1),
                  ("b_added_to_y", lambda n: 2 * n + 2), ("moe_added_to_x", lambda n: 2 * n + 2), ("c_added_to_x", lambda n: 2 * n + 2)]

        TILES0 = [(e, 0) for e in range(E0 + 1)]
        TILES1 = [(e, m) for e in range(E1) for m in range(HT1)]
        N0, N1 = 2 * len(TILES0), 2 * len(TILES1)
        ROUTED0, ROUTED1 = 2 * E0, N1

        def ring(e):
            return expert(RING[:, e % 2, :])

        def expert(r):
            return (r[:, 0:2 * HID1].rearrange("p (k c) -> p k c", k=KD),
                    r[:, 2 * HID1:4 * HID1].rearrange("p (k c) -> p k c", k=KD),
                    r[0:HW1, 4 * HID1:4 * HID1 + HT1 * D].rearrange("p (m c) -> p m c", m=HT1))

        def tile_of0(part_, e, down):
            gu, d = {"raw": (WGU0, WD0), "high": (WGU0H, WD0H), "low": (WGU0L, WD0L)}[part_]
            return d[:, e, :] if down else gu[:, :, e * I0:(e + 1) * I0]

        def tile_of(r, m, down):
            if down:
                return expert(r)[2][:, m, :]
            return r[:, 0:4 * HID1].rearrange("p (w c) -> p w c", w=4)[:, :, m * HW1:(m + 1) * HW1]

        W_PIECES = [9, 11, 13, 15]

        LAG0 = 3

        def key_bank(b, m):
            return 6 if b == 0 and m == 1 else 7

        def w_piece(w, i):
            return w[:, :, i * (TI0 // 2) * P:(i + 1) * (TI0 // 2) * P]

        SPLIT = HT1

        HEADS1 = [(ti, par, j) for ti in range(KD) for par in range(2) for j in range(4)]

        PARTS = [0, 1, 5, 6, 9, 10, 13]
        PIECES = [2, 7, 11, 14]

        block = ctx.enter_context(nc.Block())

        @block.sync
        def _(sp):
            def load(dst, src, name):
                sp.dma_start(dst, src).then_inc(sem[name], 16)

            load(X[:, :, :], t["xT"], "x_loaded")
            for dst, name in ((IDN, "ident"), (AVG, "avg"), (HS, "headsum"), (CS, "rope"), (CM, "causal"),
                              (PAR, "parity"), (RANK, "rank"), (ONES, "ones")):
                load(dst[:, :] if len(dst.shape) == 2 else dst[:, :, :], t[name], "constants_loaded")
            load(WQ0, t["WQ0"], "a_wq_loaded")

            def load_ctx(i):
                b = i % B
                if i >= 3:
                    j = i - 3
                    if j < B:
                        sp.wait_ge(sem["a_values_summed"], TI0 * (j + 1))
                    else:
                        sp.wait_ge(sem["c_values_summed"], 2 * (j - B + 1))
                load(CTX[:, i % 3, :, 0:KV], t["ctxT"][:, b, :, :], f"context_loaded{i % 3}")

            load(COLS[:, :], t["cols"], "vectors_loaded")
            load(G4[:, :], t["gates"].partition_broadcast(P), "vectors_loaded")
            load(EB[:, :], t["ebias"].partition_broadcast(S), "vectors_loaded")
            load(B2E[:, :], t["b2"], "vectors_loaded")
            load_ctx(0)
            load(WKV0, t["WKV0"], "a_wkv_loaded")
            load_ctx(1)
            load_ctx(2)
            load(WOUT0, t["WOUT0"], "a_wout_loaded")
            for dst, name in ((WQT, "WQT"), (GKV, "GKV"), (WKVA, "WKVA"), (BDV, "BDV"), (WO0, "WO0")):
                load(dst, t[name], "b_weights_loaded")
            for b in range(3, B):
                load_ctx(b)
            sp.wait_ge(sem["a_output_summed"], 4)
            sp.wait_ge(sem["a_heads_mixed"], TI0 * B)
            for dst, name in ((WGU0, "WGU0"), (WD0, "WD0"), (WGT0, "WGT0")):
                load(dst, t[name], "moe0_weights_loaded")
            load(W1A, t["W1A"], "c_weights_loaded")
            load(MK8.bitcast(U8), t["mask"].partition_broadcast(S), "mask_loaded")
            for i in range(B, B + 3):
                load_ctx(i)

            def load_expert(e):
                g, u, d = ring(e)
                if e >= 2:
                    sp.wait_ge(sem["down_summed"], N0 + 2 * HT1 * (e - 1))
                load(g, t["WG1"][e], f"expert_loaded{e % 2}")
                load(u, t["WU1"][e], f"expert_loaded{e % 2}")
                load(d, t["WD1"][e], f"expert_loaded{e % 2}")

            sp.wait_ge(sem["b_output_summed"], 4)
            sp.wait_ge(sem["b_mixed_copied"], 2 * B)
            load_expert(0)
            for i in range(B + 3, 2 * B):
                load_ctx(i)
            sp.wait_ge(sem["moe_added_to_x"], 4)
            load_expert(1)
            load(BIAS1, t["bias1"], "moe1_small_loaded")
            load(CENT, t["centT"], "moe1_small_loaded")
            for e in range(2, E1):
                load_expert(e)
            sp.wait_ge(sem["moe_added_to_x"], 8)
            load_out = sp.dma_start(t["outT"], X[:, :, :])
            load_out.then_inc(sem["out_stored"], 16)
            sp.wait_ge(sem["out_stored"], 16)

        @block.tensor
        def _(pe):
            def mm(out, lhsT, rhs, start, stop):
                return pe.matmul(out, lhsT, rhs, start=start, stop=stop)

            def norm(i):
                src, _, kind = NORM[i]
                for n in range(2):
                    if kind == "layer":
                        pe.wait_ge(sem[SOURCE[i][0]], SOURCE[i][1](n))
                        for k in range(KD):
                            m = mm(PS[:, 4 + n, 0:HALF], AVG[:, :], src[:, k, half(n)], k == 0, k == KD - 1)
                        m.then_inc(sem["norm_mean_summed"], 1)
                for n in range(2):
                    pe.wait_ge(sem["norm_squared"], 2 * i + n + 1)
                    for k in range(KD):
                        m = mm(PS[:, 4 + n, 0:HALF], AVG[:, :], SQ[:, k, half(n)], k == 0, k == KD - 1)
                    m.then_inc(sem["norm_variance_summed"], 1)

            pe.wait_ge(sem["constants_loaded"], 16 * 8)
            norm(0)
            pe.wait_ge(sem["a_wq_loaded"], 16)
            for i in range(2 * TI0):
                ti, n = divmod(i, 2)
                pe.wait_ge(sem["norm_done"], n + 1)
                if i > 1:
                    pe.wait_ge(sem["a_query_copied"], i - 1)
                for k in range(KD):
                    m = mm(PS[:, 4 + i % 2, 0:HALF], WQ0[:, k, ti * P:(ti + 1) * P], XC[:, k, half(n)], k == 0, k == 1)
                m.then_inc(sem["a_query_summed"], 1)
            pe.wait_ge(sem["a_query_copied"], 2 * TI0)
            pe.wait_ge(sem["psum_tails_set"], 1)
            pe.wait_ge(sem["a_head_rows_rounded"], 1)

            def sim(b, ti):
                i = TI0 * b + ti
                pe.wait_ge(sem["a_products_low_ready"], i + 1)
                if b > 1:
                    pe.wait_ge(sem["a_shifted"], b - 1)
                pe.wait_ge(sem["pads_set"], 4)
                out, heads = PS[0:H0, 2 + b % 2, 0:KVE], HSR[:, ti * H0:(ti + 1) * H0]
                mm(out, heads, PRODH[:, i % 4, 0:KVE], ti == 0, False)
                mm(out, heads, PRODL[:, i % 4, 0:KVE], False, ti == TI0 - 1).then_inc(sem["a_similarity_summed"], 1)

            def project_a(out, b, tile):
                cols = slice(tile * P, (tile + 1) * P)
                for k in range(KD):
                    mm(out, WKV0H[:, k, cols], CTXH[:, b % 3, k, :], k == 0, False)
                    mm(out, WKV0H[:, k, cols], CTXL[:, b % 3, k, :], False, False)
                    m = mm(out, WKV0L[:, k, cols], CTXH[:, b % 3, k, :], False, k == 1)
                return m

            def keys(b):
                pe.wait_ge(sem["a_context_low_ready"], b + 1)
                for ti in range(TI0):
                    i = TI0 * b + ti
                    if i > 1:
                        pe.wait_ge(sem["a_products_ready"], i - 1)
                    if 1 + ti // 4 > 0:
                        pe.wait_ge(sem["a_weights_low_ready"], 1 + ti // 4)
                    pe.wait_ge(sem["pads_set"], 3)
                    project_a(PS[:, i % 2, 0:KVE], b, ti).then_inc(sem["a_keys_summed"], 1)
                    if ti >= LAG0:
                        sim(b, ti - LAG0)

            def values(b):
                pe.wait_ge(sem["a_spread_rows_built"], 1)
                pe.wait_ge(sem["a_weights_low_ready"], 4)
                for ti in range(TI0):
                    i = TI0 * b + ti
                    if i > 1:
                        pe.wait_ge(sem["a_values_copied"], i - 1)
                    project_a(PS[:, 4 + i % 2, 0:KVE], b, TI0 + ti).then_inc(sem["a_values_summed"], 1)
                    if ti < LAG0 and b + 1 < B:
                        sim(b + 1, TI0 - LAG0 + ti)
                    pe.wait_ge(sem["a_probs_low_ready"], b + 1)
                    if i > 1:
                        pe.wait_ge(sem["a_weighted"], i - 1)
                    mm(PS[:, 6 + i % 2, 0:KVE], SPREAD[:, ti, :], SEH[:, b % 2, 0:KVE], True, False)
                    mm(PS[:, 6 + i % 2, 0:KVE], SPREAD[:, ti, :], SEL[:, b % 2, 0:KVE], False, True).then_inc(sem["a_weights_spread"], 1)

            for b in range(B):
                keys(b)
                if b:
                    values(b - 1)
                else:
                    for ti in range(TI0 - LAG0, TI0):
                        sim(0, ti)
            values(B - 1)
            pe.wait_ge(sem["a_wout_loaded"], 16)
            pe.wait_ge(sem["a_heads_mixed"], TI0 * B)
            for n in range(2):
                for mo in range(KD):
                    for ti in range(TI0):
                        m = mm(PS[:, 2 * n + mo, 0:HALF], WOUT0[:, ti, mo * P:(mo + 1) * P], OT0[:, ti, half(n)],
                               ti == 0, ti == TI0 - 1)
                    m.then_inc(sem["a_output_summed"], 1)

            pe.wait_ge(sem["b_weights_loaded"], 16 * 5)
            for i in range(4):
                if i > 1:
                    pe.wait_ge(sem["b_folded_copied"], i - 1)
                for ti in range(4):
                    c = i // 2
                    tq = 4 * (i % 2) + ti
                    m = mm(PS[:, 6 + i % 2, ti * P:(ti + 1) * P], WQT[:, tq, c * P:(c + 1) * P], GKV[:, tq, :], True, True)
                m.then_inc(sem["b_weights_folded"], 1)
            for i in range(2):
                pe.wait_ge(sem["b_folded_copied"], i + 3)
                for j in range(2):
                    m = mm(PS[:, 6 + i, j * D:(j + 1) * D], BDV[:, 2 * i + j, :], WO0[:, 2 * i + j, :], True, True)
                m.then_inc(sem["b_weights_folded"], 1)
            norm(1)
            norm(2)
            for n in range(2):
                pe.wait_ge(sem["norm_done"], 4 + n + 1)
                pe.wait_ge(sem["a_output_gated"], 4)
                for k in range(KD):
                    m = mm(PS[:, n, 0:HALF], WKVA[:, k, :], XC[:, k, half(n)], k == 0, k == 1)
                m.then_inc(sem["b_latent_summed"], 1)
            for b in range(B):
                for k in range(KD):
                    m = mm(PS[0:S, 2, b * LAT:(b + 1) * LAT], XC[:, k, tok(b)], WKVA[:, k, 0:LAT], k == 0, k == 1)
            m.then_inc(sem["b_latent_rows_summed"], 1)
            pe.wait_ge(sem["b_folded_copied"], 6)
            for i in range(16):
                n, tq = divmod(i, 8)
                if i > 3:
                    pe.wait_ge(sem["b_query_copied"], i - 3)
                for k in range(KD):
                    m = mm(PS[:, 4 + i % 4, 0:HALF], WQA[:, k, tq * P:(tq + 1) * P], XC[:, k, half(n)], k == 0, k == 1)
                m.then_inc(sem["b_query_summed"], 1)

            def qk(i):
                b, g = divmod(i, 2)
                if i == 0:
                    pe.wait_ge(sem["b_latent_rows_copied"], 1)
                    pe.wait_ge(sem["b_zero_keys_set"], 2)
                    pe.wait_ge(sem["b_latent_rotated"], 4)
                    pe.wait_ge(sem["b_mask_rounded"], 2)
                    pe.wait_ge(sem["b_query_rotated"], 16)
                if i > 1:
                    pe.wait_ge(sem["b_scores_shifted"], i - 1)
                if i > 1:
                    pe.wait_ge(sem["b_exp_taken"], i - 1)
                for par in range(2):
                    bank = 2 * (i % 2) + par
                    mm(PS[0:S, bank, 0:4 * S], IDNB, CMB.unsqueeze(1).to_broadcast([S, 4, S]), True, False)
                    for x in range(4):
                        m = mm(PS[0:S, bank, x * S:(x + 1) * S], QP[:, 4 * g + x, tok(b)], CKM[:, par, tok(b)],
                               False, x == 3)
                m.then_inc(sem["b_scores_summed"], 1)

            def turn(i):
                pe.wait_ge(sem["b_probs_ready"], i + 1)
                for q in range(2):
                    if 2 * i + q > 1:
                        pe.wait_ge(sem["b_turned_copied"], 2 * i + q - 1)
                    for x in range(4):
                        m = pe.transpose(PS[0:S, 4 + q, x * S:(x + 1) * S], PB[:, i % 2, (4 * q + x) * S:(4 * q + x + 1) * S],
                                         IDN[0:S, 0:S])
                    m.then_inc(sem["b_probs_turned"], 1)

            def mix(i):
                b, g = divmod(i, 2)
                pe.wait_ge(sem["b_turned_copied"], 2 * i + 2)
                if i > 1:
                    pe.wait_ge(sem["b_mixed_copied"], i - 1)
                for j in range(4):
                    at = (4 * (j % 2) + j // 2) * S
                    rhs = PT0[:, i % 2, at:at + 3 * S].rearrange("p (x c) -> p x c", c=S)[:, 0:3:2, :]
                    m = mm(PS[32 * j:32 * j + 32, 6 + i % 2, 0:2 * S], LT[:, b, :], rhs, True, True)
                m.then_inc(sem["b_heads_mixed"], 1)

            for i in range(2 * B + 3):
                if i < 2 * B:
                    qk(i)
                if 2 <= i < 2 * B + 2:
                    turn(i - 2)
                if i >= 3:
                    mix(i - 3)
            pe.wait_ge(sem["b_mixed_copied"], 2 * B)
            for n in range(2):
                for mo in range(KD):
                    for ti in range(4):
                        m = mm(PS[:, 2 * n + mo, 0:HALF], WOA[:, ti, mo * P:(mo + 1) * P], UT[:, ti, half(n)],
                               ti == 0, ti == 3)
                    m.then_inc(sem["b_output_summed"], 1)
            norm(3)

            def mixture(which, tiles):
                first = (0, N0)[which]
                before = (0, 2 * len(TILES0))[which]
                w = (I0, HW1)[which]
                count = 2 * len(tiles)
                for b in range(B):
                    if (7, 11)[which] + b // HB > 0:
                        pe.wait_ge(sem["norm_done"], (7, 11)[which] + b // HB)
                    if which:
                        if 3 + b // HB > 0:
                            pe.wait_ge(sem["router_squares_ready"], 3 + b // HB)
                    out = PS[0:S, 0, b * 8:(b + 1) * 8]
                    if which == 0:
                        pe.wait_ge(sem["moe0_weights_loaded"], 48)
                        pairs = [(XC[:, k, tok(b)], WGT0[:, k, :]) for k in range(KD)]
                    else:
                        pairs = [(XC[:, k, tok(b)], CENT2[:, k, :]) for k in range(KD)]
                        pairs += [(SQ[:, k, tok(b)], ONES[:, 0:8]) for k in range(KD)]
                    for c, (lhsT, rhs) in enumerate(pairs):
                        m = mm(out, lhsT, rhs, c == 0, c == len(pairs) - 1)
                m.then_inc(sem["router_scores_summed"], 1)

                def parts(i):
                    e, m_ = tiles[i // 2]
                    if which == 0:
                        gu = [tile_of0(part_, e, 0) for part_ in ("high", "low")]
                        d = [tile_of0(part_, e, 1) for part_ in ("high", "low")]
                    else:
                        gu = [tile_of(slots[:, e % 2, :], m_, 0) for slots in (RINGH, RINGL)]
                        d = [tile_of(slots[0:HW1, e % 2, :], m_, 1) for slots in (RINGH, RINGL)]
                    return gu, d

                def up(i):
                    n = i % 2
                    hi, lo = parts(i)[0]
                    pe.wait_ge(sem["expert_low_ready"], before + 2 * (i // 2) + 1)
                    pe.wait_ge(sem["x_low_ready"], 2 * which + n + 1)
                    if first + i > 1:
                        pe.wait_ge(sem["hidden_ready"], first + i - 1)
                    for c, name in enumerate(("gate_summed", "up_summed")):
                        out = PS[0:w, 4 + c + 2 * (i % 2), 0:HALF]
                        for k in range(KD):
                            mm(out, hi[:, KD * c + k, :], XH[:, k, half(n)], k == 0, False)
                            mm(out, hi[:, KD * c + k, :], XL[:, k, half(n)], False, False)
                            m = mm(out, lo[:, KD * c + k, :], XH[:, k, half(n)], False, k == 1)
                        m.then_inc(sem[name], 1)

                def down(i):
                    n = i % 2
                    hi, lo = parts(i)[1]
                    pe.wait_ge(sem["expert_low_ready"], before + 2 * (i // 2) + 2)
                    pe.wait_ge(sem["hidden_low_ready"], first + i + 1)
                    for mo in range(KD):
                        out, cols = PS[:, 2 * n + mo, 0:HALF], slice(mo * P, (mo + 1) * P)
                        mm(out, hi[:, cols], HTH[0:w, i % 3, :], which == 0 and i < 2, False)
                        mm(out, hi[:, cols], HTL[0:w, i % 3, :], False, False)
                        m = mm(out, lo[:, cols], HTH[0:w, i % 3, :], False, i >= count - 2)
                    m.then_inc(sem["down_summed"], 1)

                up(0)
                up(1)
                pe.wait_ge(sem["router_weights_ready"], 2 * which + 2)
                pe.wait_ge(sem["unit_rows_ready"], 3)
                for q in range(2):
                    for b in range(4):
                        bb = 4 * q + b
                        m = pe.transpose(PS[0:40, 1 + q, b * S:(b + 1) * S], RTX[:, bb, :], IDN[0:S, 0:S])
                    m.then_inc(sem["router_weights_turned"], 1)
                pe.wait_ge(sem["unit_rows_ready"], 3)
                for i in range(16):
                    e, n = divmod(i, 2)
                    pe.wait_ge(sem["router_turned_copied"], 2 * which + n + 1)
                    if i >= 4:
                        if 8 * which + i // 2 > 1:
                            pe.wait_ge(sem[("router_spread_copied", "router_spread_copied_odd")[i % 2]], 8 * which + i // 2 - 1)
                    lhsT = UNIT[:, e:e + 1].to_broadcast([40, P])
                    mm(PS[:, i % 4, 0:HALF], lhsT, WTS[:, half(n)], True, True).then_inc(sem["router_weights_spread"], 1)
                for i in range(2, count + 2):
                    if i < count:
                        up(i)
                    if i == 2:
                        pe.wait_ge(sem["router_spread_copied"], 8 * which + 8)
                        pe.wait_ge(sem["router_spread_copied_odd"], 8 * which + 8)
                        if which:
                            pe.wait_ge(sem["output_bias_low_ready"], 1)
                            for n in range(2):
                                for mo in range(KD):
                                    out, cols = PS[:, 2 * n + mo, 0:HALF], slice(mo * P, (mo + 1) * P)
                                    mm(out, B2H[:, cols], WTS[:, half(n)], True, False)
                                    mm(out, B2L[:, cols], WTS[:, half(n)], False, False)
                    down(i - 2)

            def project(b, part_):
                ci = B + b
                if part_ == 0:
                    pe.wait_ge(sem[f"context_loaded{ci % 3}"], 16 * (ci // 3 + 1))
                    if 4 * b > 0:
                        pe.wait_ge(sem["c_values_copied"], 4 * b)
                if part_ < 4:
                    m_, k = divmod(part_, KD)
                    if 2 * b + m_ if b else 0 > 0:
                        pe.wait_ge(sem["c_keys_low_ready"], 2 * b + m_ if b else 0)
                    m = mm(PS[:, key_bank(b, m_), 0:KV], W1A[:, 1, k, m_ * P:(m_ + 1) * P], CTX[:, ci % 3, k, 0:KV], k == 0, k == 1)
                    if k == 1:
                        m.then_inc(sem["c_keys_summed"], 1)
                    return
                c = part_ - 4
                pe.wait_ge(sem["c_keys_low_ready"], 2 * b + 2)
                if c == 2:
                    pe.wait_ge(sem["c_values_copied"], 4 * b + 2)
                at = (c % 2) * D
                for k in range(KD):
                    m = mm(PS[0:CHS[c], 7, at:at + D], CTX[:, ci % 3, k, c * CH:c * CH + CHS[c]], W1A[:, 2, k, :],
                           k == 0, k == 1)
                if c:
                    m.then_inc(sem["c_values_summed"], 1)

            pe.wait_ge(sem["b_added_to_y"], 4)
            mixture(0, TILES0)

            pe.wait_ge(sem["c_weights_loaded"], 16)
            for part_ in range(2 * KD):
                project(0, part_)
            norm(4)
            for i in range(4):
                n, mo = divmod(i, 2)
                pe.wait_ge(sem["norm_done"], 8 + n + 1)
                pe.wait_ge(sem["moe_added_to_x"], 4)
                for k in range(KD):
                    m = mm(PS[:, i, 0:HALF], W1A[:, 0, k, mo * P:(mo + 1) * P], XC[:, k, half(n)], k == 0, k == 1)
                m.then_inc(sem["c_query_summed"], 1)

            for part_ in range(2 * KD, 2 * KD + 3):
                project(0, part_)

            def scores(i):
                b, h = i // 16, i % 16
                if h == 0:
                    pe.wait_ge(sem["c_pads_set"], 3)
                    pe.wait_ge(sem["c_keys_low_ready"], 2 * b + 2)
                if h % 8 == 0:
                    pe.wait_ge(sem["c_query_split"], 2 * KD * b + h // 4 + 2)
                if i > 2:
                    pe.wait_ge(sem["c_maximum_found"], i - 2)
                out, ti = PS[0:S, i % 3, 0:KVE], h // 8
                q = [a[:, b % 2, ti, h % 8, :] for a in (QXH, QXL)]
                k = [KTH[b % 2][:, ti, :], KTL[:, b % 2, ti, :]]
                mm(out, q[0], k[0], True, False)
                mm(out, q[0], k[1], False, False)
                mm(out, q[1], k[0], False, True).then_inc(sem["c_scores_summed"], 1)

            def turn_p(i):
                pe.wait_ge(sem["c_probs_ready"], i + 1)
                if i > 2:
                    pe.wait_ge(sem["c_turned_copied"], i - 2)
                for c in range(3):
                    m = pe.transpose(PS[0:CH, 3 + i % 3, c * S:(c + 1) * S], PC[:, i % NPC, c * CH:(c + 1) * CH], IDN[0:S, 0:S])
                m.then_inc(sem["c_probs_turned"], 1)

            def mix_v(i):
                b, (ti, par, j) = i // 16, HEADS1[i % 16]
                pe.wait_ge(sem["c_turned_copied"], i + 1)
                if i % 16 == 0:
                    pe.wait_ge(sem["c_values_copied"], 4 * b + 4)
                    if b > 0:
                        pe.wait_ge(sem["c_mixed_copied"], b)
                for c in range(3):
                    at = ti * P + 32 * j
                    m = mm(PS[32 * j:32 * j + 32, 6, ti * S:(ti + 1) * S], VP[0:CHS[c], b % 2, par, c, at:at + 32],
                           PTC[0:CHS[c], i % 4, c * S:(c + 1) * S], par == 0 and c == 0, par == 1 and c == 2)
                m.then_inc(sem["c_heads_mixed"], 1)

            for i in range(16 * B + MIX):
                if i < 16 * B:
                    scores(i)
                if 0 <= i - TURN < 16 * B:
                    turn_p(i - TURN)
                if i >= MIX:
                    mix_v(i - MIX)
                if i % 16 in PARTS and i // 16 + 1 < B:
                    project(i // 16 + 1, PARTS.index(i % 16))
            pe.wait_ge(sem["c_mixed_copied"], B)
            pe.wait_ge(sem["router_squares_ready"], 2)
            for k in range(KD):
                m = mm(PS[0:S, 7, 0:8], ONES[:, 0:S], CENTSQ[:, k, :], k == 0, k == KD - 1)
            m.then_inc(sem["centroid_lengths_summed"], 1)
            for n in range(2):
                for mo in range(KD):
                    for ti in range(KD):
                        m = mm(PS[:, 2 * n + mo, 0:HALF], W1A[:, 3, ti, mo * P:(mo + 1) * P], OT1[:, ti, half(n)],
                               ti == 0, ti == KD - 1)
                    m.then_inc(sem["c_output_summed"], 1)
            norm(5)
            mixture(1, TILES1)

        @block.scalar
        def _(act):
            def norm(i):
                src, _, kind = NORM[i]
                for n in range(2):
                    if kind == "layer":
                        act.wait_ge(sem["norm_centred"], 2 * LAYER[i] + n + 1)
                        src_ = XC
                    else:
                        act.wait_ge(sem[SOURCE[i][0]], SOURCE[i][1](n))
                        src_ = src
                    if 2 * i > 0:
                        act.wait_ge(sem["norm_variance_summed"], 2 * i)
                    act.activation(SQ[:, :, half(n)], src_[:, :, half(n)], ACT.Square).then_inc(sem["norm_squared"], 1)
                for n in range(2):
                    act.wait_ge(sem["norm_variance_summed"], 2 * i + n + 1)
                    if 2 * i - 1 + n > 0:
                        act.wait_ge(sem["norm_done"], 2 * i - 1 + n)
                    act.activation(STD[:, n, :], PS[:, 4 + n, 0:HALF], ACT.Ln, bias=COLS[:, 15:16]).then_inc(sem["norm_log_taken"], 1)
                    act.wait_ge(sem["norm_log_taken"], 2 * i + n + 1)
                    act.activation(STD[:, n, :], STD[:, n, :], ACT.Exp, scale=-0.5).then_inc(sem["norm_rstd_ready"], 1)

            def add_bias(name, first, col, gate, done, slots):
                for i in range(4):
                    n, mo = divmod(i, 2)
                    act.wait_ge(sem[name], i + 1)
                    if i == 0:
                        act.wait_ge(sem["gated_biases_ready"], 4)
                    act.activation(slots[i], PS[:, i, 0:HALF], ACT.Identity, bias=GB[:, col + mo:col + mo + 1],
                                       scale=TG[:, gate:gate + 1]).then_inc(sem[done], 1)

            act.wait_ge(sem["vectors_loaded"], 64)
            act.activation(TG[:, :], G4[:, :], ACT.Tanh).then_inc(sem["gates_ready"], 1)
            act.preload_act_table_set("natural_log_exp_and_others")
            norm(0)
            def context_hi(b):
                act.wait_ge(sem[f"context_loaded{b % 3}"], 16 * (b // 3 + 1))
                if TI0 * (b - 2) > 0:
                    act.wait_ge(sem["a_values_summed"], TI0 * (b - 2))
                act.copy(CTXH[:, b % 3, :, 0:KV], CTX[:, b % 3, :, 0:KV]).then_inc(sem["a_context_high_ready"], 1)

            for i in range(2 * TI0):
                ti, n = divmod(i, 2)
                act.wait_ge(sem["a_query_summed"], i + 1)
                act.activation(QT0[:, ti, half(n)], PS[:, 4 + i % 2, 0:HALF], ACT.Copy, scale=DH0 ** -0.5).then_inc(sem["a_query_copied"], 1)
                if i in (3, 5):
                    context_hi(i // 4)
                if i in W_PIECES:
                    act.wait_ge(sem["a_wkv_loaded"], 16)
                    act.copy(w_piece(WKV0H, W_PIECES.index(i)), w_piece(WKV0, W_PIECES.index(i))).then_inc(sem["a_weights_high_ready"], 1)

            def exps(b):
                act.wait_ge(sem["a_shifted"], b + 1)
                if b > 0:
                    act.wait_ge(sem["a_weights_ready"], b)
                act.activation(SE[:, 0, :], SE[:, 0, :], ACT.Exp).then_inc(sem["a_exp_taken"], 1)

            def vcopy(b):
                act.wait_ge(sem["zeros_set"], 1)
                for ti in range(TI0):
                    i = TI0 * b + ti
                    act.wait_ge(sem["a_values_summed"], i + 1)
                    if i > 2:
                        act.wait_ge(sem["a_weighted"], i - 2)
                    act.copy(VSB[:, i % 3, 0:KV], PS[:, 4 + i % 2, 0:KV]).then_inc(sem["a_values_copied"], 1)

            def products_hi(b, tis):
                for ti in tis:
                    i = TI0 * b + ti
                    act.wait_ge(sem["a_products_ready"], i + 1)
                    if i > 3:
                        act.wait_ge(sem["a_similarity_summed"], i - 3)
                    act.copy(PRODH[:, i % 4, 0:KV], PROD[:, i % 3, 0:KV]).then_inc(sem["a_products_high_ready"], 1)

            products_hi(0, range(TI0))
            for b in range(B - 1):
                products_hi(b + 1, range(2))
                exps(b)
                products_hi(b + 1, range(2, TI0))
                if b + 2 < B:
                    context_hi(b + 2)
                vcopy(b)
            exps(B - 1)
            vcopy(B - 1)
            add_bias("a_output_summed", 0, 0, 0, "a_output_gated", [WK[:, i, :] for i in range(4)])

            for i in range(6):
                act.wait_ge(sem["b_weights_folded"], i + 1)
                if i < 4:
                    dst = WQA[:, i // 2, 512 * (i % 2):512 * (i % 2) + 512]
                    src = PS[:, 6 + i % 2, :]
                else:
                    dst = WOA[:, 2 * (i - 4):2 * (i - 4) + 2, :]
                    src = PS[:, 6 + i % 2, :].rearrange("p (t c) -> p t c", t=2)
                act.copy(dst, src).then_inc(sem["b_folded_copied"], 1)
            norm(1)
            norm(2)
            for n in range(2):
                act.wait_ge(sem["b_latent_summed"], n + 1)
                act.copy(CK[:, half(n)], PS[:, n, 0:HALF]).then_inc(sem["b_latent_copied"], 1)
            act.wait_ge(sem["b_latent_rows_summed"], 1)
            act.copy(LT, PS[0:S, 2, 0:B * LAT].rearrange("p (b c) -> p b c", b=B)).then_inc(sem["b_latent_rows_copied"], 1)
            act.wait_ge(sem["a_added_to_x"], 4)
            for i in range(16):
                act.wait_ge(sem["b_query_summed"], i + 1)
                if i > 2:
                    act.wait_ge(sem["b_query_read"], i - 2)
                if i > 2:
                    act.wait_ge(sem["b_query_cosines"], i - 2)
                act.copy(QS[:, i % 3, :], PS[:, 4 + i % 4, 0:HALF]).then_inc(sem["b_query_copied"], 1)

            def exp_b(i):
                act.wait_ge(sem["b_maxima_found"], i + 1)
                if 2 * (i - 1) > 0:
                    act.wait_ge(sem["b_probs_turned"], 2 * (i - 1))
                if i > 1:
                    act.wait_ge(sem["b_probs_ready"], i - 1)
                for x in range(4):
                    act.activation(PB[:, i % 2, (4 + x) * S:(5 + x) * S], PS[0:S, 2 * (i % 2) + 1, x * S:(x + 1) * S],
                                   ACT.Exp, bias=RTC[:, 5 * (i % 2), x:x + 1], scale=0.125,
                                   accum_out=RTC[:, 1 + 2 * (i % 2), 4 + x:5 + x])
                act.wait_ge(sem["b_scores_shifted"], i + 1)
                act.activation(PB[:, i % 2, 0:4 * S], SMB[:, i % 2, 0:4 * S], ACT.Exp, scale=0.125).then_inc(sem["b_exp_taken"], 1)

            def turn_b(i):
                for q in range(2):
                    act.wait_ge(sem["b_probs_turned"], 2 * i + q + 1)
                    if i > 1:
                        act.wait_ge(sem["b_heads_mixed"], i - 1)
                    act.copy(PT0[:, i % 2, 4 * q * S:4 * (q + 1) * S], PS[0:S, 4 + q, 0:4 * S]).then_inc(sem["b_turned_copied"], 1)

            def mix_b(i):
                b, g = divmod(i, 2)
                act.wait_ge(sem["b_heads_mixed"], i + 1)
                act.copy(UT[:, 2 * g:2 * g + 2, tok(b)],
                             PS[:, 6 + i % 2, 0:2 * S].rearrange("p (t c) -> p t c", t=2)).then_inc(sem["b_mixed_copied"], 1)

            for i in range(2 * B + 3):
                if i < 2 * B:
                    exp_b(i)
                if 2 <= i < 2 * B + 2:
                    turn_b(i - 2)
                if i >= 3:
                    mix_b(i - 3)
            norm(3)

            def split_hi0(e):
                act.wait_ge(sem["moe0_weights_loaded"], 48)
                act.wait_ge(sem["b_output_summed"], 4)
                for down in range(2):
                    act.copy(tile_of0("high", e, down), tile_of0("raw", e, down)).then_inc(sem["expert_high_ready"], 1)

            def split_hi(e, m):
                act.wait_ge(sem[f"expert_loaded{e % 2}"], 48 * (e // 2 + 1))
                if N0 + 2 * HT1 * (e - 1) if e > 1 else N0 > 0:
                    act.wait_ge(sem["down_summed"], N0 + 2 * HT1 * (e - 1) if e > 1 else N0)
                if e:
                    act.wait_ge(sem["c_output_summed"], 4)
                for down in range(2):
                    rows = HW1 if down else P
                    act.copy(tile_of(RINGH[0:rows, e % 2, :], m, down), tile_of(RING[0:rows, e % 2, :], m, down)).then_inc(sem["expert_high_ready"], 1)

            def mixture(which, tiles):
                first, w, count = (0, N0)[which], (I0, HW1)[which], 2 * len(tiles)

                def gated(i):
                    e, m_ = tiles[i // 2]
                    act.wait_ge(sem["gate_summed"], first + i + 1)
                    if first + i > 2:
                        act.wait_ge(sem["hidden_ready"], first + i - 2)
                    bias = 0.0 if which == 0 else BIAS1[:, e * HT1 + m_:e * HT1 + m_ + 1]
                    act.activation(SIL[0:w, i % 3, :], PS[0:w, 4 + 2 * (i % 2), 0:HALF], ACT.Silu, bias=bias).then_inc(sem["gate_activated"], 1)

                for n in range(2):
                    act.wait_ge(sem["norm_done"], (6, 10)[which] + n + 1)
                    if which == 1:
                        act.activation(SQ[:, :, half(n)], XC[:, :, half(n)], ACT.Square).then_inc(sem["router_squares_ready"], 1)
                for n in range(2):
                    act.wait_ge(sem[("b_output_summed", "c_output_summed")[which]], 4)
                    act.copy(XH[:, :, half(n)], XC[:, :, half(n)]).then_inc(sem["x_high_ready"], 1)
                if which == 0:
                    split_hi0(0)
                    split_hi0(1)
                else:
                    act.copy(B2H[:, :], B2E[:, :]).then_inc(sem["output_bias_high_ready"], 1)
                    act.wait_ge(sem["router_scores_shifted"], 2)
                    act.activation(RT[:, 0, :], RT[:, 0, :], ACT.Sqrt).then_inc(sem["router_function_taken"], 1)
                act.wait_ge(sem["router_scores_shifted"], (1, 3)[which])
                dst = RT[:, 0, :] if which == 0 else RTC[:, 2, :]
                act.activation(dst, dst, ACT.Exp).then_inc(sem["router_function_taken"], 1)
                gated(0)
                gated(1)
                for q in range(2):
                    act.wait_ge(sem["router_weights_turned"], 2 * which + q + 1)
                    act.copy(WTS[:, half(q)], PS[0:40, 1 + q, 0:HALF]).then_inc(sem["router_turned_copied"], 1)
                for i in range(0, 16, 2):
                    act.wait_ge(sem["router_weights_spread"], 16 * which + i + 1)
                    act.copy(WEB[:, i // 2, half(i % 2)], PS[:, i % 4, 0:HALF]).then_inc(sem["router_spread_copied"], 1)
                for i in range(count):
                    e = tiles[i // 2][0]
                    if i >= 2:
                        gated(i)
                    routed = which == 1 or i < ROUTED0
                    act.wait_ge(sem["hidden_weighed" if routed else "hidden_ready"], (0, ROUTED0 if routed else N0)[which] + i + 1)
                    if first + i > 2:
                        act.wait_ge(sem["down_summed"], first + i - 2)
                    act.copy(HTH[0:w, i % 3, :], HT[0:w, i % 3, :]).then_inc(sem["hidden_high_ready"], 1)
                    if which == 0 and i % 2 == 0 and i // 2 + 2 <= E0:
                        split_hi0(i // 2 + 2)
                    if which == 1 and i % 12 >= SPLIT and e + 1 < E1:
                        split_hi(e + 1, i % 12 - SPLIT)

            def copies(b, piece):
                if piece < 2:
                    act.wait_ge(sem["c_keys_summed"], 2 * b + piece + 1)
                    if b >= 2:
                        act.wait_ge(sem["c_scores_summed"], 16 * (b - 1))
                    if b < 2:
                        if (N0, 4)[b] > 0:
                            act.wait_ge(sem[("down_summed", "c_query_summed")[b]], (N0, 4)[b])
                    act.activation(KTH[b % 2][:, piece, 0:KV], PS[:, key_bank(b, piece), 0:KV], ACT.Identity,
                                       bias=COLS[:, 8 + piece:9 + piece]).then_inc(sem["c_keys_copied"], 1)
                    return
                if b >= 2:
                    act.wait_ge(sem["c_heads_mixed"], 16 * (b - 1))
                act.wait_ge(sem["zeros_set"], 3)
                if 2 * b + piece > 1:
                    act.wait_ge(sem["c_values_summed"], 2 * b + piece - 1)
                for par in range(2):
                    if piece == 2:
                        src = PS[0:CH, 7, :].rearrange("p (c h d) -> p c h d", c=2, d=32)
                        dst = VP[:, b % 2, par, 0:2, :].rearrange("p c (h d) -> p c h d", d=32)
                        src, dst = (a[:, :, :, 16 * par:16 * par + 16] for a in (src, dst))
                    else:
                        src = PS[0:CHS[2], 7, 0:D].rearrange("p (h d) -> p h d", d=32)
                        dst = VP[0:CHS[2], b % 2, par, 2, :].rearrange("p (h d) -> p h d", d=32)
                        src, dst = (a[:, :, 16 * par:16 * par + 16] for a in (src, dst))
                    act.copy(dst, src).then_inc(sem["c_values_copied"], 1)

            mixture(0, TILES0)
            act.preload_act_table_set("natural_log_exp_and_others")
            for piece in range(2):
                copies(0, piece)
            norm(4)

            def exp_c(i):
                act.wait_ge(sem["c_maximum_found"], i + 1)
                if i + 1 > NPC:
                    act.wait_ge(sem["c_probs_turned"], i + 1 - NPC)
                if i > 5:
                    act.wait_ge(sem["c_sum_inverted"], i - 5)
                act.activation(PC[:, i % NPC, 0:KV], SMK[:, i % 4, :], ACT.Exp, bias=SM1[:, 0, i % 6:i % 6 + 1],
                                   scale=-1.0, accum_out=SM1[:, 1, i % 6:i % 6 + 1]).then_inc(sem["c_exp_taken"], 1)

            def turn_c(i):
                act.wait_ge(sem["c_probs_turned"], i + 1)
                if i > 3:
                    act.wait_ge(sem["c_heads_mixed"], i - 3)
                act.copy(PTC[:, i % 4, :], PS[0:CH, 3 + i % 3, 0:3 * S]).then_inc(sem["c_turned_copied"], 1)

            for piece in range(2, 4):
                copies(0, piece)
            for i in range(16 * B + TURN + 1):
                if i > TURN:
                    turn_c(i - TURN - 1)
                if i < 16 * B:
                    exp_c(i)
                if i % 16 == 12 and i // 16 < HT1:
                    split_hi(0, i // 16)
                if i == 16 * HT1:
                    act.wait_ge(sem["moe1_small_loaded"], 32)
                    act.activation(CENTSQ, CENT, ACT.Square).then_inc(sem["router_squares_ready"], 1)
                    act.activation(CENT2, CENT, ACT.Copy, scale=-2.0).then_inc(sem["router_squares_ready"], 1)
                if i % 16 in PIECES and i // 16 + 1 < B:
                    copies(i // 16 + 1, PIECES.index(i % 16))
            add_bias("c_output_summed", 0, 2, 1, "c_output_gated", [WK[:, i, :] for i in range(4)])
            norm(5)
            mixture(1, TILES1)

        @block.gpsimd
        def _(pool):
            pool.memset(VSB, 0.0).then_inc(sem["zeros_set"], 1)
            for i in range(TI0 * B):
                pool.wait_ge(sem["a_products_high_ready"], i + 1)
                if i > 3:
                    pool.wait_ge(sem["a_similarity_summed"], i - 3)
                low, raw, high = PRODL[:, i % 4, 0:KV], PROD[:, i % 3, 0:KV], PRODH[:, i % 4, 0:KV]
                pool.tensor_tensor(low, raw, high, ALU.subtract).then_inc(sem["a_products_low_ready"], 1)
            pool.wait_ge(sem["b_folded_copied"], 6)
            pool.memset(CKM[64:P, 0, :], 0.0).then_inc(sem["b_zero_keys_set"], 1)
            pool.memset(CKM[0:64, 1, :], 0.0).then_inc(sem["b_zero_keys_set"], 1)
            pool.wait_ge(sem["b_zero_keys_set"], 2)
            for i in range(16):
                n, tq = divmod(i, 8)
                pool.wait_ge(sem["b_query_copied"], i + 1)
                v = lambda a: a.rearrange("p (b i) -> p b i", b=HB)
                co = CS[:, 0, :].unsqueeze(1).to_broadcast([P, HB, S])
                pool.tensor_tensor(v(QP[:, tq, half(n)]), v(QS[:, i % 3, :]), co, ALU.mult).then_inc(sem["b_query_cosines"], 1)
            pool.wait_ge(sem["moe_added_to_x"], 4)
            pool.memset(PC[:, :, KV:3 * CH], 0.0).then_inc(sem["zeros_set"], 1)
            pool.memset(VP, 0.0).then_inc(sem["zeros_set"], 1)
            for b in range(B):
                for mo in range(KD):
                    if mo + 1 if b < HB else 4 > 0:
                        pool.wait_ge(sem["c_query_low_ready"], mo + 1 if b < HB else 4)
                    if b >= 2:
                        pool.wait_ge(sem["c_scores_summed"], 16 * (b - 1))
                    one = PAR[:, :].unsqueeze(2).to_broadcast([P, 8, S])
                    for dst, src in ((QXH, QCH), (QXL, QCL)):
                        q = src[:, mo, tok(b)].unsqueeze(1).to_broadcast([P, 8, S])
                        pool.tensor_tensor(dst[:, b % 2, mo, :, :], q, one, ALU.mult).then_inc(sem["c_query_split"], 1)

        @block.vector
        def _(dve):
            chain = [0]

            def link(ins):
                chain[0] += 1
                ins.then_inc(sem["dve_step_done"], 1)
                dve.wait_ge(sem["dve_step_done"], chain[0])

            def norm(i):
                src, dst, kind = NORM[i]
                for n in range(2):
                    if kind == "layer":
                        li = LAYER[i]
                        dve.wait_ge(sem["norm_mean_summed"], 2 * li + n + 1)
                        mean = PS[:, 4 + n, 0:HALF].unsqueeze(1).to_broadcast([P, KD, HALF])
                        dve.tensor_tensor(XC[:, :, half(n)], src[:, :, half(n)], mean, ALU.subtract).then_inc(sem["norm_centred"], 1)
                for n in range(2):
                    dve.wait_ge(sem["norm_rstd_ready"], 2 * i + n + 1)
                    if kind == "layer":
                        dve.wait_ge(sem["norm_centred"], 2 * LAYER[i] + n + 1)
                        rstd = STD[:, n, :].unsqueeze(1).to_broadcast([P, KD, HALF])
                        dve.tensor_tensor(dst[:, :, half(n)], XC[:, :, half(n)], rstd, ALU.mult).then_inc(sem["norm_done"], 1)
                    else:
                        for k in range(KD):
                            ins = dve.scalar_tensor_tensor(XC[:, k, half(n)], src[:, k, half(n)],
                                                           COLS[:, kind + k:kind + k + 1], STD[:, n, :],
                                                           ALU.mult, ALU.mult)
                        ins.then_inc(sem["norm_done"], 1)

            dve.wait_ge(sem["constants_loaded"], 16 * 8)
            dve.memset(RTX, 0.0).then_inc(sem["unit_rows_ready"], 1)
            dve.tensor_copy(UNIT[0:32, :], IDN[0:32, 0:8]).then_inc(sem["unit_rows_ready"], 1)
            dve.tensor_copy(UNIT[32:40, :], IDN[32:40, 32:40]).then_inc(sem["unit_rows_ready"], 1)
            dve.wait_ge(sem["unit_rows_ready"], 3)
            dve.tensor_copy(HSR[:, :], HS[:, :]).then_inc(sem["a_head_rows_rounded"], 1)
            dve.memset(PS[:, 0:2, KV:HALF], 0.0)
            dve.memset(PS[:, 6:8, KV:HALF], 0.0)
            dve.memset(PS[0:H0, 2:4, KV:HALF], NEG).then_inc(sem["psum_tails_set"], 1)
            dve.wait_ge(sem["zeros_set"], 1)
            zeros = VSB[:, 0, 0:3 * KD].rearrange("p (s k c) -> p s k c", s=3, k=KD)
            dve.tensor_copy(CTXH[:, :, :, KV:KVE], zeros).then_inc(sem["pads_set"], 1)
            dve.tensor_copy(CTXL[:, :, :, KV:KVE], zeros).then_inc(sem["pads_set"], 1)
            dve.wait_ge(sem["gates_ready"], 1)
            dve.wait_ge(sem["vectors_loaded"], 64)
            for i in range(4):
                gate, col = i // 2, (4, 12)[i // 2] + i % 2
                dve.tensor_tensor(GB[:, i:i + 1], COLS[:, col:col + 1], TG[:, gate:gate + 1], ALU.mult).then_inc(sem["gated_biases_ready"], 1)
            dve.wait_ge(sem["constants_loaded"], 16 * 8)
            dve.wait_ge(sem["x_loaded"], 16)
            norm(0)

            dve.wait_ge(sem["norm_variance_summed"], 2)
            dve.tensor_copy(SPREAD.rearrange("p t (a d) -> p (t a) d", d=DH0),
                                IDN[0:H0, 0:H0].unsqueeze(2).to_broadcast([H0, H0, DH0])).then_inc(sem["a_spread_rows_built"], 1)
            dve.tensor_scalar(PRODL[:, :, KV:KVE], VSB[:, 0, 0:4].unsqueeze(2), 0.0, None, ALU.add).then_inc(sem["pads_set"], 1)
            def context_lo(b):
                dve.wait_ge(sem["a_context_high_ready"], b + 1)
                low, raw, high = (a[:, b % 3, :, 0:KV] for a in (CTXL, CTX, CTXH))
                dve.tensor_tensor(low, raw, high, ALU.subtract).then_inc(sem["a_context_low_ready"], 1)

            context_lo(0)
            context_lo(1)
            for i in range(4):
                dve.wait_ge(sem["a_weights_high_ready"], i + 1)
                dve.tensor_tensor(w_piece(WKV0L, i), w_piece(WKV0, i), w_piece(WKV0H, i), ALU.subtract).then_inc(sem["a_weights_low_ready"], 1)

            dve.wait_ge(sem["a_query_summed"], 2 * TI0)
            dve.tensor_scalar(PRODH[:, :, KV:KVE], VSB[:, 0, 0:4].unsqueeze(2), NEG, None, ALU.add).then_inc(sem["pads_set"], 1)
            dve.wait_ge(sem["a_query_copied"], 2 * TI0)

            def products(b, tis):
                for ti in tis:
                    i = TI0 * b + ti
                    dve.wait_ge(sem["a_keys_summed"], i + 1)
                    if i > 2:
                        dve.wait_ge(sem["a_products_low_ready"], i - 2)
                    q = QT0[:, ti, tok(b)].unsqueeze(1).to_broadcast([P, NC, S])
                    k = PS[:, i % 2, 0:HALF].rearrange("p (c i) -> p c i", c=NC)
                    out = PROD[:, i % 3, :].rearrange("p (c i) -> p c i", c=NC)
                    dve.tensor_tensor(out, k, q, ALU.mult).then_inc(sem["a_products_ready"], 1)

            def softmax_a(b, step):
                s = PS[0:H0, 2 + b % 2, 0:HALF]
                e = SE[:, 0, :].rearrange("p (c i) -> p c i", c=NC)
                if step == 0:
                    dve.wait_ge(sem["a_similarity_summed"], TI0 * (b + 1))
                    link(dve.tensor_reduce(SM0[:, 0, :], s.rearrange("p (c i) -> p i c", c=NC), AX_X, ALU.max))
                elif step == 1:
                    top = SM0[:, 0, :].unsqueeze(1).to_broadcast([H0, NC, S])
                    if b > 0:
                        dve.wait_ge(sem["a_probs_low_ready"], b)
                    dve.tensor_tensor(e, s.rearrange("p (c i) -> p c i", c=NC), top, ALU.subtract).then_inc(sem["a_shifted"], 1)
                elif step == 2:
                    dve.wait_ge(sem["a_exp_taken"], b + 1)
                    link(dve.tensor_reduce(SM0[:, 1, :], SE[:, 0, :].rearrange("p (c i) -> p i c", c=NC), AX_X, ALU.add))
                elif step == 3:
                    link(dve.reciprocal(SM0[:, 2, :], SM0[:, 1, :]))
                elif step == 4:
                    inv = SM0[:, 2, :].unsqueeze(1).to_broadcast([H0, NC, S])
                    dve.tensor_tensor(SE[:, 1, :].rearrange("p (c i) -> p c i", c=NC), e, inv, ALU.mult).then_inc(sem["a_weights_ready"], 1)
                elif step == 5:
                    dve.wait_ge(sem["a_weights_ready"], b + 1)
                    if TI0 * (b - 1) > 0:
                        dve.wait_ge(sem["a_weights_spread"], TI0 * (b - 1))
                    dve.tensor_copy(SEH[:, b % 2, :], SE[:, 1, :]).then_inc(sem["a_probs_high_ready"], 1)
                else:
                    dve.wait_ge(sem["a_probs_high_ready"], b + 1)
                    dve.tensor_tensor(SEL[:, b % 2, :], SE[:, 1, :], SEH[:, b % 2, :], ALU.subtract).then_inc(sem["a_probs_low_ready"], 1)

            def weigh(b):
                for ti in range(TI0):
                    i = TI0 * b + ti
                    dve.wait_ge(sem["a_weights_spread"], i + 1)
                    dve.wait_ge(sem["a_values_copied"], i + 1)
                    if i > 1:
                        dve.wait_ge(sem["a_heads_mixed"], i - 1)
                    if i == 0:
                        dve.wait_ge(sem["zeros_set"], 1)
                    dve.tensor_tensor(PV[:, i % 2, :], PS[:, 6 + i % 2, 0:HALF], VSB[:, i % 3, :], ALU.mult).then_inc(sem["a_weighted"], 1)
                    dve.wait_ge(sem["a_weighted"], i + 1)
                    dve.tensor_reduce(OT0[:, ti, tok(b)], PV[:, i % 2, :].rearrange("p (c i) -> p i c", c=NC),
                                          AX_X, ALU.add).then_inc(sem["a_heads_mixed"], 1)

            for b in range(B):
                for ti in range(TI0):
                    products(b, [ti])
                    if b and ti < 7:
                        softmax_a(b - 1, ti)
                if b:
                    if b + 1 < B:
                        context_lo(b + 1)
                    weigh(b - 1)
            for step in range(7):
                softmax_a(B - 1, step)
            weigh(B - 1)

            def add_to_x(name, done):
                for i in range(4):
                    n, mo = divmod(i, 2)
                    dve.wait_ge(sem[name], i + 1)
                    dve.tensor_tensor(X[:, mo, half(n)], X[:, mo, half(n)], WK[:, i, :], ALU.add).then_inc(sem[done], 1)

            add_to_x("a_output_gated", "a_added_to_x")

            norm(1)
            dve.wait_ge(sem["norm_done"], 4)
            norm(2)

            for n in range(2):
                dve.wait_ge(sem["b_latent_copied"], n + 1)
                co = CS[:, 0, :].unsqueeze(1).to_broadcast([P, HB, S])
                si = CS[:, 1, :].unsqueeze(1).to_broadcast([P, HB, S])
                v = lambda a: a.rearrange("p (b i) -> p b i", b=HB)
                link(dve.stream_shuffle(CK2[:, half(n)], CK[:, half(n)], [q ^ 1 for q in range(32)]))
                link(dve.tensor_tensor(v(CK2[:, half(n)]), v(CK2[:, half(n)]), si, ALU.mult))
                link(dve.tensor_tensor(v(CK[:, half(n)]), v(CK[:, half(n)]), co, ALU.mult))
                for par in range(2):
                    rows = slice(64 * par, 64 * par + 64)
                    dve.tensor_tensor(CKM[rows, par, half(n)], CK[rows, half(n)], CK2[rows, half(n)], ALU.add).then_inc(sem["b_latent_rotated"], 1)
            dve.wait_ge(sem["b_folded_copied"], 6)
            dve.tensor_copy(CMB, CM[:, :]).then_inc(sem["b_mask_rounded"], 1)
            dve.tensor_copy(IDNB, IDN[0:S, 0:S]).then_inc(sem["b_mask_rounded"], 1)
            for i in range(16):
                n, tq = divmod(i, 8)
                dve.wait_ge(sem["b_query_copied"], i + 1)
                dst = QP[:, tq, half(n)]
                if i > 2:
                    dve.wait_ge(sem["b_query_rotated"], i - 2)
                dve.stream_shuffle(SH[:, i % 3, :], QS[:, i % 3, :], [q ^ 1 for q in range(32)]).then_inc(sem["b_query_read"], 1)
                dve.wait_ge(sem["b_query_read"], i + 1)
                link(dve.tensor_tensor(v(SH[:, i % 3, :]), v(SH[:, i % 3, :]), si, ALU.mult))
                dve.wait_ge(sem["b_query_cosines"], i + 1)
                dve.tensor_tensor(dst, dst, SH[:, i % 3, :], ALU.add).then_inc(sem["b_query_rotated"], 1)

            def shift_b(i):
                dve.wait_ge(sem["b_scores_summed"], i + 1)
                s = PS[0:S, 2 * (i % 2):2 * (i % 2) + 2, 0:4 * S].rearrange("p a (x c) -> p a x c", x=4)
                out = SMB[:, i % 2, 0:4 * S].rearrange("p (x c) -> p x c", x=4)
                top = RTC[:, 6 + i % 2, :]
                link(dve.tensor_reduce(top.rearrange("p (a x) -> p a x", a=2), s, AX_X, ALU.max))
                if i > 1:
                    dve.wait_ge(sem["b_exp_taken"], i - 1)
                dve.tensor_scalar(RTC[:, 5 * (i % 2), 0:4], top[:, 4:8], -0.125, None, ALU.mult).then_inc(sem["b_maxima_found"], 1)
                dve.tensor_tensor(out, s[:, 0, :, :], top[:, 0:4].unsqueeze(2).to_broadcast([S, 4, S]),
                                      ALU.subtract).then_inc(sem["b_scores_shifted"], 1)

            def divide_b(i):
                dve.wait_ge(sem["b_exp_taken"], i + 1)
                p3 = PB[:, i % 2, :].rearrange("p (h c) -> p h c", h=8)
                sums, inv = RTC[:, 1 + 2 * (i % 2), :], RTC[:, 2 + 2 * (i % 2), :]
                link(dve.tensor_reduce(sums[:, 0:4], p3[:, 0:4, :], AX_X, ALU.add))
                link(dve.reciprocal(inv, sums))
                dve.tensor_tensor(p3, p3, inv.unsqueeze(2).to_broadcast([S, 8, S]), ALU.mult).then_inc(sem["b_probs_ready"], 1)

            for i in range(2 * B + 1):
                if i < 2 * B:
                    shift_b(i)
                if i:
                    divide_b(i - 1)
            for i in range(4):
                n, mo = divmod(i, 2)
                dve.wait_ge(sem["b_output_summed"], i + 1)
                dve.tensor_tensor(Y[:, mo, half(n)], PS[:, i, 0:HALF], Y[:, mo, half(n)], ALU.add).then_inc(sem["b_added_to_y"], 1)
            norm(3)

            def router(which):
                def v(i):
                    return RT[:, i, :].rearrange("p (b e) -> p b e", b=B)

                def wide(a):
                    return a.unsqueeze(2).to_broadcast([S, B, 8])

                dve.wait_ge(sem["router_scores_summed"], which + 1)
                ps = PS[0:S, 0, 0:B * 8].rearrange("p (b e) -> p b e", b=B)
                if which == 0:
                    link(dve.tensor_tensor(v(0), ps, EB[:, :].unsqueeze(1).to_broadcast([S, B, 8]), ALU.add))
                    link(dve.tensor_reduce(RTC[:, 0, :], v(0), AX_X, ALU.max))
                    dve.tensor_tensor(v(0), v(0), wide(RTC[:, 0, :]), ALU.subtract).then_inc(sem["router_scores_shifted"], 1)
                    dve.wait_ge(sem["router_function_taken"], 1)
                else:
                    link(dve.tensor_tensor(v(0), ps, CSQ.unsqueeze(1).to_broadcast([S, B, 8]), ALU.add))
                    dve.tensor_scalar(RT[:, 0, :], RT[:, 0, :], 1e-12, None, ALU.max).then_inc(sem["router_scores_shifted"], 1)
                    dve.wait_ge(sem["router_function_taken"], 2)
                for c in range(2):
                    src, top, one = (v(0), v(3))[c], RTC[:, 3 + c, :], v(1 + 3 * c)
                    link(dve.tensor_reduce(top, src, AX_X, ALU.max))
                    link(dve.tensor_tensor(v(5), src, wide(top), ALU.is_equal))
                    link(dve.tensor_tensor(v(5), v(5), RANK[:, :].unsqueeze(1).to_broadcast([S, B, 8]), ALU.mult))
                    link(dve.tensor_reduce(RTC[:, 5, :], v(5), AX_X, ALU.max))
                    link(dve.tensor_tensor(one, v(5), wide(RTC[:, 5, :]), ALU.is_equal))
                    if c == 0:
                        link(dve.scalar_tensor_tensor(RT[:, 3, :], RT[:, 1, :], NEG, RT[:, 0, :], ALU.mult, ALU.add))
                if which == 0:
                    link(dve.tensor_tensor(RTC[:, 5, :], RTC[:, 3, :], RTC[:, 4, :], ALU.add))
                    link(dve.reciprocal(RTC[:, 6, :], RTC[:, 5, :]))
                    link(dve.tensor_tensor(v(5), v(1), v(4), ALU.add))
                    link(dve.tensor_tensor(v(5), v(5), v(0), ALU.mult))
                    link(dve.tensor_tensor(v(13), v(5), wide(RTC[:, 6, :]), ALU.mult))
                else:
                    dve.tensor_tensor(RTC[:, 2, :], RTC[:, 4, :], RTC[:, 3, :], ALU.subtract).then_inc(sem["router_scores_shifted"], 1)
                    dve.wait_ge(sem["router_function_taken"], 3)
                    link(dve.tensor_scalar(RTC[:, 5, :], RTC[:, 2, :], 1.0, None, ALU.add))
                    link(dve.reciprocal(RTC[:, 6, :], RTC[:, 5, :]))
                    link(dve.tensor_tensor(RTC[:, 2, :], RTC[:, 2, :], RTC[:, 6, :], ALU.mult))
                    link(dve.tensor_tensor(v(1), v(1), wide(RTC[:, 6, :]), ALU.mult))
                    link(dve.tensor_tensor(v(4), v(4), wide(RTC[:, 2, :]), ALU.mult))
                    link(dve.tensor_tensor(v(13), v(1), v(4), ALU.add))
                dve.tensor_copy(RTH[:, :], RT[:, 13, :]).then_inc(sem["router_high_ready"], 1)
                dve.wait_ge(sem["router_high_ready"], which + 1)
                high = RTH[:, :].rearrange("p (b e) -> p b e", b=B)
                if which:
                    dve.wait_ge(sem["router_weights_turned"], 2)
                dve.tensor_copy(RTX[:, :, 0:8], high).then_inc(sem["router_weights_ready"], 1)
                dve.tensor_tensor(RTX[:, :, 32:40], v(13), high, ALU.subtract).then_inc(sem["router_weights_ready"], 1)

            def split_lo0(e):
                for down in range(2):
                    dve.wait_ge(sem["expert_high_ready"], 2 * e + down + 1)
                    dve.tensor_tensor(tile_of0("low", e, down), tile_of0("raw", e, down), tile_of0("high", e, down),
                                          ALU.subtract).then_inc(sem["expert_low_ready"], 1)

            def split_lo(e, m):
                for down in range(2):
                    rows = HW1 if down else P
                    dve.wait_ge(sem["expert_high_ready"], 2 * (E0 + 1) + 2 * (HT1 * e + m) + down + 1)
                    raw = tile_of(RING[0:rows, e % 2, :], m, down)
                    hi = tile_of(RINGH[0:rows, e % 2, :], m, down)
                    dve.tensor_tensor(tile_of(RINGL[0:rows, e % 2, :], m, down), raw, hi, ALU.subtract).then_inc(sem["expert_low_ready"], 1)

            def mixture(which, tiles):
                first, fw = (0, N0)[which], (0, ROUTED0)[which]
                w, count = (I0, HW1)[which], 2 * len(tiles)

                def hidden_lo(i):
                    dve.wait_ge(sem["hidden_high_ready"], first + i + 1)
                    h = [a[0:w, i % 3, :] for a in (HTL, HT, HTH)]
                    dve.tensor_tensor(h[0], h[1], h[2], ALU.subtract).then_inc(sem["hidden_low_ready"], 1)

                for n in range(2):
                    dve.wait_ge(sem["x_high_ready"], 2 * which + n + 1)
                    dve.tensor_tensor(XL[:, :, half(n)], XC[:, :, half(n)], XH[:, :, half(n)], ALU.subtract).then_inc(sem["x_low_ready"], 1)
                if which == 0:
                    split_lo0(0)
                router(which)
                if which == 0:
                    split_lo0(1)
                else:
                    dve.wait_ge(sem["output_bias_high_ready"], 1)
                    dve.tensor_tensor(B2L[:, :], B2E[:, :], B2H[:, :], ALU.subtract).then_inc(sem["output_bias_low_ready"], 1)
                def gate_up(i):
                    e, m_ = tiles[i // 2]
                    dve.wait_ge(sem["up_summed"], first + i + 1)
                    dve.wait_ge(sem["gate_activated"], first + i + 1)
                    if first + i > 2:
                        dve.wait_ge(sem["hidden_low_ready"], first + i - 2)
                    col = E1 * HT1 + e * HT1 + m_
                    b1 = 0.0 if which == 0 else BIAS1[:, col:col + 1]
                    dve.scalar_tensor_tensor(HT[0:w, i % 3, :], PS[0:w, 5 + 2 * (i % 2), 0:HALF], b1,
                                                 SIL[0:w, i % 3, :], ALU.add, ALU.mult).then_inc(sem["hidden_ready"], 1)

                gate_up(0)
                gate_up(1)
                for i in range(1, 16, 2):
                    dve.wait_ge(sem["router_weights_spread"], 16 * which + i + 1)
                    dve.tensor_copy(WEB[:, i // 2, half(i % 2)], PS[:, i % 4, 0:HALF]).then_inc(sem["router_spread_copied_odd"], 1)
                for i in range(count):
                    (e, m_), n = tiles[i // 2], i % 2
                    h = HT[0:w, i % 3, :]
                    if i >= 2:
                        gate_up(i)
                    if which == 1 or i < ROUTED0:
                        dve.wait_ge(sem["hidden_ready"], first + i + 1)
                        if i < 2:
                            dve.wait_ge(sem["router_spread_copied"], 8 * which + 8)
                            dve.wait_ge(sem["router_spread_copied_odd"], 8 * which + 8)
                        dve.tensor_tensor(h, h, WEB[0:w, e, half(n)], ALU.mult).then_inc(sem["hidden_weighed"], 1)
                    if which == 0 and i == 10:
                        dve.wait_ge(sem["mask_loaded"], 16)
                        link(dve.tensor_copy(MKB.rearrange("p b c -> p (b c)"), MK8.bitcast(U8)))
                    if which == 0 and i == 12:
                        dve.tensor_scalar(MKB.rearrange("p b c -> p (b c)"), MKB.rearrange("p b c -> p (b c)"),
                                              -NEG, NEG, ALU.mult, ALU.add).then_inc(sem["mask_ready"], 1)
                    if i:
                        hidden_lo(i - 1)
                    if which == 0 and i % 2 == 0 and i // 2 + 2 <= E0:
                        split_lo0(i // 2 + 2)
                    if which == 1 and i % 12 >= SPLIT and e + 1 < E1:
                        split_lo(e + 1, i % 12 - SPLIT)
                hidden_lo(count - 1)
                for i in range(4):
                    n, mo = divmod(i, 2)
                    dve.wait_ge(sem["down_summed"], first + 2 * len(tiles) - 1 + n)
                    ps, x = PS[:, i, 0:HALF], X[:, mo, half(n)]
                    if which == 0:
                        link(dve.tensor_tensor(Y[:, mo, half(n)], ps, Y[:, mo, half(n)], ALU.add))
                        dve.scalar_tensor_tensor(x, Y[:, mo, half(n)], TG[:, 2:3], x, ALU.mult, ALU.add).then_inc(sem["moe_added_to_x"], 1)
                    else:
                        dve.scalar_tensor_tensor(x, ps, TG[:, 3:4], x, ALU.mult, ALU.add).then_inc(sem["moe_added_to_x"], 1)

            mixture(0, TILES0)
            dve.tensor_scalar(KTL[:, :, :, KV:KVE].rearrange("p s m c -> p (s m c)"), AVG[:, 0:4], 0.0, None,
                                  ALU.mult).then_inc(sem["c_pads_set"], 1)
            dve.tensor_scalar(KTH[0][:, :, KV:KVE], AVG[:, 0:2].unsqueeze(2), 0.0, None, ALU.mult).then_inc(sem["c_pads_set"], 1)

            def keys_lo(b, ti):
                dve.wait_ge(sem["c_keys_copied"], 2 * b + ti + 1)
                if b >= 2:
                    dve.wait_ge(sem["c_scores_summed"], 16 * (b - 1))
                dve.scalar_tensor_tensor(KTL[:, b % 2, ti, 0:KV], PS[:, key_bank(b, ti), 0:KV], COLS[:, 8 + ti:9 + ti],
                                             KTH[b % 2][:, ti, 0:KV], ALU.add, ALU.subtract).then_inc(sem["c_keys_low_ready"], 1)

            norm(4)
            keys_lo(0, 0)
            keys_lo(0, 1)

            for i in range(4):
                n, mo = divmod(i, 2)
                dve.wait_ge(sem["c_query_summed"], i + 1)
                bias = COLS[:, 6 + mo:7 + mo]
                dve.tensor_scalar(QCH[:, mo, half(n)], PS[:, i, 0:HALF], bias, None, ALU.add).then_inc(sem["c_query_copied"], 1)
                dve.wait_ge(sem["c_query_copied"], i + 1)
                dve.scalar_tensor_tensor(QCL[:, mo, half(n)], PS[:, i, 0:HALF], bias, QCH[:, mo, half(n)],
                                             ALU.add, ALU.subtract).then_inc(sem["c_query_low_ready"], 1)
            dve.wait_ge(sem["c_query_summed"], 4)
            dve.tensor_scalar(KTH[1][:, :, KV:KVE], AVG[:, 0:2].unsqueeze(2), 0.0, None, ALU.mult).then_inc(sem["c_pads_set"], 1)
            dve.wait_ge(sem["mask_ready"], 1)

            def top(i):
                b = i // 16
                dve.wait_ge(sem["c_scores_summed"], i + 1)
                if i > 3:
                    dve.wait_ge(sem["c_exp_taken"], i - 3)
                dve.tensor_tensor_reduce(SMK[:, i % 4, :], PS[0:S, i % 3, 0:KV], MKB[:, b, :], -0.25, -2.0 * NEG,
                                             ALU.add, ALU.min, SM1[:, 0, i % 6:i % 6 + 1]).then_inc(sem["c_maximum_found"], 1)

            def over(i):
                dve.wait_ge(sem["c_exp_taken"], i + 1)
                dve.reciprocal(SM1[:, 2, i % 6:i % 6 + 1], SM1[:, 1, i % 6:i % 6 + 1]).then_inc(sem["c_sum_inverted"], 1)
                dve.wait_ge(sem["c_sum_inverted"], i + 1)
                if i == 0:
                    dve.wait_ge(sem["zeros_set"], 3)
                dve.tensor_scalar(PC[:, i % NPC, 0:KV], PC[:, i % NPC, 0:KV], SM1[:, 2, i % 6:i % 6 + 1], None,
                                      ALU.mult).then_inc(sem["c_probs_ready"], 1)

            def outs(b):
                dve.wait_ge(sem["c_heads_mixed"], 16 * (b + 1))
                for ti in range(KD):
                    ins = dve.tensor_scalar(OT1[:, ti, tok(b)], PS[:, 6, ti * S:(ti + 1) * S],
                                            COLS[:, 10 + ti:11 + ti], None, ALU.add)
                ins.then_inc(sem["c_mixed_copied"], 1)

            for i in range(16 * B + MIX + 1):
                if i >= 16 + MIX and (i - MIX) % 16 == 0:
                    outs((i - MIX) // 16 - 1)
                if 2 <= i < 16 * B + 2:
                    over(i - 2)
                if (i - 1) % 16 in PIECES[:2] and i // 16 + 1 < B:
                    keys_lo(i // 16 + 1, PIECES.index((i - 1) % 16))
                if i < 16 * B:
                    top(i)
                if i % 16 == 15 and i // 16 < HT1:
                    split_lo(0, i // 16)
            dve.wait_ge(sem["centroid_lengths_summed"], 1)
            dve.tensor_copy(CSQ, PS[0:S, 7, 0:8]).then_inc(sem["centroid_lengths_copied"], 1)
            dve.wait_ge(sem["centroid_lengths_copied"], 1)
            add_to_x("c_output_gated", "c_added_to_x")
            norm(5)
            mixture(1, TILES1)


def _rope_tables():
    freqs = (np.float32(1.0) / np.float32(THETA) ** (np.arange(0, ROPE, 2, dtype=np.float32) / np.float32(ROPE)))
    ang = np.outer(np.arange(S, dtype=np.float32), freqs.astype(np.float32)).astype(np.float32)
    tables = np.zeros((P, 2, S), np.float32)
    for p in range(P):
        r = p % 64 - NOPE
        if r < 0:
            tables[p, 0] = 1.0
        else:
            tables[p, 0] = np.cos(ang[:, r // 2])
            tables[p, 1] = np.sin(ang[:, r // 2]) * (-1.0 if r % 2 == 0 else 1.0)
    return tables


def kernel(**inputs):
    import concourse.bacc as _bacc
    from concourse.bass_utils import run_bass_kernel_spmd as _run

    a = {k: np.asarray(v) for k, v in inputs.items()}
    f = np.float32

    def rows(w):
        return np.ascontiguousarray(w.reshape(-1, P, w.shape[-1]).transpose(1, 0, 2))

    def col(v):
        return v.reshape(KD, P).T

    arrays = {}
    arrays["xT"] = rows(a["x"].reshape(T, D).T)
    arrays["ctxT"] = np.ascontiguousarray(a["ctx_1024"].transpose(2, 0, 1).reshape(KD, P, B, KV).transpose(1, 2, 0, 3))
    arrays["mask"] = np.ascontiguousarray(a["mask_Bx1x1xS2_bf1"].reshape(B * KV)).view(np.uint8)
    arrays["gates"] = np.ascontiguousarray(np.stack([a["g_xattn"][0], a["g_xattn"][1], a["g_ffn"][0], a["g_ffn"][1]]))
    arrays["ident"] = np.eye(P, dtype=f)
    arrays["avg"] = np.full((P, P), 1.0 / D, f)
    heads = np.zeros((P, TI0, H0), f)
    for ti in range(TI0):
        for p in range(P):
            heads[p, ti, 2 * ti + p // DH0] = 1.0
    arrays["headsum"] = heads.reshape(P, TI0 * H0)
    arrays["rope"] = _rope_tables()
    arrays["causal"] = np.triu(np.full((S, S), NEG, f), 1)
    arrays["parity"] = np.stack([(np.arange(P) // DH1 == 2 * (h % 4) + h // 4).astype(f) for h in range(8)], 1)
    arrays["rank"] = np.tile(np.arange(8, 0, -1, dtype=f), (S, 1))
    arrays["ones"] = np.ones((P, S), f)
    cols = np.zeros((P, 16), f)
    for at, name in ((0, "L0_ffn_w_ln1"), (2, "L0_ffn_w_ln2"), (4, "L0_xattn_bout"), (6, "L1_xattn_b_q"),
                     (8, "L1_xattn_b_k"), (10, "L1_xattn_b_v"), (12, "L1_xattn_b_o")):
        cols[:, at:at + 2] = col(a[name])
    cols[:, 15] = EPS
    arrays["cols"] = cols
    arrays["ebias"] = a["L0_ffn_expert_bias"]
    b2 = np.zeros((40, D), f)
    b2[0:8] = b2[32:40] = a["L1_ffn_b2"]
    arrays["b2"] = b2
    arrays["WQ0"] = rows(a["L0_xattn_Wq"])
    arrays["WKV0"] = rows(a["L0_xattn_Wkv"])
    arrays["WOUT0"] = rows(a["L0_xattn_Wout"])
    arrays["WQT"] = rows(a["L0_ffn_Wq"].T)
    wkvb = a["L0_ffn_Wkvb"].reshape(LAT, 16, NOPE)
    gkv = np.zeros((P, 8, P), f)
    bdv = np.zeros((P, 4, P), f)
    wo = np.zeros((P, 4, D), f)
    for h in range(16):
        lo = 64 * (h % 2)
        gkv[lo:lo + NOPE, h // 2, lo:lo + LAT] = wkvb[:, h, :].T
        gkv[lo + NOPE:lo + 64, h // 2, lo + LAT:lo + 64] = np.eye(ROPE, dtype=f)
        j = 32 * (h % 4)
        bdv[j:j + NOPE, h // 4, j:j + LAT] = wkvb[:, h, :].T
        wo[j:j + NOPE, h // 4, :] = a["L0_ffn_Wo"][64 * h:64 * h + NOPE]
    arrays["GKV"], arrays["BDV"], arrays["WO0"] = gkv, bdv, wo
    arrays["WKVA"] = rows(np.concatenate([a["L0_ffn_Wkva"]] * 2, 1))

    def experts(name, shared):
        w = np.concatenate([a[name], a[shared]], 0)
        return w

    arrays["WGU0"] = np.concatenate([rows(np.ascontiguousarray(experts(name, shared).transpose(1, 0, 2)).reshape(D, -1))
                                     for name, shared in (("L0_ffn_Wg", "L0_ffn_sWg"), ("L0_ffn_Wu", "L0_ffn_sWu"))], 1)
    arrays["WD0"] = np.ascontiguousarray(experts("L0_ffn_Wd", "L0_ffn_sWd").transpose(1, 0, 2))
    arrays["WGT0"] = rows(a["L0_ffn_Wgate"])
    arrays["W1A"] = np.ascontiguousarray(np.stack([rows(a["L1_xattn_" + n].T) for n in ("w_q", "w_k", "w_v", "w_o")], 1))
    bias1 = np.stack([a["L1_ffn_bg"], a["L1_ffn_b1"]]).reshape(2 * E1 * HT1, HW1)
    arrays["bias1"] = np.ascontiguousarray(bias1.T)
    arrays["centT"] = rows(a["L1_ffn_centroid"].T)
    arrays["WG1"] = np.ascontiguousarray(a["L1_ffn_Wg"].reshape(E1, KD, P, HID1).transpose(0, 2, 1, 3))
    arrays["WU1"] = np.ascontiguousarray(a["L1_ffn_W1"].reshape(E1, KD, P, HID1).transpose(0, 2, 1, 3))
    arrays["WD1"] = np.ascontiguousarray(a["L1_ffn_W2"].reshape(E1, HT1, HW1, D).transpose(0, 2, 1, 3))

    nc = _bacc.Bacc("TRN2", target_bir_lowering=False, num_devices=1)
    t = {}
    for name, v in arrays.items():
        arrays[name] = v = np.ascontiguousarray(v)
        t[name] = nc.dram_tensor(name, v.shape, mybir.dt.from_np(v.dtype), kind="ExternalInput").ap()
    t["outT"] = nc.dram_tensor("outT", (P, KD, T), F32, kind="ExternalOutput").ap()
    program(nc, t)
    r = _run(nc, [arrays], core_ids=[0])
    out = r.results[0]["outT"]
    return np.ascontiguousarray(out.transpose(1, 0, 2).reshape(D, B, S).transpose(1, 2, 0))
```

```python
from contextlib import ExitStack

import numpy as np

import concourse.bass as bass
from concourse import mybir

F32 = mybir.dt.float32
BF16 = mybir.dt.bfloat16
F32R = mybir.dt.float32r
U8 = mybir.dt.uint8
ALU = mybir.AluOpType
ACT = mybir.ActivationFunctionType
AX_X = mybir.AxisListType.X

B, S, D = 8, 100, 256
KV = 361
KVE = KV + KV % 2
T = B * S
P = 128
KD = D // P
HALF = T // 2
HB = HALF // S
H0, DH0 = 16, 64
TI0 = H0 * DH0 // P
NC = -(-KV // S)
NOPE = ROPE = LAT = 32
H1, DH1 = 16, 16
E0, I0 = 8, 128
E1, HID1 = 8, 684
NT1 = -(-E1 * HID1 // P)
CT1 = 5
CW1 = CT1 * P
NCH1 = -(-NT1 // CT1)
CH = 121
CHS = [CH, CH, KV - 2 * CH]
NEG = -1.0e30
EPS = 1e-5
THETA = 100000.0


def program(nc, t):
    with ExitStack() as ctx:
        base = {}

        def sb(name, shape, dt=F32):
            base[name] = -(-nc.sbuf_base // 32) * 32
            return ctx.enter_context(nc.sbuf_tensor(name, shape, dt))

        def part(name, shape, region, at):
            return nc.alloc_sbuf_tensor_at(name, shape, F32R, offset=base[region] + 4 * at)

        TURN, MIX = 4, 8
        NPC = TURN + 3
        X = sb("X", [P, KD, T])
        Y = sb("Y", [P, KD, T])
        XC = sb("XC", [P, KD, T])
        SQ = sb("SQ", [P, KD, T])
        STD = sb("STD", [P, 2, HALF])
        CTX = sb("CTX", [P, 3, KD, KVE])
        RQ = sb("RQ", [P, 6400])
        RO = sb("RO", [P, 6400])
        RW = sb("RW", [P, 12640])
        RB = sb("RB", [P, 11400])
        WK = sb("WK", [P, 6, 400])
        IDN = sb("IDN", [P, P])
        AVG = sb("AVG", [P, P])
        HS = sb("HS", [P, TI0 * H0])
        CS = sb("CS", [P, 2, S])
        CM = sb("CM", [S, S])
        PAR = sb("PAR", [P, 8])
        RANK = sb("RANK", [S, 8])
        ONES = sb("ONES", [P, S])
        COLS = sb("COLS", [P, 16])
        G4 = sb("G4", [P, 4])
        TG = sb("TG", [P, 4])
        GB = sb("GB", [P, 4])
        SM0 = sb("SM0", [H0, 6, S])
        RT = sb("RT", [S, 14, B * 8])
        RTC = sb("RTC", [S, 8, B])
        EB = sb("EB", [S, 8])
        UNIT = sb("UNIT", [40, 8], F32R)
        B2E = sb("B2E", [40, D])
        SM1 = sb("SM1", [S, 3, 6])
        PS = ctx.enter_context(nc.psum_tensor("PS", [P, 8, 512], F32))

        def cut(region, at, n, parts=P):
            return region[0:parts, at:at + n]

        WQ0 = cut(RW, 0, 2048).rearrange("p (k c) -> p k c", k=KD)
        WKV0 = cut(RW, 2048, 4096).rearrange("p (k c) -> p k c", k=KD)
        WOUT0 = cut(RW, 6144, 2048).rearrange("p (t c) -> p t c", t=TI0)
        PROD = cut(RW, 8192, 1200).rearrange("p (s c) -> p s c", s=3)
        VSB = cut(RW, 9392, 1200).rearrange("p (s c) -> p s c", s=3)
        PV = cut(RW, 10592, 800).rearrange("p (s c) -> p s c", s=2)
        SE = cut(RW, 11392, 1200, H0).rearrange("p (s c) -> p s c", s=3)
        SPREAD = part("SPREAD", [32 + H0, TI0, P], "SQ", 0)
        WKV0H = part("WKV0H", [P, KD, 2 * TI0 * P], "RB", 6912)
        WKV0L = part("WKV0L", [P, KD, 2 * TI0 * P], "RW", 2048)
        CTXH = part("CTXH", [P, 3, KD, KVE], "WK", 0)
        CTXL = part("CTXL", [P, 3, KD, KVE], "CTX", 0)
        OTH = part("OTH", [P, TI0, T], "RQ", 0)
        OTL = part("OTL", [P, TI0, T], "RO", 0)
        WOUT0H = part("WOUT0H", [P, TI0, D], "RW", 0)
        WOUT0L = part("WOUT0L", [P, TI0, D], "RW", 6144)
        PRODH = part("PRODH", [P, 4, HALF], "XC", 0)
        PRODL = part("PRODL", [P, 4, HALF], "Y", 0)
        HSR = part("HSR", [P, TI0 * H0], "RB", 3328 + 4 * HALF)
        SES = part("SES", [32 + H0, 2, HALF], "RB", 3328)
        QT0 = cut(RQ, 0, TI0 * T).rearrange("p (t c) -> p t c", t=TI0)
        OT0 = cut(RO, 0, TI0 * T).rearrange("p (t c) -> p t c", t=TI0)
        WQT = cut(RB, 0, 2048).rearrange("p (t c) -> p t c", t=8)
        GKV = cut(RB, 2048, 1024).rearrange("p (t c) -> p t c", t=8)
        WKVA = cut(RB, 3072, 256).rearrange("p (k c) -> p k c", k=KD)
        WQA = cut(RB, 3328, 2048).rearrange("p (k c) -> p k c", k=KD)
        BDV = cut(RB, 5376, 512).rearrange("p (t c) -> p t c", t=4)
        WO0 = cut(RB, 5888, 1024).rearrange("p (t c) -> p t c", t=4)
        WOA = cut(RB, 6912, 1024).rearrange("p (t c) -> p t c", t=4)
        CK = cut(RB, 7936, 800)
        CK2 = cut(RB, 8736, 800)
        CKM = cut(RB, 0, 1600).rearrange("p (a c) -> p a c", a=2)
        CMB = cut(RB, 1600, S // 2, S).bitcast(BF16)
        IDNB = cut(RB, 1600 + S // 2, S // 2, S).bitcast(BF16)
        PT0 = cut(RB, 9536, 1600, S).rearrange("p (s c) -> p s c", s=2)
        LT = cut(RB, 11136, 256, S).rearrange("p (b c) -> p b c", b=B)
        QP = QT0
        UT = cut(RO, 0, 3200).rearrange("p (t c) -> p t c", t=4)
        SMB = cut(RO, 3200, 800, S).rearrange("p (s c) -> p s c", s=2)
        PB = cut(RO, 4000, 2400, S).rearrange("p (s c) -> p s c", s=3)
        WGU0 = cut(RW, 0, 4608).rearrange("p (w c) -> p w c", w=2 * KD)
        WD0 = cut(RW, 4608, 2304).rearrange("p (t c) -> p t c", t=E0 + 1)
        WGU0L = part("WGU0L", [P, 2 * KD, (E0 + 1) * I0], "RW", 0)
        WD0L = part("WD0L", [P, E0 + 1, D], "RW", 4608)
        WGU0H = part("WGU0H", [P, 2 * KD, (E0 + 1) * I0], "RB", 4480)
        WD0H = part("WD0H", [P, E0 + 1, D], "RB", 9088)
        XH = part("XH", [P, KD, T], "RO", 0)
        XL = part("XL", [P, KD, T], "RO", KD * T)
        HTH = part("HTH", [P, 3, HALF], "RO", 2 * KD * T)
        HTL = part("HTL", [P, 3, HALF], "RO", 2 * KD * T + 3 * HALF)
        WTS = part("WTS", [40, T], "SQ", 0)
        WGT0 = cut(RW, 6912, 16).rearrange("p (k c) -> p k c", k=KD)
        W1A = cut(RW, 6928, 2048).rearrange("p (w k c) -> p w k c", w=4, k=KD)
        MK8 = cut(RW, 8976, 722, S)
        MKB = cut(RW, 9698, 2888, S).rearrange("p (b c) -> p b c", b=B)
        QCH = part("QCH", [P, KD, T], "RQ", 0)
        QCL = part("QCL", [P, KD, T], "RQ", KD * T)
        VP = cut(RQ, 3200, 3072, CH).rearrange("p (s a c d) -> p s a c d", s=2, a=2, c=3)
        KTH = [part("KTH0", [P, KD, KVE], "WK", 4 * HALF), part("KTH1", [P, KD, KVE], "XC", 0)]
        KTL = part("KTL", [P, 2, KD, KVE], "RW", 4480)
        QXH = part("QXH", [P, 2, KD, 8, S], "RO", 0)
        QXL = part("QXL", [P, 2, KD, 8, S], "RO", 3200)
        SMK = SQ[:, :, :].rearrange("p k c -> p (k c)")[0:S, 0:4 * KV].rearrange("p (s c) -> p s c", s=4)
        OT1 = Y
        PC = cut(RB, 8544, NPC * 3 * CH, S).rearrange("p (s c) -> p s c", s=NPC)
        PTC = WK[0:CH, 0:4, 0:3 * S]
        WEB = cut(RQ, 0, E1 * T).rearrange("p (e c) -> p e c", e=E1)
        CHUNK = 4 * CW1 + CT1 * D
        RING = RB[:, 0:2 * CHUNK].rearrange("p (s c) -> p s c", s=2)
        BIAS1 = cut(RW, 0, 2 * NCH1 * CT1)
        WEX = [cut(RW, 192 + 2 * CHUNK + j * T, T) for j in range(5)] + [Y[:, j, :] for j in range(2)]
        UNITX_IN = cut(RB, 8544, (E1 - 1) * P, 40)
        UNITX = part("UNITX", [40, (E1 - 1) * P], "RB", 8544 + (E1 - 1) * P)
        CENT = cut(RW, 96, 16).rearrange("p (k c) -> p k c", k=KD)
        CENT2 = cut(RW, 112, 16).rearrange("p (k c) -> p k c", k=KD)
        CSQ = cut(RW, 144, 8, S)
        CENTSQ = cut(RW, 128, 16).rearrange("p (k c) -> p k c", k=KD)
        RINGH = part("RINGH", [P, 2, CHUNK], "RW", 192)
        RINGL = part("RINGL", [P, 2, CHUNK], "RB", 0)
        B2H = part("B2H", [40, D], "RO", 5600)
        B2L = part("B2L", [40, D], "RO", 5600 + D)
        RTH = part("RTH", [S, B * 8], "RT", 11 * B * 8)
        RTX = RT[:, 6:11, :].rearrange("p a c -> p (a c)").rearrange("p (b c) -> p b c", c=40)
        SIL = WK[:, 0:3, :]
        HT = WK[:, 3:6, :]
        QS = WK[:, 0:3, :]
        SH = WK[:, 3:6, :]

        names = """x_loaded0 x_loaded1 averages_loaded constants_loaded vectors_loaded a_wq_loaded a_wkv_loaded
            a_wout_loaded context_loaded0 context_loaded1 context_loaded2 b_weights_loaded
            moe0_weights_loaded c_weights_loaded mask_loaded moe1_small_loaded shared_rows_loaded
            chunk_loaded0 chunk_loaded1 out_stored zeros_set pads_set a_head_rows_rounded
            psum_tails_set a_spread_rows_built dve_step_done gates_ready gated_biases_ready
            norm_mean_summed norm_centred norm_squared norm_variance_summed norm_log_taken
            norm_rstd_ready norm_done a_query_summed a_query_copied a_weights_high_ready
            a_weights_low_ready a_context_high_ready a_context_low_ready a_probs_high_ready
            a_probs_low_ready a_products_high_ready a_products_low_ready a_keys_summed
            a_products_ready a_similarity_summed a_shifted a_exp_taken a_weights_ready
            a_weights_spread a_values_summed a_values_copied a_weighted a_heads_mixed
            a_output_weights_high_ready a_output_weights_low_ready a_heads_high_ready
            a_heads_low_ready a_last_heads_low_ready a_output_summed a_output_gated a_added_to_x
            b_weights_folded b_folded_copied b_latent_summed b_latent_rotated b_latent_copied
            b_latent_rows_summed b_latent_rows_copied b_zero_keys_set b_mask_rounded b_query_summed
            b_query_copied b_query_read b_query_cosines b_query_rotated b_scores_summed
            b_maxima_found b_scores_shifted b_exp_taken b_sums_inverted b_probs_ready
            b_second_probs_ready b_probs_turned b_turned_copied b_heads_mixed b_mixed_copied
            b_output_summed b_added_to_y router_scores_summed router_scores_shifted
            router_function_taken router_weights_ready router_weights_turned router_turned_copied
            router_high_ready router_weights_spread router_spread_copied router_spread_copied_odd
            router_squares_ready centroid_lengths_summed centroid_lengths_copied unit_rows_ready
            shared_rows_rounded output_bias_high_ready output_bias_low_ready gate_summed up_summed
            gate_activated hidden_ready hidden_weighed hidden_high_ready hidden_low_ready
            down_summed moe_added_to_x x_high_ready x_low_ready expert_weights_high_ready
            expert_weights_low_ready c_query_summed c_query_copied c_query_split c_pads_set
            c_keys_summed c_keys_copied c_keys_low_ready c_query_low_ready c_values_summed
            c_values_copied c_scores_summed c_maximum_found c_exp_taken c_sum_inverted c_probs_ready
            c_probs_turned c_turned_copied c_heads_mixed c_mixed_copied c_output_summed
            c_output_gated c_added_to_x mask_ready""".split()
        sem = {n: ctx.enter_context(nc.semaphore(n)) for n in names}

        def half(n):
            return slice(n * HALF, (n + 1) * HALF)

        def tok(b):
            return slice(b * S, (b + 1) * S)

        NORM = [(X, XC, "layer"), (X, Y, "layer"), (Y, XC, 0), (Y, XC, 2), (X, XC, "layer"), (X, XC, "layer")]
        LAYER = {0: 0, 1: 1, 4: 2, 5: 3}
        SOURCE = [("", lambda n: 0), ("a_added_to_x", lambda n: 2 * n + 2), ("norm_done", lambda n: 2 + n + 1),
                  ("b_added_to_y",
                   lambda n: 2 * n + 2), ("moe_added_to_x", lambda n: 2 * n + 2), ("c_added_to_x", lambda n: 2 * n + 2)]

        TILES0 = [(e, 0) for e in range(E0 + 1)]
        TILES1 = [divmod(i, CT1) for i in range(NT1)]
        N0, N1 = 2 * len(TILES0), 2 * len(TILES1)
        ROUTED0 = 2 * E0

        def ring(e):
            return parts_of(RING[:, e % 2, :])

        def parts_of(r):
            return (r[:, 0:2 * CW1].rearrange("p (k c) -> p k c", k=KD),
                    r[:, 2 * CW1:4 * CW1].rearrange("p (k c) -> p k c", k=KD),
                    r[:, 4 * CW1:CHUNK].rearrange("p (m c) -> p m c", m=CT1))

        def weights_of(which, tile):
            if which == 0:
                return WEB[:, tile, :]
            e = tile * P // HID1
            last = min((tile + 1) * P, E1 * HID1) - 1
            return WEB[:, e, :] if last // HID1 == e else WEX[e]

        def spreads(which):
            both = []
            for e in range(E1):
                both.append((UNIT[:, e:e + 1].to_broadcast([40, P]), WEB[:, e, :]))
                if which and e + 1 < E1:
                    both.append((UNITX[:, e * P:(e + 1) * P], WEX[e]))
            return both

        SPREADS = [E1, 2 * E1 - 1]

        def tile_of0(part_, e, down):
            gu, d = {"raw": (WGU0, WD0), "high": (WGU0H, WD0H), "low": (WGU0L, WD0L)}[part_]
            return d[:, e, :] if down else gu[:, :, e * I0:(e + 1) * I0]

        def tile_of(r, m, down):
            if down:
                return parts_of(r)[2][:, m, :]
            return r[:, 0:4 * CW1].rearrange("p (w c) -> p w c", w=4)[:, :, m * P:(m + 1) * P]

        W_PIECES = [9, 11, 13, 15]

        LAG0 = 3

        def key_bank(b, m):
            return 6 if b == 0 and m == 1 else 7

        def w_piece(w, i):
            return w[:, :, i * (TI0 // 2) * P:(i + 1) * (TI0 // 2) * P]

        SPLIT = CT1

        HEADS1 = [(ti, par, j) for ti in range(KD) for par in range(2) for j in range(4)]

        PARTS = [0, 1, 5, 6, 9, 10, 13]
        PIECES = [2, 7, 11, 14]

        block = ctx.enter_context(nc.Block())

        @block.sync
        def _(sp):
            def load(dst, src, name):
                sp.dma_start(dst, src).then_inc(sem[name], 16)

            load(AVG[:, :], t["avg"], "averages_loaded")
            for n in range(2):
                load(X[:, :, half(n)], t["xT"][:, :, half(n)], f"x_loaded{n}")
            load(COLS[:, :], t["cols"], "vectors_loaded")
            load(G4[:, :], t["gates"].partition_broadcast(P), "vectors_loaded")
            load(EB[:, :], t["ebias"].partition_broadcast(S), "vectors_loaded")
            load(B2E[:, :], t["b2"], "vectors_loaded")
            for dst, name in ((IDN, "ident"), (HS, "headsum"), (CS, "rope"), (CM, "causal"),
                              (PAR, "parity"), (RANK, "rank"), (ONES, "ones")):
                load(dst[:, :] if len(dst.shape) == 2 else dst[:, :, :], t[name], "constants_loaded")
            load(WQ0, t["WQ0"], "a_wq_loaded")

            def load_ctx(i):
                b = i % B
                if i >= 3:
                    j = i - 3
                    if j < B:
                        sp.wait_ge(sem["a_values_summed"], TI0 * (j + 1))
                    else:
                        sp.wait_ge(sem["c_values_summed"], 2 * (j - B + 1))
                load(CTX[:, i % 3, :, 0:KV], t["ctxT"][:, b, :, :], f"context_loaded{i % 3}")

            load_ctx(0)
            load(WKV0, t["WKV0"], "a_wkv_loaded")
            load_ctx(1)
            load_ctx(2)
            load(WOUT0, t["WOUT0"], "a_wout_loaded")
            for dst, name in ((WQT, "WQT"), (GKV, "GKV"), (WKVA, "WKVA"), (BDV, "BDV"), (WO0, "WO0")):
                load(dst, t[name], "b_weights_loaded")
            for b in range(3, B):
                load_ctx(b)
            sp.wait_ge(sem["a_output_summed"], 4)
            sp.wait_ge(sem["a_heads_mixed"], TI0 * B)
            for dst, name in ((WGU0, "WGU0"), (WD0, "WD0"), (WGT0, "WGT0")):
                load(dst, t[name], "moe0_weights_loaded")
            load(W1A, t["W1A"], "c_weights_loaded")
            load(MK8.bitcast(U8), t["mask"].partition_broadcast(S), "mask_loaded")
            for i in range(B, B + 3):
                load_ctx(i)

            def load_chunk(e):
                g, u, d = ring(e)
                if e >= 2:
                    sp.wait_ge(sem["down_summed"], N0 + 2 * CT1 * (e - 1))
                load(g, t["WG1"][e], f"chunk_loaded{e % 2}")
                load(u, t["WU1"][e], f"chunk_loaded{e % 2}")
                load(d, t["WD1"][e], f"chunk_loaded{e % 2}")

            sp.wait_ge(sem["b_output_summed"], 4)
            sp.wait_ge(sem["b_mixed_copied"], 2 * B)
            load_chunk(0)
            for i in range(B + 3, 2 * B):
                load_ctx(i)
            sp.wait_ge(sem["moe_added_to_x"], 4)
            load_chunk(1)
            load(BIAS1, t["bias1"], "moe1_small_loaded")
            load(CENT, t["centT"], "moe1_small_loaded")
            sp.wait_ge(sem["c_heads_mixed"], 16 * B)
            load(UNITX_IN, t["shared"], "shared_rows_loaded")
            for e in range(2, NCH1):
                load_chunk(e)
            for n in range(2):
                sp.wait_ge(sem["moe_added_to_x"], 4 + 2 * (n + 1))
                sp.dma_start(t["outT"][:, :, half(n)], X[:, :, half(n)]).then_inc(sem["out_stored"], 16)
            sp.wait_ge(sem["out_stored"], 32)

        @block.tensor
        def _(pe):
            def mm(out, lhsT, rhs, start, stop):
                return pe.matmul(out, lhsT, rhs, start=start, stop=stop)

            def norm(i):
                src, _, kind = NORM[i]
                for n in range(2):
                    if kind == "layer":
                        if i == 0:
                            pe.wait_ge(sem[f"x_loaded{n}"], 16)
                        else:
                            pe.wait_ge(sem[SOURCE[i][0]], SOURCE[i][1](n))
                        for k in range(KD):
                            m = mm(PS[:, 4 + n, 0:HALF], AVG[:, :], src[:, k, half(n)], k == 0, k == KD - 1)
                        m.then_inc(sem["norm_mean_summed"], 1)
                for n in range(2):
                    pe.wait_ge(sem["norm_squared"], 2 * i + n + 1)
                    for k in range(KD):
                        m = mm(PS[:, 4 + n, 0:HALF], AVG[:, :], SQ[:, k, half(n)], k == 0, k == KD - 1)
                    m.then_inc(sem["norm_variance_summed"], 1)

            pe.wait_ge(sem["averages_loaded"], 16)
            norm(0)
            pe.wait_ge(sem["a_wq_loaded"], 16)
            for i in range(2 * TI0):
                ti, n = divmod(i, 2)
                pe.wait_ge(sem["norm_done"], n + 1)
                if i > 1:
                    pe.wait_ge(sem["a_query_copied"], i - 1)
                for k in range(KD):
                    m = mm(PS[:, 4 + i % 2, 0:HALF], WQ0[:, k, ti * P:(ti + 1) * P], XC[:, k, half(n)], k == 0, k == 1)
                m.then_inc(sem["a_query_summed"], 1)
            pe.wait_ge(sem["a_query_copied"], 2 * TI0)
            pe.wait_ge(sem["psum_tails_set"], 1)
            pe.wait_ge(sem["a_head_rows_rounded"], 1)

            def sim(b, ti):
                i = TI0 * b + ti
                pe.wait_ge(sem["a_products_low_ready"], i + 1)
                if b > 1:
                    pe.wait_ge(sem["a_shifted"], b - 1)
                pe.wait_ge(sem["pads_set"], 4)
                out, heads = PS[0:H0, 2 + b % 2, 0:KVE], HSR[:, ti * H0:(ti + 1) * H0]
                mm(out, heads, PRODH[:, i % 4, 0:KVE], ti == 0, False)
                mm(out, heads, PRODL[:, i % 4, 0:KVE], False, ti == TI0 - 1).then_inc(sem["a_similarity_summed"], 1)

            def project_a(out, b, tile):
                cols = slice(tile * P, (tile + 1) * P)
                for k in range(KD):
                    mm(out, WKV0H[:, k, cols], CTXH[:, b % 3, k, :], k == 0, False)
                    mm(out, WKV0H[:, k, cols], CTXL[:, b % 3, k, :], False, False)
                    m = mm(out, WKV0L[:, k, cols], CTXH[:, b % 3, k, :], False, k == 1)
                return m

            def keys(b):
                pe.wait_ge(sem["a_context_low_ready"], b + 1)
                for ti in range(TI0):
                    i = TI0 * b + ti
                    if i > 1:
                        pe.wait_ge(sem["a_products_ready"], i - 1)
                    pe.wait_ge(sem["a_weights_low_ready"], 1 + ti // 4)
                    pe.wait_ge(sem["pads_set"], 3)
                    project_a(PS[:, i % 2, 0:KVE], b, ti).then_inc(sem["a_keys_summed"], 1)
                    if ti >= LAG0:
                        sim(b, ti - LAG0)

            def values(b):
                pe.wait_ge(sem["a_spread_rows_built"], 3)
                pe.wait_ge(sem["a_weights_low_ready"], 4)
                for ti in range(TI0):
                    i = TI0 * b + ti
                    if i > 1:
                        pe.wait_ge(sem["a_values_copied"], i - 1)
                    project_a(PS[:, 4 + i % 2, 0:KVE], b, TI0 + ti).then_inc(sem["a_values_summed"], 1)
                    if ti < LAG0 and b + 1 < B:
                        sim(b + 1, TI0 - LAG0 + ti)
                    pe.wait_ge(sem["a_probs_low_ready"], b + 1)
                    if i > 1:
                        pe.wait_ge(sem["a_weighted"], i - 1)
                    mm(PS[:, 6 + i % 2, 0:KVE], SPREAD[:, ti, :], SES[:, b % 2, 0:KVE], True,
                       True).then_inc(sem["a_weights_spread"], 1)

            def project_out_a(n, mo):
                pe.wait_ge(sem["a_output_weights_low_ready"], 2)
                pe.wait_ge(sem["a_heads_low_ready"], (HB, B - 1)[n])
                if n:
                    pe.wait_ge(sem["a_last_heads_low_ready"], 1)
                pe.wait_ge(sem["a_products_ready"], TI0 * B)
                out, cols = PS[:, 2 * n + mo, 0:HALF], slice(mo * P, (mo + 1) * P)
                for ti in range(TI0):
                    mm(out, WOUT0H[:, ti, cols], OTH[:, ti, half(n)], ti == 0, False)
                    mm(out, WOUT0H[:, ti, cols], OTL[:, ti, half(n)], False, False)
                    m = mm(out, WOUT0L[:, ti, cols], OTH[:, ti, half(n)], False, ti == TI0 - 1)
                m.then_inc(sem["a_output_summed"], 1)

            for b in range(B):
                keys(b)
                if b:
                    values(b - 1)
                else:
                    for ti in range(TI0 - LAG0, TI0):
                        sim(0, ti)
            project_out_a(0, 0)
            values(B - 1)
            project_out_a(0, 1)
            project_out_a(1, 0)
            project_out_a(1, 1)

            pe.wait_ge(sem["b_weights_loaded"], 16 * 5)
            for i in range(4):
                if i > 1:
                    pe.wait_ge(sem["b_folded_copied"], i - 1)
                for ti in range(4):
                    c = i // 2
                    tq = 4 * (i % 2) + ti
                    m = mm(PS[:, 6 + i % 2, ti * P:(ti + 1) * P], WQT[:, tq, c * P:(c + 1) * P], GKV[:, tq, :], True,
                           True)
                m.then_inc(sem["b_weights_folded"], 1)
            for i in range(2):
                pe.wait_ge(sem["b_folded_copied"], i + 3)
                for j in range(2):
                    m = mm(PS[:, 6 + i, j * D:(j + 1) * D], BDV[:, 2 * i + j, :], WO0[:, 2 * i + j, :], True, True)
                m.then_inc(sem["b_weights_folded"], 1)
            norm(1)
            norm(2)
            for n in range(2):
                pe.wait_ge(sem["norm_done"], 4 + n + 1)
                pe.wait_ge(sem["a_output_gated"], 4)
                for k in range(KD):
                    m = mm(PS[:, n, 0:HALF], WKVA[:, k, :], XC[:, k, half(n)], k == 0, k == 1)
                m.then_inc(sem["b_latent_summed"], 1)
            for b in range(B):
                for k in range(KD):
                    m = mm(PS[0:S, 2, b * LAT:(b + 1) * LAT], XC[:, k, tok(b)], WKVA[:, k, 0:LAT], k == 0, k == 1)
            m.then_inc(sem["b_latent_rows_summed"], 1)
            pe.wait_ge(sem["b_folded_copied"], 6)
            for i in range(16):
                n, tq = divmod(i, 8)
                if i > 3:
                    pe.wait_ge(sem["b_query_copied"], i - 3)
                for k in range(KD):
                    m = mm(PS[:, 4 + i % 4, 0:HALF], WQA[:, k, tq * P:(tq + 1) * P], XC[:, k, half(n)], k == 0, k == 1)
                m.then_inc(sem["b_query_summed"], 1)

            def qk(i):
                b, g = divmod(i, 2)
                if i == 0:
                    pe.wait_ge(sem["b_latent_rows_copied"], 1)
                    pe.wait_ge(sem["b_zero_keys_set"], 2)
                    pe.wait_ge(sem["b_latent_rotated"], 4)
                    pe.wait_ge(sem["b_mask_rounded"], 2)
                    pe.wait_ge(sem["b_query_rotated"], 16)
                if i > 1:
                    pe.wait_ge(sem["b_scores_shifted"], i - 1)
                if i > 1:
                    pe.wait_ge(sem["b_exp_taken"], i - 1)
                for par in range(2):
                    bank = 2 * (i % 2) + par
                    mm(PS[0:S, bank, 0:4 * S], IDNB, CMB.unsqueeze(1).to_broadcast([S, 4, S]), True, False)
                    for x in range(4):
                        m = mm(PS[0:S, bank, x * S:(x + 1) * S], QP[:, 4 * g + x, tok(b)], CKM[:, par, tok(b)],
                               False, x == 3)
                m.then_inc(sem["b_scores_summed"], 1)

            def turn(i):
                for q in range(2):
                    pe.wait_ge(sem[("b_probs_ready", "b_second_probs_ready")[q]], i + 1)
                    if 2 * i + q > 1:
                        pe.wait_ge(sem["b_turned_copied"], 2 * i + q - 1)
                    for x in range(4):
                        m = pe.transpose(PS[0:S, 4 + q, x * S:(x + 1) * S],
                                         PB[:, i % 3, (4 * q + x) * S:(4 * q + x + 1) * S],
                                         IDN[0:S, 0:S])
                    m.then_inc(sem["b_probs_turned"], 1)

            def mix(i):
                b, g = divmod(i, 2)
                pe.wait_ge(sem["b_turned_copied"], 2 * i + 2)
                if i > 1:
                    pe.wait_ge(sem["b_mixed_copied"], i - 1)
                for j in range(4):
                    at = (4 * (j % 2) + j // 2) * S
                    rhs = PT0[:, i % 2, at:at + 3 * S].rearrange("p (x c) -> p x c", c=S)[:, 0:3:2, :]
                    m = mm(PS[32 * j:32 * j + 32, 6 + i % 2, 0:2 * S], LT[:, b, :], rhs, True, True)
                m.then_inc(sem["b_heads_mixed"], 1)

            for i in range(2 * B + 4):
                if i < 2 * B:
                    qk(i)
                if 3 <= i < 2 * B + 3:
                    turn(i - 3)
                if i >= 4:
                    mix(i - 4)
            pe.wait_ge(sem["b_mixed_copied"], 2 * B)
            for n in range(2):
                for mo in range(KD):
                    for ti in range(4):
                        m = mm(PS[:, 2 * n + mo, 0:HALF], WOA[:, ti, mo * P:(mo + 1) * P], UT[:, ti, half(n)],
                               ti == 0, ti == 3)
                    m.then_inc(sem["b_output_summed"], 1)
            norm(3)

            def mixture(which, tiles):
                first = (0, N0)[which]
                before = (0, 2 * len(TILES0))[which]
                count = 2 * len(tiles)
                for b in range(B):
                    pe.wait_ge(sem["norm_done"], (7, 11)[which] + b // HB)
                    if which:
                        pe.wait_ge(sem["router_squares_ready"], 3 + b // HB)
                    out = PS[0:S, 0, b * 8:(b + 1) * 8]
                    if which == 0:
                        pe.wait_ge(sem["moe0_weights_loaded"], 48)
                        pairs = [(XC[:, k, tok(b)], WGT0[:, k, :]) for k in range(KD)]
                    else:
                        pairs = [(XC[:, k, tok(b)], CENT2[:, k, :]) for k in range(KD)]
                        pairs += [(SQ[:, k, tok(b)], ONES[:, 0:8]) for k in range(KD)]
                    for c, (lhsT, rhs) in enumerate(pairs):
                        m = mm(out, lhsT, rhs, c == 0, c == len(pairs) - 1)
                m.then_inc(sem["router_scores_summed"], 1)

                def parts(i):
                    e, m_ = tiles[i // 2]
                    if which == 0:
                        gu = [tile_of0(part_, e, 0) for part_ in ("high", "low")]
                        d = [tile_of0(part_, e, 1) for part_ in ("high", "low")]
                    else:
                        gu = [tile_of(slots[:, e % 2, :], m_, 0) for slots in (RINGH, RINGL)]
                        d = [tile_of(slots[:, e % 2, :], m_, 1) for slots in (RINGH, RINGL)]
                    return gu, d

                def up(i):
                    n = i % 2
                    hi, lo = parts(i)[0]
                    pe.wait_ge(sem["expert_weights_low_ready"], before + 2 * (i // 2) + 1)
                    pe.wait_ge(sem["x_low_ready"], 2 * which + n + 1)
                    if first + i > 1:
                        pe.wait_ge(sem["hidden_ready"], first + i - 1)
                    for c, name in enumerate(("gate_summed", "up_summed")):
                        out = PS[:, 4 + c + 2 * (i % 2), 0:HALF]
                        for k in range(KD):
                            mm(out, hi[:, KD * c + k, :], XH[:, k, half(n)], k == 0, False)
                            mm(out, hi[:, KD * c + k, :], XL[:, k, half(n)], False, False)
                            m = mm(out, lo[:, KD * c + k, :], XH[:, k, half(n)], False, k == 1)
                        m.then_inc(sem[name], 1)

                def down(i):
                    n = i % 2
                    hi, lo = parts(i)[1]
                    pe.wait_ge(sem["expert_weights_low_ready"], before + 2 * (i // 2) + 2)
                    pe.wait_ge(sem["hidden_low_ready"], first + i + 1)
                    for mo in range(KD):
                        out, cols = PS[:, 2 * n + mo, 0:HALF], slice(mo * P, (mo + 1) * P)
                        mm(out, hi[:, cols], HTH[:, i % 3, :], which == 0 and i < 2, False)
                        mm(out, hi[:, cols], HTL[:, i % 3, :], False, False)
                        m = mm(out, lo[:, cols], HTH[:, i % 3, :], False, i >= count - 2)
                    m.then_inc(sem["down_summed"], 1)

                up(0)
                up(1)
                pe.wait_ge(sem["router_weights_ready"], 2 * which + 2)
                pe.wait_ge(sem["unit_rows_ready"], 3)
                for q in range(2):
                    for b in range(4):
                        bb = 4 * q + b
                        m = pe.transpose(PS[0:40, 1 + q, b * S:(b + 1) * S], RTX[:, bb, :], IDN[0:S, 0:S])
                    m.then_inc(sem["router_weights_turned"], 1)
                pe.wait_ge(sem["unit_rows_ready"], 3)
                if which:
                    pe.wait_ge(sem["shared_rows_rounded"], 1)
                for i in range(2 * SPREADS[which]):
                    n = i % 2
                    pe.wait_ge(sem["router_turned_copied"], 2 * which + n + 1)
                    if i >= 4:
                        if SPREADS[0] * which + i // 2 > 1:
                            pe.wait_ge(sem[("router_spread_copied", "router_spread_copied_odd")[i % 2]],
                                       SPREADS[0] * which + i // 2 - 1)
                    mm(PS[:, i % 4, 0:HALF], spreads(which)[i // 2][0], WTS[:, half(n)], True,
                       True).then_inc(sem["router_weights_spread"], 1)
                for i in range(2, count + 2):
                    if i < count:
                        up(i)
                    if i == 2:
                        pe.wait_ge(sem["router_spread_copied"], SPREADS[0] * which + SPREADS[which])
                        pe.wait_ge(sem["router_spread_copied_odd"], SPREADS[0] * which + SPREADS[which])
                        if which:
                            pe.wait_ge(sem["output_bias_low_ready"], 1)
                            for n in range(2):
                                for mo in range(KD):
                                    out, cols = PS[:, 2 * n + mo, 0:HALF], slice(mo * P, (mo + 1) * P)
                                    mm(out, B2H[:, cols], WTS[:, half(n)], True, False)
                                    mm(out, B2L[:, cols], WTS[:, half(n)], False, False)
                    down(i - 2)

            def project(b, part_):
                ci = B + b
                if part_ == 0:
                    pe.wait_ge(sem[f"context_loaded{ci % 3}"], 16 * (ci // 3 + 1))
                    if b:
                        pe.wait_ge(sem["c_values_copied"], 4 * b)
                if part_ < 4:
                    m_, k = divmod(part_, KD)
                    if b:
                        pe.wait_ge(sem["c_keys_low_ready"], 2 * b + m_)
                    m = mm(PS[:, key_bank(b, m_), 0:KV], W1A[:, 1, k, m_ * P:(m_ + 1) * P], CTX[:, ci % 3, k, 0:KV],
                           k == 0, k == 1)
                    if k == 1:
                        m.then_inc(sem["c_keys_summed"], 1)
                    return
                c = part_ - 4
                pe.wait_ge(sem["c_keys_low_ready"], 2 * b + 2)
                if c == 2:
                    pe.wait_ge(sem["c_values_copied"], 4 * b + 2)
                at = (c % 2) * D
                for k in range(KD):
                    m = mm(PS[0:CHS[c], 7, at:at + D], CTX[:, ci % 3, k, c * CH:c * CH + CHS[c]], W1A[:, 2, k, :],
                           k == 0, k == 1)
                if c:
                    m.then_inc(sem["c_values_summed"], 1)

            pe.wait_ge(sem["b_added_to_y"], 4)
            mixture(0, TILES0)

            pe.wait_ge(sem["c_weights_loaded"], 16)
            for part_ in range(2 * KD):
                project(0, part_)
            norm(4)
            for i in range(4):
                n, mo = divmod(i, 2)
                pe.wait_ge(sem["norm_done"], 8 + n + 1)
                pe.wait_ge(sem["moe_added_to_x"], 4)
                for k in range(KD):
                    m = mm(PS[:, i, 0:HALF], W1A[:, 0, k, mo * P:(mo + 1) * P], XC[:, k, half(n)], k == 0, k == 1)
                m.then_inc(sem["c_query_summed"], 1)

            for part_ in range(2 * KD, 2 * KD + 3):
                project(0, part_)

            def scores(i):
                b, h = i // 16, i % 16
                if h == 0:
                    pe.wait_ge(sem["c_pads_set"], 3)
                    pe.wait_ge(sem["c_keys_low_ready"], 2 * b + 2)
                if h % 8 == 0:
                    pe.wait_ge(sem["c_query_split"], 2 * KD * b + h // 4 + 2)
                if i > 2:
                    pe.wait_ge(sem["c_maximum_found"], i - 2)
                out, ti = PS[0:S, i % 3, 0:KVE], h // 8
                q = [a[:, b % 2, ti, h % 8, :] for a in (QXH, QXL)]
                k = [KTH[b % 2][:, ti, :], KTL[:, b % 2, ti, :]]
                mm(out, q[0], k[0], True, False)
                mm(out, q[0], k[1], False, False)
                mm(out, q[1], k[0], False, True).then_inc(sem["c_scores_summed"], 1)

            def turn_p(i):
                pe.wait_ge(sem["c_probs_ready"], i + 1)
                if i > 2:
                    pe.wait_ge(sem["c_turned_copied"], i - 2)
                for c in range(3):
                    m = pe.transpose(PS[0:CH, 3 + i % 3, c * S:(c + 1) * S], PC[:, i % NPC, c * CH:(c + 1) * CH],
                                     IDN[0:S, 0:S])
                m.then_inc(sem["c_probs_turned"], 1)

            def mix_v(i):
                b, (ti, par, j) = i // 16, HEADS1[i % 16]
                pe.wait_ge(sem["c_turned_copied"], i + 1)
                if i % 16 == 0:
                    pe.wait_ge(sem["c_values_copied"], 4 * b + 4)
                    if b > 0:
                        pe.wait_ge(sem["c_mixed_copied"], b)
                for c in range(3):
                    at = ti * P + 32 * j
                    m = mm(PS[32 * j:32 * j + 32, 6, ti * S:(ti + 1) * S], VP[0:CHS[c], b % 2, par, c, at:at + 32],
                           PTC[0:CHS[c], i % 4, c * S:(c + 1) * S], par == 0 and c == 0, par == 1 and c == 2)
                m.then_inc(sem["c_heads_mixed"], 1)

            for i in range(16 * B + MIX):
                if i < 16 * B:
                    scores(i)
                if 0 <= i - TURN < 16 * B:
                    turn_p(i - TURN)
                if i >= MIX:
                    mix_v(i - MIX)
                if i % 16 in PARTS and i // 16 + 1 < B:
                    project(i // 16 + 1, PARTS.index(i % 16))
            pe.wait_ge(sem["c_mixed_copied"], B)
            pe.wait_ge(sem["router_squares_ready"], 2)
            for k in range(KD):
                m = mm(PS[0:S, 7, 0:8], ONES[:, 0:S], CENTSQ[:, k, :], k == 0, k == KD - 1)
            m.then_inc(sem["centroid_lengths_summed"], 1)
            for n in range(2):
                for mo in range(KD):
                    for ti in range(KD):
                        m = mm(PS[:, 2 * n + mo, 0:HALF], W1A[:, 3, ti, mo * P:(mo + 1) * P], OT1[:, ti, half(n)],
                               ti == 0, ti == KD - 1)
                    m.then_inc(sem["c_output_summed"], 1)
            norm(5)
            mixture(1, TILES1)

        @block.scalar
        def _(act):
            def norm(i):
                src, _, kind = NORM[i]
                for n in range(2):
                    if kind == "layer":
                        act.wait_ge(sem["norm_centred"], 2 * LAYER[i] + n + 1)
                        src_ = XC
                    else:
                        act.wait_ge(sem[SOURCE[i][0]], SOURCE[i][1](n))
                        src_ = src
                    if 2 * i > 0:
                        act.wait_ge(sem["norm_variance_summed"], 2 * i)
                    act.activation(SQ[:, :, half(n)], src_[:, :, half(n)], ACT.Square).then_inc(sem["norm_squared"], 1)
                for n in range(2):
                    act.wait_ge(sem["norm_variance_summed"], 2 * i + n + 1)
                    if 2 * i - 1 + n > 0:
                        act.wait_ge(sem["norm_done"], 2 * i - 1 + n)
                    act.activation(STD[:, n, :], PS[:, 4 + n, 0:HALF], ACT.Ln,
                                   bias=COLS[:, 15:16]).then_inc(sem["norm_log_taken"], 1)
                    act.wait_ge(sem["norm_log_taken"], 2 * i + n + 1)
                    act.activation(STD[:, n, :], STD[:, n, :], ACT.Exp, scale=-0.5).then_inc(sem["norm_rstd_ready"], 1)

            def add_bias(name, first, col, gate, done, slots):
                for i in range(4):
                    n, mo = divmod(i, 2)
                    act.wait_ge(sem[name], i + 1)
                    if i == 0:
                        act.wait_ge(sem["gated_biases_ready"], 4)
                    act.activation(slots[i], PS[:, i, 0:HALF], ACT.Identity, bias=GB[:, col + mo:col + mo + 1],
                                       scale=TG[:, gate:gate + 1]).then_inc(sem[done], 1)

            act.preload_act_table_set("natural_log_exp_and_others")
            act.wait_ge(sem["vectors_loaded"], 64)
            norm(0)
            act.activation(TG[:, :], G4[:, :], ACT.Tanh).then_inc(sem["gates_ready"], 1)
            act.preload_act_table_set("natural_log_exp_and_others")
            def context_hi(b):
                act.wait_ge(sem[f"context_loaded{b % 3}"], 16 * (b // 3 + 1))
                if TI0 * (b - 2) > 0:
                    act.wait_ge(sem["a_values_summed"], TI0 * (b - 2))
                act.copy(CTXH[:, b % 3, :, 0:KV], CTX[:, b % 3, :, 0:KV]).then_inc(sem["a_context_high_ready"], 1)

            for i in range(2 * TI0):
                ti, n = divmod(i, 2)
                act.wait_ge(sem["a_query_summed"], i + 1)
                act.activation(QT0[:, ti, half(n)], PS[:, 4 + i % 2, 0:HALF], ACT.Copy,
                               scale=DH0 ** -0.5).then_inc(sem["a_query_copied"], 1)
                if i in (3, 5):
                    context_hi(i // 4)
                if i in W_PIECES:
                    act.wait_ge(sem["a_wkv_loaded"], 16)
                    act.copy(w_piece(WKV0H, W_PIECES.index(i)),
                             w_piece(WKV0, W_PIECES.index(i))).then_inc(sem["a_weights_high_ready"], 1)

            def exps(b):
                act.wait_ge(sem["a_shifted"], b + 1)
                if b > 0:
                    act.wait_ge(sem["a_weights_ready"], b)
                act.activation(SE[:, 0, :], SE[:, 0, :], ACT.Exp).then_inc(sem["a_exp_taken"], 1)

            def vcopy(b):
                act.wait_ge(sem["zeros_set"], 1)
                for ti in range(TI0):
                    i = TI0 * b + ti
                    act.wait_ge(sem["a_values_summed"], i + 1)
                    if i > 2:
                        act.wait_ge(sem["a_weighted"], i - 2)
                    act.copy(VSB[:, i % 3, 0:KV], PS[:, 4 + i % 2, 0:KV]).then_inc(sem["a_values_copied"], 1)

            def products_hi(b, tis):
                for ti in tis:
                    i = TI0 * b + ti
                    act.wait_ge(sem["a_products_ready"], i + 1)
                    if i > 3:
                        act.wait_ge(sem["a_similarity_summed"], i - 3)
                    act.copy(PRODH[:, i % 4, 0:KV], PROD[:, i % 3, 0:KV]).then_inc(sem["a_products_high_ready"], 1)

            def outs_hi(b):
                act.wait_ge(sem["a_heads_mixed"], TI0 * (b + 1))
                act.copy(OTH[:, :, tok(b)], OT0[:, :, tok(b)]).then_inc(sem["a_heads_high_ready"], 1)

            products_hi(0, range(TI0))
            for b in range(B - 1):
                products_hi(b + 1, range(2))
                exps(b)
                products_hi(b + 1, range(2, 4))
                if b:
                    outs_hi(b - 1)
                products_hi(b + 1, range(4, 5))
                if b + 2 < B:
                    context_hi(b + 2)
                products_hi(b + 1, range(5, TI0))
                if b < 2:
                    act.wait_ge(sem["a_wout_loaded"], 16)
                    act.wait_ge(sem["a_query_summed"], 2 * TI0)
                    tis = slice(b * TI0 // 2, (b + 1) * TI0 // 2)
                    act.copy(WOUT0H[:, tis, :], WOUT0[:, tis, :]).then_inc(sem["a_output_weights_high_ready"], 1)
                vcopy(b)
            outs_hi(B - 2)
            exps(B - 1)
            vcopy(B - 1)
            outs_hi(B - 1)
            add_bias("a_output_summed", 0, 0, 0, "a_output_gated", [WK[:, i, :] for i in range(4)])

            for i in range(6):
                act.wait_ge(sem["b_weights_folded"], i + 1)
                if i < 4:
                    dst = WQA[:, i // 2, 512 * (i % 2):512 * (i % 2) + 512]
                    src = PS[:, 6 + i % 2, :]
                else:
                    dst = WOA[:, 2 * (i - 4):2 * (i - 4) + 2, :]
                    src = PS[:, 6 + i % 2, :].rearrange("p (t c) -> p t c", t=2)
                act.copy(dst, src).then_inc(sem["b_folded_copied"], 1)
            norm(1)
            norm(2)
            for n in range(2):
                act.wait_ge(sem["b_latent_summed"], n + 1)
                act.copy(CK[:, half(n)], PS[:, n, 0:HALF]).then_inc(sem["b_latent_copied"], 1)
            act.wait_ge(sem["b_latent_rows_summed"], 1)
            act.copy(LT,
                     PS[0:S, 2, 0:B * LAT].rearrange("p (b c) -> p b c", b=B)).then_inc(sem["b_latent_rows_copied"], 1)
            act.wait_ge(sem["a_added_to_x"], 4)
            for i in range(16):
                act.wait_ge(sem["b_query_summed"], i + 1)
                if i > 2:
                    act.wait_ge(sem["b_query_read"], i - 2)
                if i > 2:
                    act.wait_ge(sem["b_query_cosines"], i - 2)
                act.copy(QS[:, i % 3, :], PS[:, 4 + i % 4, 0:HALF]).then_inc(sem["b_query_copied"], 1)

            def exp_b(i):
                act.wait_ge(sem["b_maxima_found"], i + 1)
                if 2 * (i - 2) > 0:
                    act.wait_ge(sem["b_probs_turned"], 2 * (i - 2))
                if i > 1:
                    act.wait_ge(sem["b_probs_ready"], i - 1)
                if i > 1:
                    act.wait_ge(sem["b_second_probs_ready"], i - 1)
                for x in range(4):
                    act.activation(PB[:, i % 3, (4 + x) * S:(5 + x) * S], PS[0:S, 2 * (i % 2) + 1, x * S:(x + 1) * S],
                                   ACT.Exp, bias=RTC[:, 5 * (i % 2), x:x + 1], scale=0.125,
                                   accum_out=RTC[:, 1 + 2 * (i % 2), 4 + x:5 + x])
                act.wait_ge(sem["b_scores_shifted"], i + 1)
                act.activation(PB[:, i % 3, 0:4 * S], SMB[:, i % 2, 0:4 * S], ACT.Exp,
                               scale=0.125).then_inc(sem["b_exp_taken"], 1)

            def turn_b(i):
                for q in range(2):
                    act.wait_ge(sem["b_probs_turned"], 2 * i + q + 1)
                    if i > 1:
                        act.wait_ge(sem["b_heads_mixed"], i - 1)
                    act.copy(PT0[:, i % 2, 4 * q * S:4 * (q + 1) * S],
                             PS[0:S, 4 + q, 0:4 * S]).then_inc(sem["b_turned_copied"], 1)

            def mix_b(i):
                b, g = divmod(i, 2)
                act.wait_ge(sem["b_heads_mixed"], i + 1)
                act.copy(UT[:, 2 * g:2 * g + 2, tok(b)],
                             PS[:, 6 + i % 2, 0:2 * S].rearrange("p (t c) -> p t c",
                                                                 t=2)).then_inc(sem["b_mixed_copied"], 1)

            for i in range(2 * B + 4):
                if 3 <= i < 2 * B + 3:
                    turn_b(i - 3)
                if i < 2 * B:
                    exp_b(i)
                if i >= 4:
                    mix_b(i - 4)
            norm(3)

            def split_hi0(e):
                act.wait_ge(sem["moe0_weights_loaded"], 48)
                act.wait_ge(sem["b_output_summed"], 4)
                for down in range(2):
                    act.copy(tile_of0("high", e, down),
                             tile_of0("raw", e, down)).then_inc(sem["expert_weights_high_ready"], 1)

            def split_hi(e, m):
                act.wait_ge(sem[f"chunk_loaded{e % 2}"], 48 * (e // 2 + 1))
                act.wait_ge(sem["down_summed"], N0 + 2 * CT1 * (e - 1) if e > 1 else N0)
                if e:
                    act.wait_ge(sem["c_output_summed"], 4)
                for down in range(2):
                    act.copy(tile_of(RINGH[:, e % 2, :], m, down),
                             tile_of(RING[:, e % 2, :], m, down)).then_inc(sem["expert_weights_high_ready"], 1)

            def mixture(which, tiles):
                first, count = (0, N0)[which], 2 * len(tiles)

                def gated(i):
                    act.wait_ge(sem["gate_summed"], first + i + 1)
                    if first + i > 2:
                        act.wait_ge(sem["hidden_ready"], first + i - 2)
                    bias = 0.0 if which == 0 else BIAS1[:, i // 2:i // 2 + 1]
                    act.activation(SIL[:, i % 3, :], PS[:, 4 + 2 * (i % 2), 0:HALF], ACT.Silu,
                                   bias=bias).then_inc(sem["gate_activated"], 1)

                for n in range(2):
                    act.wait_ge(sem["norm_done"], (6, 10)[which] + n + 1)
                    if which == 1:
                        act.activation(SQ[:, :, half(n)], XC[:, :, half(n)],
                                       ACT.Square).then_inc(sem["router_squares_ready"], 1)
                for n in range(2):
                    act.wait_ge(sem[("b_output_summed", "c_output_summed")[which]], 4)
                    act.copy(XH[:, :, half(n)], XC[:, :, half(n)]).then_inc(sem["x_high_ready"], 1)
                if which == 0:
                    split_hi0(0)
                    split_hi0(1)
                else:
                    act.copy(B2H[:, :], B2E[:, :]).then_inc(sem["output_bias_high_ready"], 1)
                    act.wait_ge(sem["router_scores_shifted"], 2)
                    act.activation(RT[:, 0, :], RT[:, 0, :], ACT.Sqrt).then_inc(sem["router_function_taken"], 1)
                act.wait_ge(sem["router_scores_shifted"], (1, 3)[which])
                dst = RT[:, 0, :] if which == 0 else RTC[:, 2, :]
                act.activation(dst, dst, ACT.Exp).then_inc(sem["router_function_taken"], 1)
                gated(0)
                gated(1)
                for q in range(2):
                    act.wait_ge(sem["router_weights_turned"], 2 * which + q + 1)
                    act.copy(WTS[:, half(q)], PS[0:40, 1 + q, 0:HALF]).then_inc(sem["router_turned_copied"], 1)
                for i in range(0, 2 * SPREADS[which], 2):
                    act.wait_ge(sem["router_weights_spread"], 2 * SPREADS[0] * which + i + 1)
                    act.copy(spreads(which)[i // 2][1][:, half(0)],
                             PS[:, i % 4, 0:HALF]).then_inc(sem["router_spread_copied"], 1)
                for i in range(count):
                    e = tiles[i // 2][0]
                    if i >= 2:
                        gated(i)
                    routed = which == 1 or i < ROUTED0
                    act.wait_ge(sem["hidden_weighed" if routed else "hidden_ready"],
                                (0, ROUTED0 if routed else N0)[which] + i + 1)
                    if first + i > 2:
                        act.wait_ge(sem["down_summed"], first + i - 2)
                    act.copy(HTH[:, i % 3, :], HT[:, i % 3, :]).then_inc(sem["hidden_high_ready"], 1)
                    if which == 0 and i % 2 == 0 and i // 2 + 2 <= E0:
                        split_hi0(i // 2 + 2)
                    if which == 1 and (e + 1, i % (2 * CT1) - SPLIT) in tiles:
                        split_hi(e + 1, i % (2 * CT1) - SPLIT)

            def copies(b, piece):
                if piece < 2:
                    act.wait_ge(sem["c_keys_summed"], 2 * b + piece + 1)
                    if b >= 2:
                        act.wait_ge(sem["c_scores_summed"], 16 * (b - 1))
                    if b < 2:
                        act.wait_ge(sem[("down_summed", "c_query_summed")[b]], (N0, 4)[b])
                    act.activation(KTH[b % 2][:, piece, 0:KV], PS[:, key_bank(b, piece), 0:KV], ACT.Identity,
                                       bias=COLS[:, 8 + piece:9 + piece]).then_inc(sem["c_keys_copied"], 1)
                    return
                if b >= 2:
                    act.wait_ge(sem["c_heads_mixed"], 16 * (b - 1))
                act.wait_ge(sem["zeros_set"], 3)
                if 2 * b + piece > 1:
                    act.wait_ge(sem["c_values_summed"], 2 * b + piece - 1)
                for par in range(2):
                    if piece == 2:
                        src = PS[0:CH, 7, :].rearrange("p (c h d) -> p c h d", c=2, d=32)
                        dst = VP[:, b % 2, par, 0:2, :].rearrange("p c (h d) -> p c h d", d=32)
                        src, dst = (a[:, :, :, 16 * par:16 * par + 16] for a in (src, dst))
                    else:
                        src = PS[0:CHS[2], 7, 0:D].rearrange("p (h d) -> p h d", d=32)
                        dst = VP[0:CHS[2], b % 2, par, 2, :].rearrange("p (h d) -> p h d", d=32)
                        src, dst = (a[:, :, 16 * par:16 * par + 16] for a in (src, dst))
                    act.copy(dst, src).then_inc(sem["c_values_copied"], 1)

            mixture(0, TILES0)
            act.preload_act_table_set("natural_log_exp_and_others")
            for piece in range(2):
                copies(0, piece)
            norm(4)

            def exp_c(i):
                act.wait_ge(sem["c_maximum_found"], i + 1)
                if i + 1 > NPC:
                    act.wait_ge(sem["c_probs_turned"], i + 1 - NPC)
                if i > 5:
                    act.wait_ge(sem["c_sum_inverted"], i - 5)
                act.activation(PC[:, i % NPC, 0:KV], SMK[:, i % 4, :], ACT.Exp, bias=SM1[:, 0, i % 6:i % 6 + 1],
                                   scale=-1.0, accum_out=SM1[:, 1, i % 6:i % 6 + 1]).then_inc(sem["c_exp_taken"], 1)

            def turn_c(i):
                act.wait_ge(sem["c_probs_turned"], i + 1)
                if i > 3:
                    act.wait_ge(sem["c_heads_mixed"], i - 3)
                act.copy(PTC[:, i % 4, :], PS[0:CH, 3 + i % 3, 0:3 * S]).then_inc(sem["c_turned_copied"], 1)

            for piece in range(2, 4):
                copies(0, piece)
            for i in range(16 * B + TURN + 1):
                if i > TURN:
                    turn_c(i - TURN - 1)
                if i < 16 * B:
                    exp_c(i)
                if i % 16 == 12 and i // 16 < CT1:
                    split_hi(0, i // 16)
                if i == 16 * CT1:
                    act.wait_ge(sem["moe1_small_loaded"], 32)
                    act.activation(CENTSQ, CENT, ACT.Square).then_inc(sem["router_squares_ready"], 1)
                    act.activation(CENT2, CENT, ACT.Copy, scale=-2.0).then_inc(sem["router_squares_ready"], 1)
                if i % 16 in PIECES and i // 16 + 1 < B:
                    copies(i // 16 + 1, PIECES.index(i % 16))
            add_bias("c_output_summed", 0, 2, 1, "c_output_gated", [WK[:, i, :] for i in range(4)])
            norm(5)
            mixture(1, TILES1)

        @block.gpsimd
        def _(pool):
            pool.memset(VSB, 0.0).then_inc(sem["zeros_set"], 1)
            def outs_lo(b):
                pool.wait_ge(sem["a_heads_high_ready"], b + 1)
                low, raw, high = (a[:, :, tok(b)] for a in (OTL, OT0, OTH))
                pool.tensor_tensor(low, raw, high, ALU.subtract).then_inc(sem["a_heads_low_ready"], 1)

            for i in range(TI0 * B):
                pool.wait_ge(sem["a_products_high_ready"], i + 1)
                if i > 3:
                    pool.wait_ge(sem["a_similarity_summed"], i - 3)
                low, raw, high = PRODL[:, i % 4, 0:KV], PROD[:, i % 3, 0:KV], PRODH[:, i % 4, 0:KV]
                pool.tensor_tensor(low, raw, high, ALU.subtract).then_inc(sem["a_products_low_ready"], 1)
                b = i // TI0
                if i % TI0 == TI0 - 1 and b in (1, 2):
                    if b > 0:
                        pool.wait_ge(sem["a_output_weights_high_ready"], b)
                    tis = slice((b - 1) * TI0 // 2, b * TI0 // 2)
                    pool.tensor_tensor(WOUT0L[:, tis, :], WOUT0[:, tis, :], WOUT0H[:, tis, :],
                                       ALU.subtract).then_inc(sem["a_output_weights_low_ready"], 1)
                if i % TI0 == TI0 - 1 and b >= 2:
                    outs_lo(b - 2)
            outs_lo(B - 2)
            pool.wait_ge(sem["b_folded_copied"], 6)
            pool.memset(CKM[64:P, 0, :], 0.0).then_inc(sem["b_zero_keys_set"], 1)
            pool.memset(CKM[0:64, 1, :], 0.0).then_inc(sem["b_zero_keys_set"], 1)
            pool.wait_ge(sem["b_zero_keys_set"], 2)
            for i in range(16):
                n, tq = divmod(i, 8)
                pool.wait_ge(sem["b_query_copied"], i + 1)
                v = lambda a: a.rearrange("p (b i) -> p b i", b=HB)
                co = CS[:, 0, :].unsqueeze(1).to_broadcast([P, HB, S])
                pool.tensor_tensor(v(QP[:, tq, half(n)]), v(QS[:, i % 3, :]), co,
                                   ALU.mult).then_inc(sem["b_query_cosines"], 1)
            for i in range(2 * B):
                pool.wait_ge(sem["b_sums_inverted"], i + 1)
                p = PB[:, i % 3, 4 * S:8 * S].rearrange("p (h c) -> p h c", h=4)
                inv = RTC[:, 2 + 2 * (i % 2), 4:8].unsqueeze(2).to_broadcast([S, 4, S])
                pool.tensor_tensor(p, p, inv, ALU.mult).then_inc(sem["b_second_probs_ready"], 1)
            pool.wait_ge(sem["moe_added_to_x"], 4)
            pool.memset(PC[:, :, KV:3 * CH], 0.0).then_inc(sem["zeros_set"], 1)
            pool.memset(VP, 0.0).then_inc(sem["zeros_set"], 1)
            for b in range(B):
                for mo in range(KD):
                    pool.wait_ge(sem["c_query_low_ready"], mo + 1 if b < HB else 4)
                    if b >= 2:
                        pool.wait_ge(sem["c_scores_summed"], 16 * (b - 1))
                    one = PAR[:, :].unsqueeze(2).to_broadcast([P, 8, S])
                    for dst, src in ((QXH, QCH), (QXL, QCL)):
                        q = src[:, mo, tok(b)].unsqueeze(1).to_broadcast([P, 8, S])
                        pool.tensor_tensor(dst[:, b % 2, mo, :, :], q, one, ALU.mult).then_inc(sem["c_query_split"], 1)

        @block.vector
        def _(dve):
            chain = [0]

            def link(ins):
                chain[0] += 1
                ins.then_inc(sem["dve_step_done"], 1)
                dve.wait_ge(sem["dve_step_done"], chain[0])

            def norm(i):
                src, dst, kind = NORM[i]
                for n in range(2):
                    if kind == "layer":
                        li = LAYER[i]
                        dve.wait_ge(sem["norm_mean_summed"], 2 * li + n + 1)
                        mean = PS[:, 4 + n, 0:HALF].unsqueeze(1).to_broadcast([P, KD, HALF])
                        dve.tensor_tensor(XC[:, :, half(n)], src[:, :, half(n)], mean,
                                          ALU.subtract).then_inc(sem["norm_centred"], 1)
                for n in range(2):
                    dve.wait_ge(sem["norm_rstd_ready"], 2 * i + n + 1)
                    if kind == "layer":
                        dve.wait_ge(sem["norm_centred"], 2 * LAYER[i] + n + 1)
                        rstd = STD[:, n, :].unsqueeze(1).to_broadcast([P, KD, HALF])
                        dve.tensor_tensor(dst[:, :, half(n)], XC[:, :, half(n)], rstd,
                                          ALU.mult).then_inc(sem["norm_done"], 1)
                    else:
                        for k in range(KD):
                            ins = dve.scalar_tensor_tensor(XC[:, k, half(n)], src[:, k, half(n)],
                                                           COLS[:, kind + k:kind + k + 1], STD[:, n, :],
                                                           ALU.mult, ALU.mult)
                        ins.then_inc(sem["norm_done"], 1)

            dve.wait_ge(sem["x_loaded0"], 16)
            dve.wait_ge(sem["x_loaded1"], 16)
            norm(0)
            dve.wait_ge(sem["constants_loaded"], 16 * 7)
            dve.memset(RTX, 0.0).then_inc(sem["unit_rows_ready"], 1)
            dve.tensor_copy(UNIT[0:32, :], IDN[0:32, 0:8]).then_inc(sem["unit_rows_ready"], 1)
            dve.tensor_copy(UNIT[32:40, :], IDN[32:40, 32:40]).then_inc(sem["unit_rows_ready"], 1)
            dve.wait_ge(sem["unit_rows_ready"], 3)
            dve.tensor_copy(HSR[:, :], HS[:, :]).then_inc(sem["a_head_rows_rounded"], 1)
            dve.memset(PS[:, 0:2, KV:HALF], 0.0)
            dve.memset(PS[:, 6:8, KV:HALF], 0.0)
            dve.memset(PS[0:H0, 2:4, KV:HALF], NEG).then_inc(sem["psum_tails_set"], 1)
            dve.wait_ge(sem["zeros_set"], 1)
            zeros = VSB[:, 0, 0:3 * KD].rearrange("p (s k c) -> p s k c", s=3, k=KD)
            dve.tensor_copy(CTXH[:, :, :, KV:KVE], zeros).then_inc(sem["pads_set"], 1)
            dve.tensor_copy(CTXL[:, :, :, KV:KVE], zeros).then_inc(sem["pads_set"], 1)
            dve.wait_ge(sem["gates_ready"], 1)
            dve.wait_ge(sem["vectors_loaded"], 64)
            for i in range(4):
                gate, col = i // 2, (4, 12)[i // 2] + i % 2
                dve.tensor_tensor(GB[:, i:i + 1], COLS[:, col:col + 1], TG[:, gate:gate + 1],
                                  ALU.mult).then_inc(sem["gated_biases_ready"], 1)

            dve.wait_ge(sem["norm_variance_summed"], 2)
            rows_ = SPREAD.rearrange("p t (a d) -> p (t a) d", d=DH0)
            for lo, n, c in ((0, 32, 0), (32, H0, 32)):
                dve.tensor_copy(rows_[lo:lo + n],
                        IDN[lo:lo + n, c:c + H0].unsqueeze(2).to_broadcast([n, H0, DH0])).then_inc(sem["a_spread_rows_built"], 1)
            dve.tensor_scalar(SES[0:32, :, :].rearrange("p s c -> p (s c)"),
                              AVG[0:32, 0:1].to_broadcast([32, 2 * HALF]),
                                  0.0, None, ALU.mult).then_inc(sem["a_spread_rows_built"], 1)
            dve.wait_ge(sem["a_spread_rows_built"], 3)
            dve.tensor_scalar(PRODL[:, :, KV:KVE], VSB[:, 0, 0:4].unsqueeze(2), 0.0, None,
                              ALU.add).then_inc(sem["pads_set"], 1)
            def context_lo(b):
                dve.wait_ge(sem["a_context_high_ready"], b + 1)
                low, raw, high = (a[:, b % 3, :, 0:KV] for a in (CTXL, CTX, CTXH))
                dve.tensor_tensor(low, raw, high, ALU.subtract).then_inc(sem["a_context_low_ready"], 1)

            context_lo(0)
            context_lo(1)
            for i in range(4):
                dve.wait_ge(sem["a_weights_high_ready"], i + 1)
                dve.tensor_tensor(w_piece(WKV0L, i), w_piece(WKV0, i), w_piece(WKV0H, i),
                                  ALU.subtract).then_inc(sem["a_weights_low_ready"], 1)

            dve.wait_ge(sem["a_query_summed"], 2 * TI0)
            dve.tensor_scalar(PRODH[:, :, KV:KVE], VSB[:, 0, 0:4].unsqueeze(2), NEG, None,
                              ALU.add).then_inc(sem["pads_set"], 1)
            dve.wait_ge(sem["a_query_copied"], 2 * TI0)

            def products(b, tis):
                for ti in tis:
                    i = TI0 * b + ti
                    dve.wait_ge(sem["a_keys_summed"], i + 1)
                    if i > 2:
                        dve.wait_ge(sem["a_products_low_ready"], i - 2)
                    q = QT0[:, ti, tok(b)].unsqueeze(1).to_broadcast([P, NC, S])
                    k = PS[:, i % 2, 0:HALF].rearrange("p (c i) -> p c i", c=NC)
                    out = PROD[:, i % 3, :].rearrange("p (c i) -> p c i", c=NC)
                    dve.tensor_tensor(out, k, q, ALU.mult).then_inc(sem["a_products_ready"], 1)

            def softmax_a(b, step):
                s = PS[0:H0, 2 + b % 2, 0:HALF]
                e = SE[:, 0, :].rearrange("p (c i) -> p c i", c=NC)
                if step == 0:
                    dve.wait_ge(sem["a_similarity_summed"], TI0 * (b + 1))
                    link(dve.tensor_reduce(SM0[:, 0, :], s.rearrange("p (c i) -> p i c", c=NC), AX_X, ALU.max))
                elif step == 1:
                    top = SM0[:, 0, :].unsqueeze(1).to_broadcast([H0, NC, S])
                    if b > 0:
                        dve.wait_ge(sem["a_probs_low_ready"], b)
                    dve.tensor_tensor(e, s.rearrange("p (c i) -> p c i", c=NC), top,
                                      ALU.subtract).then_inc(sem["a_shifted"], 1)
                elif step == 2:
                    dve.wait_ge(sem["a_exp_taken"], b + 1)
                    link(dve.tensor_reduce(SM0[:, 1, :], SE[:, 0, :].rearrange("p (c i) -> p i c", c=NC), AX_X,
                                           ALU.add))
                elif step == 3:
                    link(dve.reciprocal(SM0[:, 2, :], SM0[:, 1, :]))
                elif step == 4:
                    inv = SM0[:, 2, :].unsqueeze(1).to_broadcast([H0, NC, S])
                    dve.tensor_tensor(SE[:, 1, :].rearrange("p (c i) -> p c i", c=NC), e, inv,
                                      ALU.mult).then_inc(sem["a_weights_ready"], 1)
                elif step == 5:
                    dve.wait_ge(sem["a_weights_ready"], b + 1)
                    if TI0 * (b - 1) > 0:
                        dve.wait_ge(sem["a_weights_spread"], TI0 * (b - 1))
                    dve.tensor_copy(SES[0:H0, b % 2, :], SE[:, 1, :]).then_inc(sem["a_probs_high_ready"], 1)
                else:
                    dve.wait_ge(sem["a_probs_high_ready"], b + 1)
                    dve.tensor_tensor(SES[32:32 + H0, b % 2, :], SE[:, 1, :], SES[0:H0, b % 2, :],
                                      ALU.subtract).then_inc(sem["a_probs_low_ready"], 1)

            def weigh(b):
                for ti in range(TI0):
                    i = TI0 * b + ti
                    dve.wait_ge(sem["a_weights_spread"], i + 1)
                    dve.wait_ge(sem["a_values_copied"], i + 1)
                    if i > 1:
                        dve.wait_ge(sem["a_heads_mixed"], i - 1)
                    if i == 0:
                        dve.wait_ge(sem["zeros_set"], 1)
                    dve.tensor_tensor(PV[:, i % 2, :], PS[:, 6 + i % 2, 0:HALF], VSB[:, i % 3, :],
                                      ALU.mult).then_inc(sem["a_weighted"], 1)
                    dve.wait_ge(sem["a_weighted"], i + 1)
                    dve.tensor_reduce(OT0[:, ti, tok(b)], PV[:, i % 2, :].rearrange("p (c i) -> p i c", c=NC),
                                          AX_X, ALU.add).then_inc(sem["a_heads_mixed"], 1)

            for b in range(B):
                for ti in range(TI0):
                    products(b, [ti])
                    if b and ti < 7:
                        softmax_a(b - 1, ti)
                if b:
                    if b + 1 < B:
                        context_lo(b + 1)
                    weigh(b - 1)
            for step in range(7):
                softmax_a(B - 1, step)
            weigh(B - 1)
            dve.wait_ge(sem["a_heads_high_ready"], B)
            low, raw, high = (a[:, :, tok(B - 1)] for a in (OTL, OT0, OTH))
            dve.tensor_tensor(low, raw, high, ALU.subtract).then_inc(sem["a_last_heads_low_ready"], 1)

            def add_to_x(name, done):
                for i in range(4):
                    n, mo = divmod(i, 2)
                    dve.wait_ge(sem[name], i + 1)
                    dve.tensor_tensor(X[:, mo, half(n)], X[:, mo, half(n)], WK[:, i, :], ALU.add).then_inc(sem[done], 1)

            add_to_x("a_output_gated", "a_added_to_x")

            norm(1)
            dve.wait_ge(sem["norm_done"], 4)
            norm(2)

            for n in range(2):
                dve.wait_ge(sem["b_latent_copied"], n + 1)
                co = CS[:, 0, :].unsqueeze(1).to_broadcast([P, HB, S])
                si = CS[:, 1, :].unsqueeze(1).to_broadcast([P, HB, S])
                v = lambda a: a.rearrange("p (b i) -> p b i", b=HB)
                link(dve.stream_shuffle(CK2[:, half(n)], CK[:, half(n)], [q ^ 1 for q in range(32)]))
                link(dve.tensor_tensor(v(CK2[:, half(n)]), v(CK2[:, half(n)]), si, ALU.mult))
                link(dve.tensor_tensor(v(CK[:, half(n)]), v(CK[:, half(n)]), co, ALU.mult))
                for par in range(2):
                    rows = slice(64 * par, 64 * par + 64)
                    dve.tensor_tensor(CKM[rows, par, half(n)], CK[rows, half(n)], CK2[rows, half(n)],
                                      ALU.add).then_inc(sem["b_latent_rotated"], 1)
            dve.wait_ge(sem["b_folded_copied"], 6)
            dve.tensor_copy(CMB, CM[:, :]).then_inc(sem["b_mask_rounded"], 1)
            dve.tensor_copy(IDNB, IDN[0:S, 0:S]).then_inc(sem["b_mask_rounded"], 1)
            for i in range(16):
                n, tq = divmod(i, 8)
                dve.wait_ge(sem["b_query_copied"], i + 1)
                dst = QP[:, tq, half(n)]
                if i > 2:
                    dve.wait_ge(sem["b_query_rotated"], i - 2)
                dve.stream_shuffle(SH[:, i % 3, :], QS[:, i % 3, :],
                                   [q ^ 1 for q in range(32)]).then_inc(sem["b_query_read"], 1)
                dve.wait_ge(sem["b_query_read"], i + 1)
                link(dve.tensor_tensor(v(SH[:, i % 3, :]), v(SH[:, i % 3, :]), si, ALU.mult))
                dve.wait_ge(sem["b_query_cosines"], i + 1)
                dve.tensor_tensor(dst, dst, SH[:, i % 3, :], ALU.add).then_inc(sem["b_query_rotated"], 1)

            def shift_b(i):
                dve.wait_ge(sem["b_scores_summed"], i + 1)
                s = PS[0:S, 2 * (i % 2):2 * (i % 2) + 2, 0:4 * S].rearrange("p a (x c) -> p a x c", x=4)
                out = SMB[:, i % 2, 0:4 * S].rearrange("p (x c) -> p x c", x=4)
                top = RTC[:, 6 + i % 2, :]
                link(dve.tensor_reduce(top.rearrange("p (a x) -> p a x", a=2), s, AX_X, ALU.max))
                if i > 1:
                    dve.wait_ge(sem["b_exp_taken"], i - 1)
                dve.tensor_scalar(RTC[:, 5 * (i % 2), 0:4], top[:, 4:8], -0.125, None,
                                  ALU.mult).then_inc(sem["b_maxima_found"], 1)
                dve.tensor_tensor(out, s[:, 0, :, :], top[:, 0:4].unsqueeze(2).to_broadcast([S, 4, S]),
                                      ALU.subtract).then_inc(sem["b_scores_shifted"], 1)

            def divide_b(i):
                dve.wait_ge(sem["b_exp_taken"], i + 1)
                p3 = PB[:, i % 3, :].rearrange("p (h c) -> p h c", h=8)
                if i > 1:
                    dve.wait_ge(sem["b_second_probs_ready"], i - 1)
                sums, inv = RTC[:, 1 + 2 * (i % 2), :], RTC[:, 2 + 2 * (i % 2), :]
                link(dve.tensor_reduce(sums[:, 0:4], p3[:, 0:4, :], AX_X, ALU.add))
                dve.reciprocal(inv, sums).then_inc(sem["b_sums_inverted"], 1)
                dve.wait_ge(sem["b_sums_inverted"], i + 1)
                dve.tensor_tensor(p3[:, 0:4, :], p3[:, 0:4, :], inv[:, 0:4].unsqueeze(2).to_broadcast([S, 4, S]),
                                      ALU.mult).then_inc(sem["b_probs_ready"], 1)

            for i in range(2 * B + 1):
                if i < 2 * B:
                    shift_b(i)
                if i:
                    divide_b(i - 1)
            for i in range(4):
                n, mo = divmod(i, 2)
                dve.wait_ge(sem["b_output_summed"], i + 1)
                dve.tensor_tensor(Y[:, mo, half(n)], PS[:, i, 0:HALF], Y[:, mo, half(n)],
                                  ALU.add).then_inc(sem["b_added_to_y"], 1)
            norm(3)

            def router(which):
                def v(i):
                    return RT[:, i, :].rearrange("p (b e) -> p b e", b=B)

                def wide(a):
                    return a.unsqueeze(2).to_broadcast([S, B, 8])

                dve.wait_ge(sem["router_scores_summed"], which + 1)
                ps = PS[0:S, 0, 0:B * 8].rearrange("p (b e) -> p b e", b=B)
                if which == 0:
                    link(dve.tensor_tensor(v(0), ps, EB[:, :].unsqueeze(1).to_broadcast([S, B, 8]), ALU.add))
                    link(dve.tensor_reduce(RTC[:, 0, :], v(0), AX_X, ALU.max))
                    dve.tensor_tensor(v(0), v(0), wide(RTC[:, 0, :]),
                                      ALU.subtract).then_inc(sem["router_scores_shifted"], 1)
                    dve.wait_ge(sem["router_function_taken"], 1)
                else:
                    link(dve.tensor_tensor(v(0), ps, CSQ.unsqueeze(1).to_broadcast([S, B, 8]), ALU.add))
                    dve.tensor_scalar(RT[:, 0, :], RT[:, 0, :], 1e-12, None,
                                      ALU.max).then_inc(sem["router_scores_shifted"], 1)
                    dve.wait_ge(sem["router_function_taken"], 2)
                for c in range(2):
                    src, top, one = (v(0), v(3))[c], RTC[:, 3 + c, :], v(1 + 3 * c)
                    link(dve.tensor_reduce(top, src, AX_X, ALU.max))
                    link(dve.tensor_tensor(v(5), src, wide(top), ALU.is_equal))
                    link(dve.tensor_tensor(v(5), v(5), RANK[:, :].unsqueeze(1).to_broadcast([S, B, 8]), ALU.mult))
                    link(dve.tensor_reduce(RTC[:, 5, :], v(5), AX_X, ALU.max))
                    link(dve.tensor_tensor(one, v(5), wide(RTC[:, 5, :]), ALU.is_equal))
                    if c == 0:
                        link(dve.scalar_tensor_tensor(RT[:, 3, :], RT[:, 1, :], NEG, RT[:, 0, :], ALU.mult, ALU.add))
                if which == 0:
                    link(dve.tensor_tensor(RTC[:, 5, :], RTC[:, 3, :], RTC[:, 4, :], ALU.add))
                    link(dve.reciprocal(RTC[:, 6, :], RTC[:, 5, :]))
                    link(dve.tensor_tensor(v(5), v(1), v(4), ALU.add))
                    link(dve.tensor_tensor(v(5), v(5), v(0), ALU.mult))
                    link(dve.tensor_tensor(v(13), v(5), wide(RTC[:, 6, :]), ALU.mult))
                else:
                    dve.tensor_tensor(RTC[:, 2, :], RTC[:, 4, :], RTC[:, 3, :],
                                      ALU.subtract).then_inc(sem["router_scores_shifted"], 1)
                    dve.wait_ge(sem["router_function_taken"], 3)
                    link(dve.tensor_scalar(RTC[:, 5, :], RTC[:, 2, :], 1.0, None, ALU.add))
                    link(dve.reciprocal(RTC[:, 6, :], RTC[:, 5, :]))
                    link(dve.tensor_tensor(RTC[:, 2, :], RTC[:, 2, :], RTC[:, 6, :], ALU.mult))
                    link(dve.tensor_tensor(v(1), v(1), wide(RTC[:, 6, :]), ALU.mult))
                    link(dve.tensor_tensor(v(4), v(4), wide(RTC[:, 2, :]), ALU.mult))
                    link(dve.tensor_tensor(v(13), v(1), v(4), ALU.add))
                dve.tensor_copy(RTH[:, :], RT[:, 13, :]).then_inc(sem["router_high_ready"], 1)
                dve.wait_ge(sem["router_high_ready"], which + 1)
                high = RTH[:, :].rearrange("p (b e) -> p b e", b=B)
                if which:
                    dve.wait_ge(sem["router_weights_turned"], 2)
                dve.tensor_copy(RTX[:, :, 0:8], high).then_inc(sem["router_weights_ready"], 1)
                dve.tensor_tensor(RTX[:, :, 32:40], v(13), high, ALU.subtract).then_inc(sem["router_weights_ready"], 1)

            def split_lo0(e):
                for down in range(2):
                    dve.wait_ge(sem["expert_weights_high_ready"], 2 * e + down + 1)
                    dve.tensor_tensor(tile_of0("low", e, down), tile_of0("raw", e, down), tile_of0("high", e, down),
                                          ALU.subtract).then_inc(sem["expert_weights_low_ready"], 1)

            def split_lo(e, m):
                for down in range(2):
                    dve.wait_ge(sem["expert_weights_high_ready"], 2 * (E0 + 1) + 2 * (CT1 * e + m) + down + 1)
                    raw, hi, lo = (tile_of(a[:, e % 2, :], m, down) for a in (RING, RINGH, RINGL))
                    dve.tensor_tensor(lo, raw, hi, ALU.subtract).then_inc(sem["expert_weights_low_ready"], 1)

            def mixture(which, tiles):
                first, fw = (0, N0)[which], (0, ROUTED0)[which]
                count = 2 * len(tiles)

                def hidden_lo(i):
                    dve.wait_ge(sem["hidden_high_ready"], first + i + 1)
                    h = [a[:, i % 3, :] for a in (HTL, HT, HTH)]
                    dve.tensor_tensor(h[0], h[1], h[2], ALU.subtract).then_inc(sem["hidden_low_ready"], 1)

                for n in range(2):
                    dve.wait_ge(sem["x_high_ready"], 2 * which + n + 1)
                    dve.tensor_tensor(XL[:, :, half(n)], XC[:, :, half(n)], XH[:, :, half(n)],
                                      ALU.subtract).then_inc(sem["x_low_ready"], 1)
                if which == 0:
                    split_lo0(0)
                else:
                    dve.wait_ge(sem["shared_rows_loaded"], 16)
                    dve.tensor_copy(UNITX[:, :], UNITX_IN).then_inc(sem["shared_rows_rounded"], 1)
                router(which)
                if which == 0:
                    split_lo0(1)
                else:
                    dve.wait_ge(sem["output_bias_high_ready"], 1)
                    dve.tensor_tensor(B2L[:, :], B2E[:, :], B2H[:, :],
                                      ALU.subtract).then_inc(sem["output_bias_low_ready"], 1)
                def gate_up(i):
                    dve.wait_ge(sem["up_summed"], first + i + 1)
                    dve.wait_ge(sem["gate_activated"], first + i + 1)
                    if first + i > 2:
                        dve.wait_ge(sem["hidden_low_ready"], first + i - 2)
                    col = NCH1 * CT1 + i // 2
                    b1 = 0.0 if which == 0 else BIAS1[:, col:col + 1]
                    dve.scalar_tensor_tensor(HT[:, i % 3, :], PS[:, 5 + 2 * (i % 2), 0:HALF], b1,
                                                 SIL[:, i % 3, :], ALU.add, ALU.mult).then_inc(sem["hidden_ready"], 1)

                gate_up(0)
                gate_up(1)
                for i in range(1, 2 * SPREADS[which], 2):
                    dve.wait_ge(sem["router_weights_spread"], 2 * SPREADS[0] * which + i + 1)
                    dve.tensor_copy(spreads(which)[i // 2][1][:, half(1)],
                                    PS[:, i % 4, 0:HALF]).then_inc(sem["router_spread_copied_odd"], 1)
                for i in range(count):
                    (e, m_), n = tiles[i // 2], i % 2
                    h = HT[:, i % 3, :]
                    if i >= 2:
                        gate_up(i)
                    if which == 1 or i < ROUTED0:
                        dve.wait_ge(sem["hidden_ready"], first + i + 1)
                        if i < 2:
                            dve.wait_ge(sem["router_spread_copied"], SPREADS[0] * which + SPREADS[which])
                            dve.wait_ge(sem["router_spread_copied_odd"], SPREADS[0] * which + SPREADS[which])
                        dve.tensor_tensor(h, h, weights_of(which, i // 2)[:, half(n)],
                                          ALU.mult).then_inc(sem["hidden_weighed"], 1)
                    if which == 0 and i == 10:
                        dve.wait_ge(sem["mask_loaded"], 16)
                        link(dve.tensor_copy(MKB.rearrange("p b c -> p (b c)"), MK8.bitcast(U8)))
                    if which == 0 and i == 12:
                        dve.tensor_scalar(MKB.rearrange("p b c -> p (b c)"), MKB.rearrange("p b c -> p (b c)"),
                                              -NEG, NEG, ALU.mult, ALU.add).then_inc(sem["mask_ready"], 1)
                    if i:
                        hidden_lo(i - 1)
                    if which == 0 and i % 2 == 0 and i // 2 + 2 <= E0:
                        split_lo0(i // 2 + 2)
                    if which == 1 and (e + 1, i % (2 * CT1) - SPLIT) in tiles:
                        split_lo(e + 1, i % (2 * CT1) - SPLIT)
                hidden_lo(count - 1)
                for i in range(4):
                    n, mo = divmod(i, 2)
                    dve.wait_ge(sem["down_summed"], first + 2 * len(tiles) - 1 + n)
                    ps, x = PS[:, i, 0:HALF], X[:, mo, half(n)]
                    if which == 0:
                        link(dve.tensor_tensor(Y[:, mo, half(n)], ps, Y[:, mo, half(n)], ALU.add))
                        dve.scalar_tensor_tensor(x, Y[:, mo, half(n)], TG[:, 2:3], x, ALU.mult,
                                                 ALU.add).then_inc(sem["moe_added_to_x"], 1)
                    else:
                        dve.scalar_tensor_tensor(x, ps, TG[:, 3:4], x, ALU.mult,
                                                 ALU.add).then_inc(sem["moe_added_to_x"], 1)

            mixture(0, TILES0)
            dve.tensor_scalar(KTL[:, :, :, KV:KVE].rearrange("p s m c -> p (s m c)"), AVG[:, 0:4], 0.0, None,
                                  ALU.mult).then_inc(sem["c_pads_set"], 1)
            dve.tensor_scalar(KTH[0][:, :, KV:KVE], AVG[:, 0:2].unsqueeze(2), 0.0, None,
                              ALU.mult).then_inc(sem["c_pads_set"], 1)

            def keys_lo(b, ti):
                dve.wait_ge(sem["c_keys_copied"], 2 * b + ti + 1)
                if b >= 2:
                    dve.wait_ge(sem["c_scores_summed"], 16 * (b - 1))
                dve.scalar_tensor_tensor(KTL[:, b % 2, ti, 0:KV], PS[:, key_bank(b, ti), 0:KV], COLS[:, 8 + ti:9 + ti],
                                             KTH[b % 2][:, ti, 0:KV], ALU.add, ALU.subtract).then_inc(sem["c_keys_low_ready"], 1)

            norm(4)
            keys_lo(0, 0)
            keys_lo(0, 1)

            for i in range(4):
                n, mo = divmod(i, 2)
                dve.wait_ge(sem["c_query_summed"], i + 1)
                bias = COLS[:, 6 + mo:7 + mo]
                dve.tensor_scalar(QCH[:, mo, half(n)], PS[:, i, 0:HALF], bias, None,
                                  ALU.add).then_inc(sem["c_query_copied"], 1)
                dve.wait_ge(sem["c_query_copied"], i + 1)
                dve.scalar_tensor_tensor(QCL[:, mo, half(n)], PS[:, i, 0:HALF], bias, QCH[:, mo, half(n)],
                                             ALU.add, ALU.subtract).then_inc(sem["c_query_low_ready"], 1)
            dve.wait_ge(sem["c_query_summed"], 4)
            dve.tensor_scalar(KTH[1][:, :, KV:KVE], AVG[:, 0:2].unsqueeze(2), 0.0, None,
                              ALU.mult).then_inc(sem["c_pads_set"], 1)
            dve.wait_ge(sem["mask_ready"], 1)

            def top(i):
                b = i // 16
                dve.wait_ge(sem["c_scores_summed"], i + 1)
                if i > 3:
                    dve.wait_ge(sem["c_exp_taken"], i - 3)
                dve.tensor_tensor_reduce(SMK[:, i % 4, :], PS[0:S, i % 3, 0:KV], MKB[:, b, :], -0.25, -2.0 * NEG,
                                             ALU.add, ALU.min, SM1[:, 0, i % 6:i % 6 + 1]).then_inc(sem["c_maximum_found"], 1)

            def over(i):
                dve.wait_ge(sem["c_exp_taken"], i + 1)
                dve.reciprocal(SM1[:, 2, i % 6:i % 6 + 1],
                               SM1[:, 1, i % 6:i % 6 + 1]).then_inc(sem["c_sum_inverted"], 1)
                dve.wait_ge(sem["c_sum_inverted"], i + 1)
                if i == 0:
                    dve.wait_ge(sem["zeros_set"], 3)
                dve.tensor_scalar(PC[:, i % NPC, 0:KV], PC[:, i % NPC, 0:KV], SM1[:, 2, i % 6:i % 6 + 1], None,
                                      ALU.mult).then_inc(sem["c_probs_ready"], 1)

            def outs(b):
                dve.wait_ge(sem["c_heads_mixed"], 16 * (b + 1))
                for ti in range(KD):
                    ins = dve.tensor_scalar(OT1[:, ti, tok(b)], PS[:, 6, ti * S:(ti + 1) * S],
                                            COLS[:, 10 + ti:11 + ti], None, ALU.add)
                ins.then_inc(sem["c_mixed_copied"], 1)

            for i in range(16 * B + MIX + 1):
                if i >= 16 + MIX and (i - MIX) % 16 == 0:
                    outs((i - MIX) // 16 - 1)
                if 2 <= i < 16 * B + 2:
                    over(i - 2)
                if (i - 1) % 16 in PIECES[:2] and i // 16 + 1 < B:
                    keys_lo(i // 16 + 1, PIECES.index((i - 1) % 16))
                if i < 16 * B:
                    top(i)
                if i % 16 == 15 and i // 16 < CT1:
                    split_lo(0, i // 16)
            dve.wait_ge(sem["centroid_lengths_summed"], 1)
            dve.tensor_copy(CSQ, PS[0:S, 7, 0:8]).then_inc(sem["centroid_lengths_copied"], 1)
            dve.wait_ge(sem["centroid_lengths_copied"], 1)
            add_to_x("c_output_gated", "c_added_to_x")
            norm(5)
            mixture(1, TILES1)


def _rope_tables():
    freqs = (np.float32(1.0) / np.float32(THETA) ** (np.arange(0, ROPE, 2, dtype=np.float32) / np.float32(ROPE)))
    ang = np.outer(np.arange(S, dtype=np.float32), freqs.astype(np.float32)).astype(np.float32)
    tables = np.zeros((P, 2, S), np.float32)
    for p in range(P):
        r = p % 64 - NOPE
        if r < 0:
            tables[p, 0] = 1.0
        else:
            tables[p, 0] = np.cos(ang[:, r // 2])
            tables[p, 1] = np.sin(ang[:, r // 2]) * (-1.0 if r % 2 == 0 else 1.0)
    return tables


def kernel(**inputs):
    import concourse.bacc as _bacc
    from concourse.bass_utils import run_bass_kernel_spmd as _run

    a = {k: np.asarray(v) for k, v in inputs.items()}
    f = np.float32

    def rows(w):
        return np.ascontiguousarray(w.reshape(-1, P, w.shape[-1]).transpose(1, 0, 2))

    def col(v):
        return v.reshape(KD, P).T

    arrays = {}
    arrays["xT"] = rows(a["x"].reshape(T, D).T)
    arrays["ctxT"] = np.ascontiguousarray(a["ctx_1024"].transpose(2, 0, 1).reshape(KD, P, B, KV).transpose(1, 2, 0, 3))
    arrays["mask"] = np.ascontiguousarray(a["mask_Bx1x1xS2_bf1"].reshape(B * KV)).view(np.uint8)
    arrays["gates"] = np.ascontiguousarray(np.stack([a["g_xattn"][0], a["g_xattn"][1], a["g_ffn"][0], a["g_ffn"][1]]))
    arrays["ident"] = np.eye(P, dtype=f)
    arrays["avg"] = np.full((P, P), 1.0 / D, f)
    heads = np.zeros((P, TI0, H0), f)
    for ti in range(TI0):
        for p in range(P):
            heads[p, ti, 2 * ti + p // DH0] = 1.0
    arrays["headsum"] = heads.reshape(P, TI0 * H0)
    arrays["rope"] = _rope_tables()
    arrays["causal"] = np.triu(np.full((S, S), NEG, f), 1)
    arrays["parity"] = np.stack([(np.arange(P) // DH1 == 2 * (h % 4) + h // 4).astype(f) for h in range(8)], 1)
    arrays["rank"] = np.tile(np.arange(8, 0, -1, dtype=f), (S, 1))
    arrays["ones"] = np.ones((P, S), f)
    cols = np.zeros((P, 16), f)
    for at, name in ((0, "L0_ffn_w_ln1"), (2, "L0_ffn_w_ln2"), (4, "L0_xattn_bout"), (6, "L1_xattn_b_q"),
                     (8, "L1_xattn_b_k"), (10, "L1_xattn_b_v"), (12, "L1_xattn_b_o")):
        cols[:, at:at + 2] = col(a[name])
    cols[:, 15] = EPS
    arrays["cols"] = cols
    arrays["ebias"] = a["L0_ffn_expert_bias"]
    b2 = np.zeros((40, D), f)
    b2[0:8] = b2[32:40] = a["L1_ffn_b2"]
    arrays["b2"] = b2
    arrays["WQ0"] = rows(a["L0_xattn_Wq"])
    arrays["WKV0"] = rows(a["L0_xattn_Wkv"])
    arrays["WOUT0"] = rows(a["L0_xattn_Wout"])
    arrays["WQT"] = rows(a["L0_ffn_Wq"].T)
    wkvb = a["L0_ffn_Wkvb"].reshape(LAT, 16, NOPE)
    gkv = np.zeros((P, 8, P), f)
    bdv = np.zeros((P, 4, P), f)
    wo = np.zeros((P, 4, D), f)
    for h in range(16):
        lo = 64 * (h % 2)
        gkv[lo:lo + NOPE, h // 2, lo:lo + LAT] = wkvb[:, h, :].T
        gkv[lo + NOPE:lo + 64, h // 2, lo + LAT:lo + 64] = np.eye(ROPE, dtype=f)
        j = 32 * (h % 4)
        bdv[j:j + NOPE, h // 4, j:j + LAT] = wkvb[:, h, :].T
        wo[j:j + NOPE, h // 4, :] = a["L0_ffn_Wo"][64 * h:64 * h + NOPE]
    arrays["GKV"], arrays["BDV"], arrays["WO0"] = gkv, bdv, wo
    arrays["WKVA"] = rows(np.concatenate([a["L0_ffn_Wkva"]] * 2, 1))

    def experts(name, shared):
        w = np.concatenate([a[name], a[shared]], 0)
        return w

    arrays["WGU0"] = np.concatenate([rows(np.ascontiguousarray(experts(name, shared).transpose(1, 0, 2)).reshape(D, -1))
                                     for name, shared in (("L0_ffn_Wg", "L0_ffn_sWg"), ("L0_ffn_Wu", "L0_ffn_sWu"))], 1)
    arrays["WD0"] = np.ascontiguousarray(experts("L0_ffn_Wd", "L0_ffn_sWd").transpose(1, 0, 2))
    arrays["WGT0"] = rows(a["L0_ffn_Wgate"])
    arrays["W1A"] = np.ascontiguousarray(np.stack([rows(a["L1_xattn_" + n].T) for n in ("w_q", "w_k", "w_v", "w_o")],
                                                  1))
    rows1 = NCH1 * CW1

    def padded(w):
        return np.concatenate([w, np.zeros((rows1 - E1 * HID1,) + w.shape[1:], f)])

    bias1 = np.stack([padded(a["L1_ffn_bg"].reshape(-1)), padded(a["L1_ffn_b1"].reshape(-1))])
    arrays["bias1"] = np.ascontiguousarray(bias1.reshape(2 * NCH1 * CT1, P).T)
    shared = np.zeros((40, E1 - 1, P), f)
    for e in range(E1 - 1):
        cut = (e + 1) * HID1 % P
        for at in (0, 32):
            shared[at + e, e, :cut] = 1.0
            shared[at + e + 1, e, cut:] = 1.0
    arrays["shared"] = shared.reshape(40, -1)
    arrays["centT"] = rows(a["L1_ffn_centroid"].T)
    for dst, name in (("WG1", "L1_ffn_Wg"), ("WU1", "L1_ffn_W1")):
        w = padded(a[name].transpose(0, 2, 1).reshape(E1 * HID1, D))
        arrays[dst] = np.ascontiguousarray(w.reshape(NCH1, CW1, KD, P).transpose(0, 3, 2, 1))
    w = padded(a["L1_ffn_W2"].reshape(E1 * HID1, D))
    arrays["WD1"] = np.ascontiguousarray(w.reshape(NCH1, CT1, P, D).transpose(0, 2, 1, 3))

    nc = _bacc.Bacc("TRN2", target_bir_lowering=False, num_devices=1)
    t = {}
    for name, v in arrays.items():
        arrays[name] = v = np.ascontiguousarray(v)
        t[name] = nc.dram_tensor(name, v.shape, mybir.dt.from_np(v.dtype), kind="ExternalInput").ap()
    t["outT"] = nc.dram_tensor("outT", (P, KD, T), F32, kind="ExternalOutput").ap()
    program(nc, t)
    r = _run(nc, [arrays], core_ids=[0])
    out = r.results[0]["outT"]
    return np.ascontiguousarray(out.transpose(1, 0, 2).reshape(D, B, S).transpose(1, 2, 0))
```
